# Optimizing a Trainium2 kernel written in Bass

```python
import numpy as np
import jax
import jax.numpy as jnp

def _softmax(x, axis=-1):
    return jax.nn.softmax(x, axis=axis)

def _gelu(x):
    return jax.nn.gelu(x, approximate=True)

def _silu(x):
    return jax.nn.silu(x)

def _sigmoid(x):
    return jax.nn.sigmoid(x)

def _layernorm(x, axis=-1, eps=1e-05):
    m = jnp.mean(x, axis=axis, keepdims=True)
    v = jnp.var(x, axis=axis, keepdims=True)
    return (x - m) / jnp.sqrt(v + eps)

def _scatter_add(tgt, idx, src, axis=0):
    return tgt.at[idx].add(src)

def _segment_sum(src, seg, n):
    return jax.ops.segment_sum(src, seg, n)
kernel_name = 'mk_xattn_ffn_d2_seqx_r4_ecdf10'

def setup_inputs(seed: int=0):
    np.random.seed(seed)
    _w = jnp.asarray

    def _rec_inputs():
        import jax
        import jax.numpy as jnp
        _rk = jax.random.key(seed)
        x = -0.0002928 + 1 * jax.random.normal(jax.random.fold_in(_rk, 1), (32, 128, 256), jnp.float32)
        _lenS = 128 - jax.random.randint(jax.random.fold_in(_rk, 7), (32,), 0, max(1, 128 // 4) + 1, jnp.int32)
        _lenS2 = 128 - jax.random.randint(jax.random.fold_in(_rk, 8), (32,), 0, max(1, 128 // 4) + 1, jnp.int32)
        _ctx_1024P = jax.random.normal(jax.random.fold_in(_rk, 11), (32, 16, 256), jnp.float32)
        _ctx_1024c = jax.random.dirichlet(jax.random.fold_in(_rk, 511), 0.3 * jnp.ones((16,), jnp.float32), (32, 128))
        _ctx_1024t = jnp.einsum('bsk,bkd->bsd', _ctx_1024c, _ctx_1024P)
        _ctx_1024t = _ctx_1024t * jax.lax.rsqrt(jnp.mean(jnp.square(_ctx_1024t)) + 1e-12) * 0.953939
        ctx_1024 = -1.39393e-06 + 0.999914 * (_ctx_1024t + 0.3 * jax.random.normal(jax.random.fold_in(_rk, 611), (32, 128, 256), jnp.float32))
        return (x, ctx_1024)
    x, ctx_1024 = _rec_inputs()

    def _L0_xattn_setup():
        import jax, jax.numpy as jnp
        import numpy as np
        D_MODEL = 256
        N_HEADS = 16
        D_K = D_MODEL // N_HEADS
        key = jax.random.key(seed)
        ks = jax.random.split(key, 11)
        B, S = (2, 512)
        scale = 1.0 / np.sqrt(D_MODEL)
        inp = {'q': jax.random.normal(ks[0], (B, S, D_MODEL), jnp.float32), 'k': jax.random.normal(ks[1], (B, S, D_MODEL), jnp.float32), 'v': jax.random.normal(ks[2], (B, S, D_MODEL), jnp.float32), 'w_q': jax.random.normal(ks[3], (D_MODEL, D_MODEL), jnp.float32) * scale, 'b_q': jnp.zeros((D_MODEL,), jnp.float32), 'w_k': jax.random.normal(ks[4], (D_MODEL, D_MODEL), jnp.float32) * scale, 'b_k': jnp.zeros((D_MODEL,), jnp.float32), 'w_v': jax.random.normal(ks[5], (D_MODEL, D_MODEL), jnp.float32) * scale, 'b_v': jnp.zeros((D_MODEL,), jnp.float32), 'w_o': jax.random.normal(ks[6], (D_MODEL, D_MODEL), jnp.float32) * scale, 'b_o': jnp.zeros((D_MODEL,), jnp.float32)}
        return inp
    _L0_xattn_all = _L0_xattn_setup()
    _L0_xattn_in = {k: v for k, v in _L0_xattn_all.items() if k in ('w_q', 'b_q', 'w_k', 'b_k', 'w_v', 'b_v', 'w_o', 'b_o')}
    del _L0_xattn_all

    def _L0_ffn_setup():
        import jax, jax.numpy as jnp
        import numpy as np
        TOP_K = 2
        NUM_EXPERTS = 8
        key = jax.random.key(seed)
        ks = jax.random.split(key, 8)
        h, d, ds, E = (256, 128, 256, NUM_EXPERTS)
        s = 1.0 / np.sqrt(h)
        return {'x': jax.random.normal(ks[0], (2, 512, h), jnp.float32), 'router': jax.random.normal(ks[1], (h, E), jnp.float32) * s, 'experts_gate': jax.random.normal(ks[2], (E, h, d), jnp.float32) * s, 'experts_up': jax.random.normal(ks[3], (E, h, d), jnp.float32) * s, 'experts_down': jax.random.normal(ks[4], (E, d, h), jnp.float32) * (1.0 / np.sqrt(d)), 'shared_gate': jax.random.normal(ks[5], (h, ds), jnp.float32) * s, 'shared_up': jax.random.normal(ks[6], (h, ds), jnp.float32) * s, 'shared_down': jax.random.normal(ks[7], (ds, h), jnp.float32) * (1.0 / np.sqrt(ds))}
    _L0_ffn_all = _L0_ffn_setup()
    _L0_ffn_in = {k: v for k, v in _L0_ffn_all.items() if k in ('router', 'experts_gate', 'experts_up', 'experts_down', 'shared_gate', 'shared_up', 'shared_down')}
    del _L0_ffn_all

    def _L1_xattn_setup():
        import jax, jax.numpy as jnp
        import numpy as np
        import math
        D_MODEL = 256
        NUM_HEADS = 16
        D_K = D_MODEL // NUM_HEADS
        MAX_LEN = 512
        BATCH = 2
        SEQ = 512
        key = jax.random.key(seed)
        ks = jax.random.split(key, 12)
        w_scale = 0.02
        inp = {'q': jax.random.normal(ks[0], (BATCH, SEQ, D_MODEL), jnp.float32), 'k': jax.random.normal(ks[1], (BATCH, SEQ, D_MODEL), jnp.float32), 'v': jax.random.normal(ks[2], (BATCH, SEQ, D_MODEL), jnp.float32), 'rel_emb': jax.random.normal(ks[3], (2 * MAX_LEN, D_K), jnp.float32), 'wq': jax.random.normal(ks[4], (D_MODEL, D_MODEL), jnp.float32) * w_scale, 'bq': jnp.zeros((D_MODEL,), jnp.float32), 'wk': jax.random.normal(ks[5], (D_MODEL, D_MODEL), jnp.float32) * w_scale, 'bk': jnp.zeros((D_MODEL,), jnp.float32), 'wv': jax.random.normal(ks[6], (D_MODEL, D_MODEL), jnp.float32) * w_scale, 'bv': jnp.zeros((D_MODEL,), jnp.float32), 'wo': jax.random.normal(ks[7], (D_MODEL, D_MODEL), jnp.float32) * w_scale, 'bo': jnp.zeros((D_MODEL,), jnp.float32)}
        return inp
    _L1_xattn_all = _L1_xattn_setup()
    _L1_xattn_in = {k: v for k, v in _L1_xattn_all.items() if k in ('rel_emb', 'wq', 'bq', 'wk', 'bk', 'wv', 'bv', 'wo', 'bo')}
    del _L1_xattn_all

    def _L1_ffn_setup():
        import jax, jax.numpy as jnp
        import numpy as np
        B, S, D_MODEL, D_HIDDEN = (4, 512, 256, 1024)

        def act_quant(x):
            scale = 127.0 / jnp.clip(jnp.max(jnp.abs(x), axis=-1, keepdims=True), 1e-05)
            return jnp.clip(jnp.round(x * scale), -128, 127) / scale

        def weight_quant(w):
            scale = 1.0 / jnp.clip(jnp.mean(jnp.abs(w)), 1e-05)
            return jnp.clip(jnp.round(w * scale), -1, 1) / scale

        def bit_linear(x, w):
            xq = x + jax.lax.stop_gradient(act_quant(x) - x)
            wq = w + jax.lax.stop_gradient(weight_quant(w) - w)
            return jnp.einsum('bsd,hd->bsh', xq, wq)

        def depthwise_conv1d(x_bcl, w, b):
            y = jax.lax.conv_general_dilated(x_bcl, w, window_strides=(1,), padding=[(1, 1)], dimension_numbers=('NCH', 'OIH', 'NCH'), feature_group_count=x_bcl.shape[1])
            return y + b[None, :, None]
        key = jax.random.key(seed)
        ks = jax.random.split(key, 5)
        lim1 = 1.0 / np.sqrt(D_MODEL)
        lim2 = 1.0 / np.sqrt(D_HIDDEN)
        limc = 1.0 / np.sqrt(3.0)
        return {'x': jax.random.normal(ks[0], (B, S, D_MODEL), dtype=jnp.float32), 'w1': jax.random.uniform(ks[1], (D_HIDDEN, D_MODEL), jnp.float32, -lim1, lim1), 'conv_w': jax.random.uniform(ks[2], (D_HIDDEN, 1, 3), jnp.float32, -limc, limc), 'conv_b': jax.random.uniform(ks[3], (D_HIDDEN,), jnp.float32, -limc, limc), 'w2': jax.random.uniform(ks[4], (D_MODEL, D_HIDDEN), jnp.float32, -lim2, lim2)}
    _L1_ffn_all = _L1_ffn_setup()
    _L1_ffn_in = {k: v for k, v in _L1_ffn_all.items() if k in ('w1', 'conv_w', 'conv_b', 'w2')}
    del _L1_ffn_all
    return {'x': x, 'ctx_1024': ctx_1024, 'L0_xattn_w_q': _L0_xattn_in['w_q'], 'L0_xattn_b_q': _L0_xattn_in['b_q'], 'L0_xattn_w_k': _L0_xattn_in['w_k'], 'L0_xattn_b_k': _L0_xattn_in['b_k'], 'L0_xattn_w_v': _L0_xattn_in['w_v'], 'L0_xattn_b_v': _L0_xattn_in['b_v'], 'L0_xattn_w_o': _L0_xattn_in['w_o'], 'L0_xattn_b_o': _L0_xattn_in['b_o'], 'L0_ffn_router': _L0_ffn_in['router'], 'L0_ffn_experts_gate': _L0_ffn_in['experts_gate'], 'L0_ffn_experts_up': _L0_ffn_in['experts_up'], 'L0_ffn_experts_down': _L0_ffn_in['experts_down'], 'L0_ffn_shared_gate': _L0_ffn_in['shared_gate'], 'L0_ffn_shared_up': _L0_ffn_in['shared_up'], 'L0_ffn_shared_down': _L0_ffn_in['shared_down'], 'L1_xattn_rel_emb': _L1_xattn_in['rel_emb'], 'L1_xattn_wq': _L1_xattn_in['wq'], 'L1_xattn_bq': _L1_xattn_in['bq'], 'L1_xattn_wk': _L1_xattn_in['wk'], 'L1_xattn_bk': _L1_xattn_in['bk'], 'L1_xattn_wv': _L1_xattn_in['wv'], 'L1_xattn_bv': _L1_xattn_in['bv'], 'L1_xattn_wo': _L1_xattn_in['wo'], 'L1_xattn_bo': _L1_xattn_in['bo'], 'L1_ffn_w1': _L1_ffn_in['w1'], 'L1_ffn_conv_w': _L1_ffn_in['conv_w'], 'L1_ffn_conv_b': _L1_ffn_in['conv_b'], 'L1_ffn_w2': _L1_ffn_in['w2']}

def reference(x, ctx_1024, L0_xattn_w_q, L0_xattn_b_q, L0_xattn_w_k, L0_xattn_b_k, L0_xattn_w_v, L0_xattn_b_v, L0_xattn_w_o, L0_xattn_b_o, L0_ffn_router, L0_ffn_experts_gate, L0_ffn_experts_up, L0_ffn_experts_down, L0_ffn_shared_gate, L0_ffn_shared_up, L0_ffn_shared_down, L1_xattn_rel_emb, L1_xattn_wq, L1_xattn_bq, L1_xattn_wk, L1_xattn_bk, L1_xattn_wv, L1_xattn_bv, L1_xattn_wo, L1_xattn_bo, L1_ffn_w1, L1_ffn_conv_w, L1_ffn_conv_b, L1_ffn_w2):
    import jax
    import jax.numpy as jnp

    def _L0_xattn_ref(q, k, v, w_q, b_q, w_k, b_k, w_v, b_v, w_o, b_o):
        import jax, jax.numpy as jnp
        import numpy as np
        D_MODEL = 256
        N_HEADS = 16
        D_K = D_MODEL // N_HEADS
        B, S, _ = q.shape

        def proj(x, w, b):
            y = x @ w.T + b
            return y.reshape(B, -1, N_HEADS, D_K).transpose(0, 2, 1, 3)
        qh = proj(q, w_q, b_q)
        kh = proj(k, w_k, b_k)
        vh = proj(v, w_v, b_v)
        scores = jnp.einsum('bhsd,bhtd->bhst', qh, kh) / np.sqrt(D_K)
        attn = jax.nn.softmax(scores, axis=-1)
        out = jnp.einsum('bhst,bhtd->bhsd', attn, vh)
        out = out.transpose(0, 2, 1, 3).reshape(B, S, N_HEADS * D_K)
        return out @ w_o.T + b_o

    def _L0_ffn_ref(x, router, experts_gate, experts_up, experts_down, shared_gate, shared_up, shared_down):
        import jax, jax.numpy as jnp
        import numpy as np
        TOP_K = 2
        NUM_EXPERTS = 8
        b, s, h = x.shape
        E = router.shape[1]
        shared_act = jax.nn.silu(jnp.einsum('bsh,hd->bsd', x, shared_gate))
        shared_up_out = jnp.einsum('bsh,hd->bsd', x, shared_up)
        shared_out = jnp.einsum('bsd,dh->bsh', shared_act * shared_up_out, shared_down)
        router_probs = jax.nn.softmax(jnp.einsum('bsh,he->bse', x, router), axis=-1)
        topk_probs, topk_idx = jax.lax.top_k(router_probs, TOP_K)
        coef = jnp.sum(jax.nn.one_hot(topk_idx, E, dtype=x.dtype) * topk_probs[..., None], axis=2)
        coef = coef.reshape(b * s, E)
        x_flat = x.reshape(b * s, h)
        gate = jnp.einsum('th,ehd->etd', x_flat, experts_gate)
        up = jnp.einsum('th,ehd->etd', x_flat, experts_up)
        expert_out = jnp.einsum('etd,edh->eth', jax.nn.silu(gate) * up, experts_down)
        routed = jnp.einsum('eth,te->th', expert_out, coef)
        return routed.reshape(b, s, h) + shared_out

    def _L1_xattn_ref(q, k, v, rel_emb, wq, bq, wk, bk, wv, bv, wo, bo):
        import jax, jax.numpy as jnp
        import numpy as np
        import math
        D_MODEL = 256
        NUM_HEADS = 16
        D_K = D_MODEL // NUM_HEADS
        MAX_LEN = 512
        BATCH = 2
        SEQ = 512
        B, L, D = q.shape
        H, dk = (NUM_HEADS, D // NUM_HEADS)

        def split_heads(x):
            return x.reshape(B, L, H, dk).transpose(0, 2, 1, 3)
        qh = split_heads(q @ wq.T + bq)
        kh = split_heads(k @ wk.T + bk)
        vh = split_heads(v @ wv.T + bv)
        r = jnp.arange(L)
        rel_pos = r[None, :] - r[:, None] + MAX_LEN
        content_score = jnp.einsum('bhid,bhjd->bhij', qh, kh)
        rel = rel_emb[rel_pos]
        pos_score = jnp.einsum('bhid,ijd->bhij', qh, rel)
        scores = (content_score + pos_score) / math.sqrt(dk)
        attn = jax.nn.softmax(scores, axis=-1)
        out = jnp.einsum('bhij,bhjd->bhid', attn, vh)
        out = out.transpose(0, 2, 1, 3).reshape(B, L, D)
        return out @ wo.T + bo

    def _L1_ffn_ref(x, w1, conv_w, conv_b, w2):
        import jax, jax.numpy as jnp
        import numpy as np
        B, S, D_MODEL, D_HIDDEN = (4, 512, 256, 1024)

        def act_quant(x):
            scale = 127.0 / jnp.clip(jnp.max(jnp.abs(x), axis=-1, keepdims=True), 1e-05)
            return jnp.clip(jnp.round(x * scale), -128, 127) / scale

        def weight_quant(w):
            scale = 1.0 / jnp.clip(jnp.mean(jnp.abs(w)), 1e-05)
            return jnp.clip(jnp.round(w * scale), -1, 1) / scale

        def bit_linear(x, w):
            xq = x + jax.lax.stop_gradient(act_quant(x) - x)
            wq = w + jax.lax.stop_gradient(weight_quant(w) - w)
            return jnp.einsum('bsd,hd->bsh', xq, wq)

        def depthwise_conv1d(x_bcl, w, b):
            y = jax.lax.conv_general_dilated(x_bcl, w, window_strides=(1,), padding=[(1, 1)], dimension_numbers=('NCH', 'OIH', 'NCH'), feature_group_count=x_bcl.shape[1])
            return y + b[None, :, None]
        h = bit_linear(x, w1)
        h = depthwise_conv1d(h.transpose(0, 2, 1), conv_w, conv_b)
        h = h.transpose(0, 2, 1)
        h = jax.nn.silu(h)
        return bit_linear(h, w2)
    x = x + _L0_xattn_ref(_layernorm(x, axis=-1), ctx_1024, ctx_1024, L0_xattn_w_q, L0_xattn_b_q, L0_xattn_w_k, L0_xattn_b_k, L0_xattn_w_v, L0_xattn_b_v, L0_xattn_w_o, L0_xattn_b_o)
    x = x + _L0_ffn_ref(_layernorm(x, axis=-1), L0_ffn_router, L0_ffn_experts_gate, L0_ffn_experts_up, L0_ffn_experts_down, L0_ffn_shared_gate, L0_ffn_shared_up, L0_ffn_shared_down)
    x = x + _L1_xattn_ref(_layernorm(x, axis=-1), ctx_1024, ctx_1024, L1_xattn_rel_emb, L1_xattn_wq, L1_xattn_bq, L1_xattn_wk, L1_xattn_bk, L1_xattn_wv, L1_xattn_bv, L1_xattn_wo, L1_xattn_bo)
    x = x + _L1_ffn_ref(_layernorm(x, axis=-1), L1_ffn_w1, L1_ffn_conv_w, L1_ffn_conv_b, L1_ffn_w2)
    return x

_drawn_inputs = setup_inputs


def setup_inputs(seed=0):
    import zlib

    import numpy as np

    out = dict(_drawn_inputs(seed))
    spreads = {'L0_xattn_b_q': (0.0, 0.273),
     'L0_xattn_b_k': (0.0, 0.8),
     'L0_xattn_b_v': (0.0, 0.1),
     'L0_xattn_b_o': (0.0, 0.1),
     'L1_xattn_bq': (0.0, 0.8),
     'L1_xattn_bk': (0.0, 0.8),
     'L1_xattn_bv': (0.0, 0.35),
     'L1_xattn_bo': (0.0, 0.1)}
    factors = {'L1_xattn_rel_emb': 8.0, 'L1_xattn_wq': 8.0, 'L1_xattn_wk': 8.0}
    for name, (base, spread) in spreads.items():
        noise = np.random.default_rng([zlib.crc32(name.encode()), seed]).standard_normal(out[name].shape)
        drawn = base * np.exp(spread * noise) if base else spread * noise
        out[name] = jnp.asarray(drawn.astype(out[name].dtype))
    for name, factor in factors.items():
        out[name] = (out[name] * factor).astype(out[name].dtype)
    return out
```

```python
from contextlib import ExitStack

import concourse.bass as bass
from concourse import mybir
from concourse.alu_op_type import AluOpType as ALU

F32 = mybir.dt.float32
BF16 = mybir.dt.bfloat16
ACT = mybir.ActivationFunctionType
X = mybir.AxisListType.X

P = 128
D = 256
C = D // P
H = 16
DK = D // H
H8 = H // C
QUADS = H // 4
VW = DK + 1
PARTS = 3
ROWS = 6 * DK
NE = 8
DE = 128
HID = 1024
HC = HID // P
LN_EPS = 1e-5
ROUND = 12582912.0
MAXLEN = 512

ATT = ["L0_xattn_w_q", "L0_xattn_w_k", "L0_xattn_w_v", "L0_xattn_w_o",
       "L1_xattn_wq", "L1_xattn_wk", "L1_xattn_wv", "L1_xattn_wo"]
BIASES = ["L0_xattn_b_q", "L0_xattn_b_k", "L1_xattn_bq", "L1_xattn_bk"]
ROW_BIASES = ["L0_xattn_b_v", "L0_xattn_b_o", "L1_xattn_bv", "L1_xattn_bo"]


class Net:
    pass


class Semaphores:

    def __init__(self, nc, tag):
        self.nc, self.tag, self.all = nc, tag, []

    def __call__(self, name):
        self.all.append(self.nc.alloc_semaphore(f"{self.tag}_{name}"))
        return self.all[-1]

    def release(self):
        self.nc.clear_and_free_semaphores(self.all)
        self.nc.all_engine_barrier()


def at(ap, index):
    return ap[:, bass.ds(index, 1), :].rearrange("p o n -> p (o n)")


def lay_out(nc, ctx, net):
    def sb(name, shape, dt=F32):
        return ctx.enter_context(nc.sbuf_tensor(name, shape, dt))

    net.bank = [ctx.enter_context(nc.psum_tensor(f"bank{i}", [P, 512], F32)) for i in range(8)]
    nb = net.nb
    net.x = sb("x_all", [P, nb, D])
    net.mean = sb("mean_all", [P, nb, 1])
    net.var_eps = sb("var_eps_all", [P, nb, 1])
    net.rstd = sb("rstd_all", [P, nb, 1])
    net.minus_half = sb("minus_half", [P, nb, 1])
    net.wT = sb("wT", [P, 8, C, D])
    net.w1T = sb("w1T", [P, C, HID], BF16)
    net.w2T = sb("w2T", [P, HC, D], BF16)
    net.w_dequant = sb("w_dequant", [P, 2])
    net.conv_w = sb("conv_w", [P, HC, 3])
    net.conv_b = sb("conv_b", [P, HC])
    net.rel = sb("rel", [P, 2 * P], BF16)
    net.bias_col = sb("bias_col", [P, C, 4])
    net.bias_row = sb("bias_row", [P, 4, D])
    net.id_f = sb("id_f", [P, P])
    net.id_b = sb("id_b", [P, P], BF16)
    net.ones_f = sb("ones_f", [P, P])
    net.pick = sb("pick", [PARTS * H, H, P], BF16)


def prepare(nc, net, ins):
    with ExitStack() as ctx:
        def sb(name, shape, dt=F32):
            return ctx.enter_context(nc.sbuf_tensor(name, shape, dt))

        sem = Semaphores(nc, "w")

        raw = sb("raw_att", [P, 8, C, D])
        w_raw = sb("w_raw", [P, 2, 2048])
        w_q = sb("w_q", [P, 2, 2048], BF16)
        w_abs = sb("w_abs", [P, 2])
        w_mean = sb("w_mean", [P, 2])
        w_scale = sb("w_scale", [P, 2])
        rel_raw = sb("rel_raw", [P, 2, DK])
        rel_r1 = sb("rel_r1", [P, 2, DK])
        rel_r2 = sb("rel_r2", [P, 2, DK])
        rel_parts = sb("rel_parts", [P, 2, 6, DK], BF16)
        bias_raw = sb("bias_raw", [4, D])
        conv_b_raw = sb("conv_b_raw", [HC, P])
        bias_apart = sb("bias_apart", [4, C, P])
        stats = sb("stats0", [P, 6])
        agg = sb("agg0", [P, 2])

        att_loaded = sem("att_loaded")
        w12_loaded = sem("w12_loaded")
        x_loaded = sem("x_loaded")
        small_loaded = sem("small_loaded")
        rows_loaded = sem("rows_loaded")
        zeroed = sem("zeroed")
        consts = sem("consts")
        att_done = sem("att_done")
        att_copied = sem("att_copied")
        abs_done = sem("abs_done")
        mean_done = sem("mean_done")
        dve = sem("dve")
        w12_quantised = sem("w12_quantised")
        w12_done = sem("w12_done")
        w12_copied = sem("w12_copied")
        rel_ready = sem("rel_ready")
        rel_done = sem("rel_done")
        bias_ordered = sem("bias_ordered")
        bias_done = sem("bias_done")
        small_copied = sem("small_copied")
        ln = sem("ln")
        nb = net.nb

        with nc.Block() as block:
            @block.sync
            def _(sp):
                for m in range(8):
                    sp.dma_start(raw[:, m, :, :], ins[ATT[m]].rearrange("(c p) i -> p c i", p=P)).then_inc(att_loaded, 16)
                sp.dma_start(w_raw[:, 0, :].rearrange("p (c i) -> p c i", c=HC),
                             ins["L1_ffn_w1"].rearrange("(c p) i -> p c i", p=P)).then_inc(w12_loaded, 16)
                sp.dma_start(w_raw[:, 1, :].rearrange("p (c i) -> p c i", c=C),
                             ins["L1_ffn_w2"].rearrange("(c p) i -> p c i", p=P)).then_inc(w12_loaded, 16)
                for n in range(4):
                    s = slice(n * nb // 4, (n + 1) * nb // 4)
                    sp.dma_start(net.x[:, s, :], ins["x"][s].rearrange("b p d -> p b d")).then_inc(x_loaded, 16)
                for s in (att_loaded,):
                    sp.wait_ge(s, 128)
                sp.wait_ge(x_loaded, 64)
                sp.wait_ge(w12_loaded, 32)

            @block.scalar
            def _(act):
                act.dma_start(rel_raw[:, :, :], ins["L1_xattn_rel_emb"][MAXLEN - P + 1:MAXLEN + P + 1, :]
                              .rearrange("(c p) d -> p c d", p=P)).then_inc(small_loaded, 16)
                for n, name in enumerate(BIASES):
                    act.dma_start(bias_raw[n:n + 1, :], ins[name].rearrange("(a n) -> a n", a=1)).then_inc(small_loaded, 16)
                for n, name in enumerate(ROW_BIASES):
                    act.dma_start(net.bias_row[:, n, :], ins[name].partition_broadcast(P)).then_inc(rows_loaded, 16)
                act.dma_start(net.conv_w[:, :, :], ins["L1_ffn_conv_w"].rearrange("(c p) o k -> p c (o k)", p=P)).then_inc(rows_loaded, 16)
                act.dma_start(conv_b_raw[:, :], ins["L1_ffn_conv_b"].rearrange("(c p) -> c p", p=P)).then_inc(small_loaded, 16)
                act.wait_ge(small_loaded, 96)
                nc.scalar.activation(bias_apart[:, :, :].rearrange("n o (d h) -> n o d h", d=DK),
                                     bias_raw[:, :].rearrange("n (h o d) -> n o d h", o=C, d=DK), ACT.Copy).then_inc(bias_ordered, 1)
                for m in range(8):
                    act.wait_ge(att_done, m + 1)
                    src = net.bank[m % 4][:, :]
                    quarter = 0.25 if m in (0, 4) else 1.0
                    if m % 4 < 2:
                        for c in range(C):
                            i = nc.scalar.activation(
                                net.wT[:, m, c, :].rearrange("p (o d h) -> p o d h", o=C, d=DK),
                                src[:, c * D:(c + 1) * D].rearrange("p (h o d) -> p o d h", o=C, d=DK),
                                ACT.Copy, scale=quarter)
                    else:
                        i = nc.scalar.activation(net.wT[:, m, :, :].rearrange("p c o -> p (c o)"), src, ACT.Copy)
                    i.then_inc(att_copied, 1)
                for n in range(4):
                    act.wait_ge(w12_done, n + 1)
                    src = net.bank[4 + n][:, :].bitcast(BF16)
                    if n < 2:
                        i = nc.scalar.activation(net.w1T[:, n, :], src, ACT.Copy)
                    else:
                        i = nc.scalar.activation(net.w2T[:, :, (n - 2) * P:(n - 1) * P],
                                                 src.rearrange("p (c o) -> p c o", c=HC), ACT.Copy)
                    i.then_inc(w12_copied, 1)
                act.wait_ge(rel_done, 1)
                nc.scalar.activation(net.rel[0:ROWS, :], net.bank[1][0:ROWS, 0:P].bitcast(BF16), ACT.Copy).then_inc(small_copied, 1)
                act.wait_ge(bias_done, 1)
                for o in range(C):
                    nc.scalar.activation(net.bias_col[:, o, 0:4:2], net.bank[0][:, 4 * o:4 * o + 4:2], ACT.Copy, scale=0.25).then_inc(small_copied, 1)
                    nc.scalar.activation(net.bias_col[:, o, 1:4:2], net.bank[0][:, 4 * o + 1:4 * o + 4:2], ACT.Copy).then_inc(small_copied, 1)
                nc.scalar.activation(net.conv_b[:, :], net.bank[0][:, 8:8 + HC], ACT.Copy).then_inc(small_copied, 1)
                act.wait_ge(small_copied, 6)
                act.wait_ge(att_copied, 8)
                act.wait_ge(w12_copied, 4)
                act.wait_ge(rows_loaded, 80)
                act.wait_ge(small_loaded, 96)

            @block.gpsimd
            def _(pool):
                nc.gpsimd.memset(net.id_f[:, :], 0.0).then_inc(zeroed, 1)
                nc.gpsimd.memset(net.id_b[:, :], 0.0).then_inc(zeroed, 1)
                nc.gpsimd.memset(net.pick[:, :, :], 0.0).then_inc(zeroed, 1)
                nc.gpsimd.memset(net.ones_f[:, :], 1.0).then_inc(consts, 1)
                nc.gpsimd.memset(net.minus_half[:, :, :], -0.5).then_inc(consts, 1)
                pool.wait_ge(zeroed, 3)
                for m in (net.id_f, net.id_b):
                    nc.gpsimd.affine_select(out=m[:, :], in_=m[:, :], compare_op=ALU.not_equal, fill=1.0, base=0,
                                            pattern=[[-1, P]], channel_multiplier=1).then_inc(consts, 1)
                for part in range(PARTS):
                    pool.wait_ge(zeroed, 3 + part)
                    nc.gpsimd.affine_select(out=net.pick[:, :, :], in_=net.pick[:, :, :], compare_op=ALU.not_equal,
                                            fill=1.0, base=-part * H, pattern=[[-1, H], [0, P]],
                                            channel_multiplier=1).then_inc(zeroed, 1)
                pool.wait_ge(zeroed, 6)
                pool.wait_ge(ln, 3 * nb)
                pool.wait_ge(consts, 4)
                nc.gpsimd.tensor_tensor(net.rstd[:, :, 0], net.var_eps[:, :, 0], net.minus_half[:, :, 0], ALU.pow).then_inc(consts, 1)
                pool.wait_ge(consts, 5)

            @block.vector
            def _(v):
                step = 0
                v.wait_ge(w12_loaded, 32)
                nc.vector.tensor_reduce(w_abs[:, :], w_raw[:, :, :], X, ALU.add, apply_absolute_value=True).then_inc(abs_done, 1)
                v.wait_ge(mean_done, 1)
                nc.vector.tensor_scalar(w_mean[:, :], net.bank[7][:, 0:2], 1.0 / (HID * D), 1e-5, ALU.mult, ALU.max).then_inc(dve, 1)
                v.wait_ge(dve, 1)
                nc.vector.reciprocal(w_scale[:, :], w_mean[:, :]).then_inc(dve, 1)
                v.wait_ge(dve, 2)
                nc.vector.reciprocal(net.w_dequant[:, :], w_scale[:, :]).then_inc(dve, 1)
                for n in range(2):
                    nc.vector.tensor_scalar(w_raw[:, n, :], w_raw[:, n, :], w_scale[:, n:n + 1], 1.0, ALU.mult, ALU.min).then_inc(dve, 1)
                    v.wait_ge(dve, 4 + 2 * n)
                    nc.vector.tensor_scalar(w_raw[:, n, :], w_raw[:, n, :], -1.0, ROUND, ALU.max, ALU.add).then_inc(dve, 1)
                    v.wait_ge(dve, 5 + 2 * n)
                    nc.vector.tensor_scalar(w_q[:, n, :], w_raw[:, n, :], -ROUND, None, ALU.add).then_inc(w12_quantised, 1)
                v.wait_ge(dve, 7)
                v.wait_ge(small_loaded, 96)
                ra, rb, rc = (rel_parts[:, :, n, :] for n in (2, 1, 0))
                nc.vector.tensor_copy(ra, rel_raw[:, :, :]).then_inc(dve, 1)
                v.wait_ge(dve, 8)
                nc.vector.tensor_tensor(rel_r1[:, :, :], rel_raw[:, :, :], ra, ALU.subtract).then_inc(dve, 1)
                v.wait_ge(dve, 9)
                nc.vector.tensor_copy(rb, rel_r1[:, :, :]).then_inc(dve, 1)
                v.wait_ge(dve, 10)
                nc.vector.tensor_tensor(rel_r2[:, :, :], rel_r1[:, :, :], rb, ALU.subtract).then_inc(dve, 1)
                v.wait_ge(dve, 11)
                nc.vector.tensor_copy(rc, rel_r2[:, :, :]).then_inc(rel_ready, 1)
                nc.vector.tensor_copy(rel_parts[:, :, 3, :], rb).then_inc(rel_ready, 1)
                nc.vector.tensor_copy(rel_parts[:, :, 4, :], ra).then_inc(rel_ready, 1)
                nc.vector.tensor_copy(rel_parts[:, :, 5, :], ra).then_inc(rel_ready, 1)
                v.wait_ge(x_loaded, 64)
                with v.Fori(0, nb) as b:
                    nc.vector.bn_stats(stats[:, :], at(net.x, b)).then_inc(ln, 1)
                    apart(v, ln, 3 * b + 1)
                    nc.vector.bn_aggr(agg[:, :], stats[:, :]).then_inc(ln, 1)
                    v.wait_ge(ln, 3 * b + 2)
                    nc.vector.tensor_scalar(at(net.var_eps, b), agg[:, 1:2], LN_EPS, None, ALU.add)
                    nc.vector.tensor_copy(at(net.mean, b), agg[:, 0:1]).then_inc(ln, 1)
                    apart(v, ln, 3 * b + 3)

            @block.tensor
            def _(pe):
                pe.wait_ge(consts, 4)
                pe.wait_ge(att_loaded, 128)
                for m in range(8):
                    if m >= 4:
                        pe.wait_ge(att_copied, m - 3)
                    for c in range(C):
                        for o in range(C):
                            i = nc.tensor.transpose(net.bank[m % 4][:, (c * C + o) * P:(c * C + o + 1) * P],
                                                    raw[:, m, o, c * P:(c + 1) * P], net.id_f[:, :])
                    i.then_inc(att_done, 1)
                pe.wait_ge(abs_done, 1)
                nc.tensor.matmul(net.bank[7][:, 0:2], net.ones_f[:, :], w_abs[:, :], start=True, stop=True).then_inc(mean_done, 1)
                pe.wait_ge(w12_quantised, 2)
                pe.wait_ge(dve, 1)
                for n in range(4):
                    dst = net.bank[4 + n][:, :].bitcast(BF16)
                    for c in range(HC):
                        if n < 2:
                            src = w_q[:, 0, c * D + n * P:c * D + (n + 1) * P]
                        else:
                            src = w_q[:, 1, (n - 2) * HID + c * P:(n - 2) * HID + (c + 1) * P]
                        i = nc.tensor.transpose(dst[:, c * P:(c + 1) * P], src, net.id_b[:, :])
                    i.then_inc(w12_done, 1)
                pe.wait_ge(att_copied, 8)
                pe.wait_ge(rel_ready, 4)
                for c in range(2):
                    i = nc.tensor.transpose(net.bank[1][0:ROWS, 0:P].bitcast(BF16)[:, c * P:(c + 1) * P],
                                            rel_parts[:, c, :, :].rearrange("p n d -> p (n d)"), net.id_b[:, :])
                i.then_inc(rel_done, 1)
                pe.wait_ge(small_loaded, 96)
                pe.wait_ge(bias_ordered, 1)
                for o in range(C):
                    i = nc.tensor.transpose(net.bank[0][:, 4 * o:4 * o + 4], bias_apart[:, o, :], net.id_f[0:4, 0:4])
                i = nc.tensor.transpose(net.bank[0][:, 8:8 + HC], conv_b_raw[:, :], net.id_f[0:HC, 0:HC])
                i.then_inc(bias_done, 1)
        sem.release()


def project(nc, net, layer, with_context, ins):
    tag = f"p{layer}"
    pairs = net.nb // 2
    jobs = [(4 * layer, 2 * layer, net.q_scr[layer], (0, 1, 2))]
    if with_context:
        jobs += [(1, 1, net.k_scr[0], (2, 1, 0)), (5, 3, net.k_scr[1], (2, 1, 0))]
    nj = len(jobs)
    values = [(2, 0, net.v_scr[0]), (6, 2, net.v_scr[1])] if with_context else []
    with ExitStack() as ctx:
        def sb(name, shape, dt=F32):
            return ctx.enter_context(nc.sbuf_tensor(f"{tag}_{name}", shape, dt))

        sem = Semaphores(nc, tag)

        normed = sb("normed", [P, 2, 2, D])
        ctx_in = sb("ctx_in", [P, 2, 2, D])
        xT = sb("xT", [P, 2, C, 2 * P])
        cT = sb("cT", [P, 2, C, 2 * P])
        parts = [sb(f"parts{j}", [P, 2, PARTS, C * 2 * P], BF16) for j in range(nj)]
        rest = [sb(f"rest{j}", [P, 2, C * 2 * P]) for j in range(nj)]
        val = [sb(f"val{j}", [P, 2, 2, H, VW]) for j in range(len(values))]

        ctx_loaded = [sem(f"ctx_loaded{i}") for i in range(2)]
        normed_ready = sem("normed_ready")
        xT_done = sem("xT_done")
        cT_done = sem("cT_done")
        xT_copied = sem("xT_copied")
        cT_copied = sem("cT_copied")
        proj_done = [sem(f"proj_done{j}") for j in range(nj)]
        val_done = [sem(f"val_done{j}") for j in range(len(values))]
        part_a = [sem(f"part_a{j}") for j in range(nj)]
        rest1 = [sem(f"rest1_{j}") for j in range(nj)]
        part_b = [sem(f"part_b{j}") for j in range(nj)]
        part_c = [sem(f"part_c{j}") for j in range(nj)]
        val_ready = [sem(f"val_ready{j}") for j in range(len(values))]
        ones = sem("ones")
        stored = [sem(f"stored{i}") for i in range(2)]
        per_store = 16 * (nj + len(values))
        bank_x, bank_c = net.bank[0], net.bank[1]
        bank_j = net.bank[2:2 + nj]
        bank_v = net.bank[5:7]

        with nc.Block() as block:
            @block.sync
            def _(sp):
                def load(p, u):
                    sp.dma_start(ctx_in[:, u, :, :], ins["ctx_1024"].rearrange("(n b) p d -> n p b d", b=2)[bass.ds(p, 1)]
                                 .rearrange("n p b d -> p (n b) d")).then_inc(ctx_loaded[u], 16)

                def store(p, u):
                    for j, (_, _, scr, _) in enumerate(jobs):
                        sp.wait_ge(part_c[j], p + 1)
                        sp.wait_ge(part_b[j], p + 1)
                        sp.dma_start(scr.rearrange("n k p t -> n p k t")[bass.ds(p, 1)].rearrange("n p k t -> p (n k) t"),
                                     parts[j][:, u, :, :]).then_inc(stored[u], 16)
                    for j, (_, _, scr) in enumerate(values):
                        sp.wait_ge(val_ready[j], p + 1)
                        sp.dma_start(scr[bass.ds(p, 1)].rearrange("n p t -> p (n t)"),
                                     val[j][:, u, :, :, :].rearrange("p b h w -> p (b h w)")).then_inc(stored[u], 16)

                if with_context:
                    load(0, 0)
                    load(1, 1)
                with sp.Fori(0, pairs // 2 - 1) as t:
                    for u in range(2):
                        store(2 * t + u, u)
                        if with_context:
                            sp.wait_ge(cT_done, 2 * t + u + 1)
                            load(2 * t + u + 2, u)
                for u in range(2):
                    store(pairs - 2 + u, u)
                for u in range(2):
                    sp.wait_ge(stored[u], per_store * (pairs // 2))

            @block.vector
            def _(v):
                def norm(p, u, first):
                    if not first:
                        v.wait_ge(xT_done, p - 1)
                    for s in range(2):
                        i = nc.vector.tensor_scalar(normed[:, u, s, :], at(net.x, 2 * p + s), at(net.mean, 2 * p + s),
                                                    at(net.rstd, 2 * p + s), ALU.subtract, ALU.mult)
                    i.then_inc(normed_ready, 1)

                def work(p, u, first, t):
                    for j, (_, bias, _, _) in enumerate(jobs):
                        v.wait_ge(part_a[j], p + 1)
                        if not first:
                            v.wait_ge(part_c[j], p - 1)
                        for o in range(C):
                            s = slice(o * 2 * P, (o + 1) * 2 * P)
                            i = nc.vector.scalar_tensor_tensor(
                                out=rest[j][:, u, s], in0=bank_j[j][:, s], scalar=net.bias_col[:, o, bias:bias + 1],
                                in1=parts[j][:, u, jobs[j][3].index(0), s], op0=ALU.add, op1=ALU.subtract)
                        i.then_inc(rest1[j], 1)
                    for j, (_, bias, _) in enumerate(values):
                        v.wait_ge(val_done[j], p + 1)
                        if not first:
                            v.wait_ge(stored[u], per_store * t)
                        for s in range(2):
                            i = nc.vector.tensor_tensor(
                                val[j][:, u, s, :, 0:DK], bank_v[j][:, s * D:(s + 1) * D].rearrange("p (h w) -> p h w", w=DK),
                                net.bias_row[:, bias, :].rearrange("p (h w) -> p h w", w=DK), ALU.add)
                        i.then_inc(val_ready[j], 1)

                for j in range(len(values)):
                    for u in range(2):
                        nc.vector.memset(val[j][:, u, :, :, DK:VW], 1.0).then_inc(ones, 1)
                if values:
                    v.wait_ge(ones, 2 * len(values))
                norm(0, 0, True)
                norm(1, 1, True)
                for u in range(2):
                    work(u, u, True, 0)
                    norm(2 + u, u, False)
                with v.Fori(1, pairs // 2 - 1) as t:
                    for u in range(2):
                        work(2 * t + u, u, False, t)
                        norm(2 * t + u + 2, u, False)
                for u in range(2):
                    work(pairs - 2 + u, u, False, pairs // 2 - 1)

            @block.scalar
            def _(act):
                def work(p, u, first, t):
                    act.wait_ge(xT_done, p + 1)
                    if not first:
                        act.wait_ge(proj_done[0], p - 1)
                    nc.scalar.activation(xT[:, u, :, :].rearrange("p c t -> p (c t)"), bank_x[:, :], ACT.Copy).then_inc(xT_copied, 1)
                    if with_context:
                        act.wait_ge(cT_done, p + 1)
                        if not first:
                            act.wait_ge(val_done[1], p - 1)
                        nc.scalar.activation(cT[:, u, :, :].rearrange("p c t -> p (c t)"), bank_c[:, :], ACT.Copy).then_inc(cT_copied, 1)
                    if not first:
                        act.wait_ge(stored[u], per_store * t)
                    for j, (_, bias, _, order) in enumerate(jobs):
                        act.wait_ge(proj_done[j], p + 1)
                        for o in range(C):
                            s = slice(o * 2 * P, (o + 1) * 2 * P)
                            i = nc.scalar.activation(parts[j][:, u, order.index(0), s], bank_j[j][:, s], ACT.Identity,
                                                     bias=net.bias_col[:, o, bias:bias + 1])
                        i.then_inc(part_a[j], 1)

                for u in range(2):
                    work(u, u, True, 0)
                with act.Fori(1, pairs // 2) as t:
                    for u in range(2):
                        work(2 * t + u, u, False, t)

            @block.gpsimd
            def _(pool):
                def work(p, u, first, t):
                    for j, (_, _, _, order) in enumerate(jobs):
                        ge(pool, rest1[j], p + 1)
                        if not first:
                            apart(pool, stored[u], per_store * t)
                        nc.gpsimd.tensor_copy(parts[j][:, u, order.index(1), :], rest[j][:, u, :]).then_inc(part_b[j], 1)
                        pool.wait_ge(part_b[j], p + 1)
                        nc.gpsimd.tensor_tensor(parts[j][:, u, order.index(2), :], rest[j][:, u, :],
                                                parts[j][:, u, order.index(1), :], ALU.subtract).then_inc(part_c[j], 1)

                for u in range(2):
                    work(u, u, True, 0)
                with pool.Fori(1, pairs // 2) as t:
                    for u in range(2):
                        work(2 * t + u, u, False, t)

            @block.tensor
            def _(pe):
                def turn(p, u, first, loads):
                    pe.wait_ge(normed_ready, p + 1)
                    if not first:
                        pe.wait_ge(xT_copied, p)
                    for c in range(C):
                        for s in range(2):
                            i = nc.tensor.transpose(bank_x[:, (c * 2 + s) * P:(c * 2 + s + 1) * P],
                                                    normed[:, u, s, c * P:(c + 1) * P], net.id_f[:, :])
                    i.then_inc(xT_done, 1)
                    if with_context:
                        if not first:
                            pe.wait_ge(cT_copied, p)
                        pe.wait_ge(ctx_loaded[u], 16 * loads)
                        for c in range(C):
                            for s in range(2):
                                i = nc.tensor.transpose(bank_c[:, (c * 2 + s) * P:(c * 2 + s + 1) * P],
                                                        ctx_in[:, u, s, c * P:(c + 1) * P], net.id_f[:, :])
                        i.then_inc(cT_done, 1)

                def products(p, u, first):
                    pe.wait_ge(xT_copied, p + 1)
                    for j, (m, _, _, _) in enumerate(jobs):
                        src = xT if j == 0 else cT
                        if j == 1:
                            pe.wait_ge(cT_copied, p + 1)
                        if not first:
                            pe.wait_ge(rest1[j], p)
                        for o in range(C):
                            for c in range(C):
                                i = nc.tensor.matmul(bank_j[j][:, o * 2 * P:(o + 1) * 2 * P], net.wT[:, m, c, o * P:(o + 1) * P],
                                                     src[:, u, c, :], start=(c == 0), stop=(c == C - 1))
                        i.then_inc(proj_done[j], 1)
                    for j, (m, _, _) in enumerate(values):
                        if not first:
                            pe.wait_ge(val_ready[j], p)
                        for s in range(2):
                            for c in range(C):
                                i = nc.tensor.matmul(bank_v[j][:, s * D:(s + 1) * D], cT[:, u, c, s * P:(s + 1) * P],
                                                     net.wT[:, m, c, :], start=(c == 0), stop=(c == C - 1))
                        i.then_inc(val_done[j], 1)

                turn(0, 0, True, 1)
                turn(1, 1, False, 1)
                products(0, 0, True)
                turn(2, 0, False, 2)
                products(1, 1, False)
                with pe.Fori(1, pairs // 2 - 1) as t:
                    turn(2 * t + 1, 1, False, t + 1)
                    products(2 * t, 0, False)
                    turn(2 * t + 2, 0, False, t + 2)
                    products(2 * t + 1, 1, False)
                turn(pairs - 1, 1, False, pairs // 2)
                products(pairs - 2, 0, False)
                products(pairs - 1, 1, False)
        sem.release()


def pipeline(engine, nb, slot):
    groups = nb // 4
    for u in range(4):
        slot(u, u, 0)
    with engine.Fori(1, groups - 1) as t:
        for u in range(4):
            slot(4 * t + u, u, t)
    for u in range(4):
        slot(nb - 4 + u, u, groups - 1)
    for u in range(2):
        slot(nb + u, u, groups)


def ge(engine, semaphore, value):
    if not (isinstance(value, int) and value <= 0):
        engine.wait_ge(semaphore, value)


def apart(engine, semaphore, value):
    ge(engine, semaphore, value)
    if not isinstance(value, int):
        engine.nop(nofuse=True)


def attend(nc, net, layer):
    tag = f"a{layer}"
    nb = net.nb
    pos = layer == 1
    m_out = 4 * layer + 3
    with ExitStack() as ctx:
        def sb(name, shape, dt=F32):
            return ctx.enter_context(nc.sbuf_tensor(f"{tag}_{name}", shape, dt))

        sem = Semaphores(nc, tag)

        qr = sb("q_rows", [ROWS, 2, H, 2, P], BF16)
        kr = sb("k_rows", [ROWS, 2, H, 2, P], BF16)
        val = sb("values", [P, 2, 2, H, VW])
        probs = sb("probs", [P, 2, H, P])
        neg_max = sb("neg_max", [P, 2, H])
        neg_rest = sb("neg_rest", [P, H])
        neg_parts = sb("neg_parts", [P, 2, PARTS, H], BF16)
        neg_rows = sb("neg_rows", [PARTS * H, 2, P], BF16)
        sums = sb("recip_sums", [P, H])
        attn = sb("attn", [P, D])
        attnT = sb("attnT", [P, C, P])
        x_bias = sb("x_bias", [P, 2, D])
        stats = sb("stats", [P, 6])
        agg = sb("agg", [P, 2])
        if pos:
            pos_T = sb("pos_T", [P, 2, P, 2 * H])
            s_T = sb("scores_T", [P, 2, H, P])

        qk_loaded = [sem(f"qk_loaded{g}") for g in range(2)]
        v_loaded = [sem(f"v_loaded{g}") for g in range(2)]
        scores_done = sem("scores_done")
        added = sem("added")
        turned = sem("turned")
        max_done = sem("max_done")
        neg_step = sem("neg_step")
        neg_ready = sem("neg_ready")
        rows_done = sem("rows_done")
        rows_copied = sem("rows_copied")
        shifted = sem("shifted")
        z_ready = sem("z_ready")
        probs_ready = sem("probs_ready")
        pv_done = sem("pv_done")
        recip = sem("recip")
        attn_ready = sem("attn_ready")
        attnT_done = sem("attnT_done")
        attnT_copied = sem("attnT_copied")
        out_done = sem("out_done")
        x_biased = sem("x_biased")
        x_added = sem("x_added")
        ln = sem("ln")
        stats_ready = sem("stats_ready")
        final = sem("final")
        pos_done = sem("pos_done")
        pos_copied = sem("pos_copied")

        bank_s = net.bank[0:2]
        bank_t = net.bank[2:4]
        bank_pv = net.bank[4]
        bank_turn = net.bank[5]
        bank_pos = net.bank[6]
        bank_misc = net.bank[7]
        FILLS = 8
        fill = P // FILLS

        with nc.Block() as block:
            @block.sync
            def _(sp):
                def load(p, g, first):
                    if not first:
                        sp.wait_ge(scores_done if pos else shifted, 8 * p - 8)
                    for r0, r1, c0, c1 in ((0, 3, 0, 3), (3, 5, 0, 2), (5, 6, 0, 1)):
                        for dst, scr, lo in ((qr, net.q_scr[layer], c0), (kr, net.k_scr[layer], PARTS - (c1 - c0))):
                            sp.dma_start(
                                dst[r0 * DK:r1 * DK, g, :, :, :].rearrange("r h b t -> r (h b t)"),
                                scr.rearrange("n k (d h) t -> n (k d) (h t)", d=DK)[bass.ds(p, 1), lo * DK:(lo + c1 - c0) * DK, :]
                                .rearrange("n r t -> (n r) t")).then_inc(qk_loaded[g], 16)
                    if not first:
                        sp.wait_ge(pv_done, 2 * p - 2)
                    sp.dma_start(val[:, g, :, :, :].rearrange("p b h w -> p (b h w)"),
                                 net.v_scr[layer][bass.ds(p, 1)].rearrange("n p t -> (n p) t")).then_inc(v_loaded[g], 16)

                for g in range(2):
                    load(g, g, True)
                with sp.Fori(1, nb // 4) as t:
                    for g in range(2):
                        load(2 * t + g, g, False)

            def active(k, u, t):
                static = isinstance(k, int)
                return (not static or k < nb, not static or 1 <= k <= nb, not static or k >= 2)

            @block.tensor
            def _(pe):
                def scores(k, u, q):
                    g, b = u // 2, u % 2
                    ge(pe, added if pos else max_done, 4 * k + q - 1)
                    for n in range(4):
                        h = 4 * q + n
                        a, o = (kr, qr) if pos else (qr, kr)
                        i = nc.tensor.matmul(bank_s[q % 2][:, n * P:(n + 1) * P], a[0:ROWS, g, h, b, :], o[0:ROWS, g, h, b, :],
                                             start=True, stop=True)
                    i.then_inc(scores_done, 1)

                def turn(k, u, q):
                    pe.wait_ge(added, 4 * k + q + 1)
                    ge(pe, max_done, 4 * k + q)
                    for n in range(4):
                        i = nc.tensor.transpose(bank_turn[:, n * P:(n + 1) * P], s_T[:, u % 2, 4 * q + n, :], net.id_f[:, :])
                    i.then_inc(turned, 1)

                def shift(m, u, q):
                    g, b = ((u - 1) % 4) // 2, (u - 1) % 2
                    if q == 0:
                        pe.wait_ge(rows_copied, m + 1)
                    ge(pe, z_ready if pos else probs_ready, 4 * m + q - 1)
                    for n in range(4):
                        h = 4 * q + n
                        dst = bank_t[q % 2][:, n * P:(n + 1) * P]
                        if not pos:
                            nc.tensor.matmul(dst, kr[0:ROWS, g, h, b, :], qr[0:ROWS, g, h, b, :], start=True, stop=False)
                        i = nc.tensor.matmul(dst, net.pick[:, h, :], neg_rows[:, b, :], start=pos, stop=True)
                    i.then_inc(shifted, 1)

                def weigh(n, u, t):
                    g, b = ((u - 2) % 4) // 2, u % 2
                    pe.wait_ge(v_loaded[g], 16 * (t + 1 if u >= 2 else t))
                    ge(pe, attn_ready, n)
                    for q in range(QUADS):
                        pe.wait_ge(probs_ready, 4 * n + q + 1)
                        for j in range(4):
                            h = 4 * q + j
                            i = nc.tensor.matmul(bank_pv[:, h * VW:(h + 1) * VW], probs[:, b, h, :], val[:, g, b, h, :],
                                                 start=True, stop=True)
                    i.then_inc(pv_done, 1)

                def positions(p, g, f):
                    ge(pe, pos_copied, FILLS * p + f)
                    for n in range(fill):
                        i0 = f * fill + n
                        i = nc.tensor.matmul(bank_pos[:, n * 2 * H:(n + 1) * 2 * H], net.rel[0:ROWS, P - 1 - i0:2 * P - 1 - i0],
                                             qr[0:ROWS, g, :, :, i0],
                                             start=True, stop=True)
                    i.then_inc(pos_done, 1)

                def slot(k, u, t):
                    do_s, do_e, do_o = active(k, u, t)
                    m, n = k - 1, k - 2
                    next_pair, fills = None, []
                    if pos and do_s and u % 2 and not (isinstance(k, int) and k == nb - 1):
                        next_pair, g2 = (2 * t + 1, 1) if u == 1 else (2 * t + 2, 0)
                        fills = list(range(FILLS))
                        pe.wait_ge(qk_loaded[g2], 96 * (t + 1 if u == 1 else t + 2))

                    def some():
                        for f in (fills.pop(0), fills.pop(0)) if fills else ():
                            positions(next_pair, g2, f)

                    if do_o:
                        weigh(n, u, t)
                    if do_s:
                        pe.wait_ge(qk_loaded[u // 2], 96 * (t + 1))
                        scores(k, u, 0)
                        scores(k, u, 1)
                    some()
                    if do_o:
                        pe.wait_ge(attn_ready, n + 1)
                        ge(pe, rows_copied, n + 2 if do_e else nb)
                        ge(pe, x_added, n)
                        for c in range(C):
                            i = nc.tensor.transpose(bank_misc[:, c * P:(c + 1) * P], attn[:, c * P:(c + 1) * P], net.id_f[:, :])
                        i.then_inc(attnT_done, 1)
                    if do_e:
                        shift(m, u, 0)
                        shift(m, u, 1)
                    some()
                    for q in (0, 1):
                        if do_s:
                            if pos:
                                turn(k, u, q)
                            scores(k, u, q + 2)
                    some()
                    if do_e:
                        shift(m, u, 2)
                        shift(m, u, 3)
                    if do_o:
                        pe.wait_ge(attnT_copied, n + 1)
                        for c in range(C):
                            i = nc.tensor.matmul(bank_misc[:, 0:D], attnT[:, c, :], net.wT[:, m_out, c, :], start=(c == 0), stop=(c == C - 1))
                        i.then_inc(out_done, 1)
                    some()
                    if do_s and pos:
                        turn(k, u, 2)
                        turn(k, u, 3)
                    if do_s:
                        pe.wait_ge(neg_ready, k + 1)
                        ge(pe, x_added, n + 1)
                        apart(pe, rows_copied, k)
                        nc.tensor.transpose(bank_misc[0:PARTS * H, 0:P // 2].bitcast(BF16),
                                            neg_parts[:, u % 2, :, :].rearrange("p n h -> p (n h)"), net.id_b[:, :]).then_inc(rows_done, 1)

                if pos:
                    pe.wait_ge(qk_loaded[0], 96)
                    for f in range(FILLS):
                        positions(0, 0, f)
                pipeline(pe, nb, slot)

            @block.scalar
            def _(act):
                def copy_positions(p, g, f):
                    act.wait_ge(pos_done, FILLS * p + f + 1)
                    if f == 0:
                        ge(act, added, 8 * p - 8)
                    nc.scalar.activation(pos_T[:, g, f * fill:(f + 1) * fill, :].rearrange("p i n -> p (i n)"), bank_pos[:, :],
                                         ACT.Copy).then_inc(pos_copied, 1)

                def exponential(m, u, q):
                    b = (u - 1) % 2
                    act.wait_ge(z_ready if pos else shifted, 4 * m + q + 1)
                    if q == 0:
                        ge(act, pv_done, m - 1)
                    dst = probs[:, b, 4 * q:4 * q + 4, :].rearrange("p h t -> p (h t)")
                    src = s_T[:, b, 4 * q:4 * q + 4, :].rearrange("p h t -> p (h t)") if pos else bank_t[q % 2][:, :]
                    nc.scalar.activation(dst, src, ACT.Exp).then_inc(probs_ready, 1)

                def slot(k, u, t):
                    do_s, do_e, do_o = active(k, u, t)
                    m, n = k - 1, k - 2
                    next_pair, fills = None, []
                    if pos and do_s and u % 2 and not (isinstance(k, int) and k == nb - 1):
                        next_pair, g2 = (2 * t + 1, 1) if u == 1 else (2 * t + 2, 0)
                        fills = list(range(FILLS))

                    def some():
                        for f in (fills.pop(0), fills.pop(0)) if fills else ():
                            copy_positions(next_pair, g2, f)

                    some()
                    if do_o:
                        act.wait_ge(attnT_done, n + 1)
                        ge(act, out_done, n)
                        nc.scalar.activation(attnT[:, :, :].rearrange("p c t -> p (c t)"), bank_misc[:, 0:D], ACT.Copy).then_inc(attnT_copied, 1)
                    some()
                    if do_e:
                        exponential(m, u, 0)
                        exponential(m, u, 1)
                    some()
                    if do_e:
                        exponential(m, u, 2)
                        exponential(m, u, 3)
                    some()
                    if do_s:
                        act.wait_ge(rows_done, k + 1)
                        ge(act, shifted, 4 * k - 4)
                        nc.scalar.activation(neg_rows[:, u % 2, :], bank_misc[0:PARTS * H, 0:P // 2].bitcast(BF16), ACT.Copy).then_inc(rows_copied, 1)

                if pos:
                    for f in range(FILLS):
                        copy_positions(0, 0, f)
                pipeline(act, nb, slot)

            @block.gpsimd
            def _(pool):
                def slot(k, u, t):
                    do_s, do_e, do_o = active(k, u, t)
                    if do_o:
                        n = k - 2
                        ge(pool, x_added, n - 1)
                        nc.gpsimd.tensor_tensor(x_bias[:, u % 2, :], at(net.x, n), net.bias_row[:, 2 * layer + 1, :], ALU.add).then_inc(x_biased, 1)
                    if do_s:
                        b = u % 2
                        a, bb, c = (neg_parts[:, b, n, :] for n in range(PARTS))
                        pool.wait_ge(max_done, 4 * k + 4)
                        apart(pool, rows_done, k - 1)
                        nc.gpsimd.tensor_copy(a, neg_max[:, b, :]).then_inc(neg_step, 1)
                        pool.wait_ge(neg_step, 3 * k + 1)
                        nc.gpsimd.tensor_tensor(neg_rest[:, :], neg_max[:, b, :], a, ALU.subtract).then_inc(neg_step, 1)
                        apart(pool, neg_step, 3 * k + 2)
                        nc.gpsimd.tensor_copy(bb, neg_rest[:, :]).then_inc(neg_step, 1)
                        pool.wait_ge(neg_step, 3 * k + 3)
                        nc.gpsimd.tensor_tensor(c, neg_rest[:, :], bb, ALU.subtract).then_inc(neg_ready, 1)

                pipeline(pool, nb, slot)
                pool.wait_ge(stats_ready, nb)
                nc.gpsimd.tensor_tensor(net.rstd[:, :, 0], net.var_eps[:, :, 0], net.minus_half[:, :, 0], ALU.pow).then_inc(final, 1)
                pool.wait_ge(final, 1)

            @block.vector
            def _(v):
                def quad(ap, q):
                    return ap[:, 4 * q:4 * q + 4, :]

                def maximum(k, u, q):
                    v.wait_ge(turned if pos else scores_done, 4 * k + q + 1)
                    if q == 0:
                        ge(v, neg_ready, k - 1)
                    src = (bank_turn if pos else bank_s[q % 2])[:, :].rearrange("p (h t) -> p h t", h=4)
                    nc.vector.tensor_reduce(neg_max[:, u % 2, 4 * q:4 * q + 4], src, X, ALU.max, negate=True).then_inc(max_done, 1)

                def add_positions(k, u, q, pair):
                    v.wait_ge(scores_done, 4 * k + q + 1)
                    ge(v, probs_ready, 4 * k + q - 7)
                    if q == 0:
                        v.wait_ge(pos_copied, FILLS * (pair + 1))
                    nc.vector.tensor_tensor(quad(s_T[:, u % 2, :, :], q), bank_s[q % 2][:, :].rearrange("p (h t) -> p h t", h=4),
                                            pos_T[:, u // 2, :, :].rearrange("p i (h b) -> p b h i", b=2)[:, u % 2, 4 * q:4 * q + 4, :],
                                            ALU.add).then_inc(added, 1)

                def add_shift(m, u, q):
                    b = (u - 1) % 2
                    v.wait_ge(shifted, 4 * m + q + 1)
                    z = quad(s_T[:, b, :, :], q)
                    nc.vector.tensor_tensor(z, bank_t[q % 2][:, :].rearrange("p (h t) -> p h t", h=4), z, ALU.add).then_inc(z_ready, 1)

                def slot(k, u, t):
                    do_s, do_e, do_o = active(k, u, t)
                    m, n = k - 1, k - 2
                    if do_o:
                        v.wait_ge(pv_done, n + 1)
                        out = bank_pv[:, 0:H * VW].rearrange("p (h w) -> p h w", w=VW)
                        nc.vector.reciprocal(sums[:, :], out[:, :, DK]).then_inc(recip, 1)
                        v.wait_ge(recip, n + 1)
                        ge(v, attnT_done, n)
                        nc.vector.tensor_tensor(attn[:, :].rearrange("p (h w) -> p h w", w=DK), out[:, :, 0:DK],
                                                sums[:, :].unsqueeze(2).to_broadcast([P, H, DK]), ALU.mult).then_inc(attn_ready, 1)
                    if pos:
                        if do_s:
                            add_positions(k, u, 0, 2 * t + u // 2)
                            add_positions(k, u, 1, 2 * t + u // 2)
                        if do_e:
                            add_shift(m, u, 0)
                            add_shift(m, u, 1)
                        if do_s:
                            maximum(k, u, 0)
                            add_positions(k, u, 2, 2 * t + u // 2)
                            maximum(k, u, 1)
                            add_positions(k, u, 3, 2 * t + u // 2)
                        if do_e:
                            add_shift(m, u, 2)
                            add_shift(m, u, 3)
                    elif do_s:
                        for q in range(QUADS):
                            maximum(k, u, q)
                    if do_o:
                        v.wait_ge(out_done, n + 1)
                        v.wait_ge(x_biased, n + 1)
                        nc.vector.tensor_tensor(at(net.x, n), bank_misc[:, 0:D], x_bias[:, u % 2, :], ALU.add).then_inc(x_added, 1)
                    if do_s and pos:
                        maximum(k, u, 2)
                        maximum(k, u, 3)
                    if do_o:
                        apart(v, x_added, n + 1)
                        nc.vector.bn_stats(stats[:, :], at(net.x, n)).then_inc(ln, 1)
                        apart(v, ln, 2 * n + 1)
                        nc.vector.bn_aggr(agg[:, :], stats[:, :]).then_inc(ln, 1)
                        v.wait_ge(ln, 2 * n + 2)
                        nc.vector.tensor_scalar(at(net.var_eps, n), agg[:, 1:2], LN_EPS, None, ALU.add)
                        nc.vector.tensor_copy(at(net.mean, n), agg[:, 0:1]).then_inc(stats_ready, 1)

                pipeline(v, nb, slot)
                v.wait_ge(stats_ready, nb)
        sem.release()


def experts(nc, net, ins):
    nb = net.nb
    with ExitStack() as ctx:
        def sb(name, shape, dt=F32):
            return ctx.enter_context(nc.sbuf_tensor(f"m_{name}", shape, dt))

        sem = Semaphores(nc, "m")

        NC = NE + C
        gate = sb("gate", [P, C, NE, DE])
        up = sb("up", [P, C, NE, DE])
        shared = sb("shared", [P, C, 2, D])
        down = sb("down", [P, NC, D])
        router = sb("router", [P, C, NE])
        normed = sb("normed", [P, 2, D])
        xT = sb("xT", [P, 2, C, P])
        tanh = sb("tanh", [P, 3, 512])
        gated = sb("gated", [P, 3, 512])
        acts = sb("acts", [P, NC, P])
        actsT = sb("actsT", [P, NC, P])
        top = sb("top", [P, 8])
        neg_top = sb("neg_top", [P, 1])
        expd = sb("expd", [P, NE])
        exp_sum = sb("exp_sum", [P, 1])
        recip = sb("recip", [P, 1])
        prob = sb("prob", [P, 16])
        best = sb("best", [P, 8])
        left = sb("left", [P, 16])
        coef = sb("coef", [P, 2, NE])
        stats = sb("stats", [P, 6])
        agg = sb("agg", [P, 2])

        loaded = sem("loaded")
        filled = sem("filled")
        normed_ready = sem("normed_ready")
        xT_done = sem("xT_done")
        xT_copied = sem("xT_copied")
        logits_done = sem("logits_done")
        route = sem("route")
        exp_ready = sem("exp_ready")
        unit_done = sem("unit_done")
        tanh_ready = sem("tanh_ready")
        gated_ready = sem("gated_ready")
        acts_ready = sem("acts_ready")
        actsT_done = sem("actsT_done")
        actsT_copied = sem("actsT_copied")
        out_done = sem("out_done")
        x_added = sem("x_added")
        ln = sem("ln")
        stats_ready = sem("stats_ready")
        final = sem("final")

        bank_x = net.bank[0]
        logits = bank_x[:, D:D + NE]
        bank_g = [net.bank[1], net.bank[3], net.bank[1]]
        bank_u = [net.bank[2], net.bank[4], net.bank[1]]
        bank_a = net.bank[5:7]
        bank_o = net.bank[7]
        UNITS = ((0, 4), (4, 8), (8, 10))

        def steps(engine, slot):
            for u in range(2):
                slot(u, u)
            with engine.Fori(1, nb // 2 - 1) as t:
                for u in range(2):
                    slot(2 * t + u, u)
            for u in range(2):
                slot(nb - 2 + u, u)

        with nc.Block() as block:
            @block.sync
            def _(sp):
                sp.dma_start(router[:, :, :], ins["L0_ffn_router"].rearrange("(c p) e -> p c e", p=P)).then_inc(loaded, 16)
                for c in range(C):
                    s = slice(c * P, (c + 1) * P)
                    sp.dma_start(gate[:, c, :, :], ins["L0_ffn_experts_gate"][:, s, :].rearrange("e p d -> p e d")).then_inc(loaded, 16)
                    sp.dma_start(up[:, c, :, :], ins["L0_ffn_experts_up"][:, s, :].rearrange("e p d -> p e d")).then_inc(loaded, 16)
                    sp.dma_start(shared[:, c, 0, :], ins["L0_ffn_shared_gate"][s, :]).then_inc(loaded, 16)
                    sp.dma_start(shared[:, c, 1, :], ins["L0_ffn_shared_up"][s, :]).then_inc(loaded, 16)
                    sp.dma_start(down[:, NE + c, :], ins["L0_ffn_shared_down"][s, :]).then_inc(loaded, 16)
                sp.dma_start(down[:, 0:NE, :], ins["L0_ffn_experts_down"].rearrange("e p d -> p e d")).then_inc(loaded, 16)
                sp.wait_ge(loaded, 192)

            @block.tensor
            def _(pe):
                def turn(k, u):
                    pe.wait_ge(normed_ready, k + 1)
                    ge(pe, exp_ready, k)
                    for c in range(C):
                        i = nc.tensor.transpose(bank_x[:, c * P:(c + 1) * P], normed[:, u, c * P:(c + 1) * P], net.id_f[:, :])
                    i.then_inc(xT_done, 1)

                def route_logits(k, u):
                    pe.wait_ge(xT_copied, k + 1)
                    for c in range(C):
                        i = nc.tensor.matmul(logits, xT[:, u, c, :], router[:, c, :], start=(c == 0), stop=(c == C - 1))
                    i.then_inc(logits_done, 1)

                def slot(k, u):
                    for n, (lo, hi) in enumerate(UNITS):
                        if n == 2:
                            pe.wait_ge(acts_ready, 3 * k + 1)
                            if not (isinstance(k, int) and k == nb - 1):
                                turn(k + 1, 1 - u)
                        elif n == 0:
                            ge(pe, acts_ready, 3 * k)
                        else:
                            ge(pe, acts_ready, 3 * k - 1)
                        for w, bank in (((gate, bank_g[n]), (up, bank_u[n])) if n < 2 else ((shared, bank_g[n]),)):
                            for c in range(C):
                                rhs = w[:, c, lo:hi, :] if n < 2 else w[:, c, :, :]
                                i = nc.tensor.matmul(bank[:, :], xT[:, u, c, :], rhs.rearrange("p e d -> p (e d)"),
                                                     start=(c == 0), stop=(c == C - 1))
                        i.then_inc(unit_done, 1)
                    if not (isinstance(k, int) and k == nb - 1):
                        route_logits(k + 1, 1 - u)

                    def turn_acts(n):
                        lo, hi = UNITS[n]
                        pe.wait_ge(acts_ready, 3 * k + n + 1)
                        ge(pe, actsT_copied, 3 * k + n - 1)
                        for e in range(lo, hi):
                            i = nc.tensor.transpose(bank_a[n % 2][:, (e - lo) * P:(e - lo + 1) * P], acts[:, e, :], net.id_f[:, :])
                        i.then_inc(actsT_done, 1)

                    def sum_down(n):
                        lo, hi = UNITS[n]
                        pe.wait_ge(actsT_copied, 3 * k + n + 1)
                        for e in range(lo, hi):
                            i = nc.tensor.matmul(bank_o[:, 0:D], actsT[:, e, :], down[:, e, :], start=(e == 0), stop=(e == NC - 1))
                        return i

                    turn_acts(0)
                    turn_acts(1)
                    ge(pe, x_added, k)
                    sum_down(0)
                    turn_acts(2)
                    sum_down(1)
                    sum_down(2).then_inc(out_done, 1)

                pe.wait_ge(loaded, 192)
                turn(0, 0)
                route_logits(0, 0)
                steps(pe, slot)

            @block.scalar
            def _(act):
                def copy_x(k, u):
                    act.wait_ge(xT_done, k + 1)
                    ge(act, unit_done, 3 * k - 3)
                    nc.scalar.activation(xT[:, u, :, :].rearrange("p c t -> p (c t)"), bank_x[:, 0:D], ACT.Copy).then_inc(xT_copied, 1)

                def route_exp(k):
                    act.wait_ge(route, 9 * k + 2)
                    nc.scalar.activation(expd[:, :], logits, ACT.Exp, bias=neg_top[:, :], accum_out=exp_sum[:, :]).then_inc(exp_ready, 1)

                def slot(k, u):
                    last = isinstance(k, int) and k == nb - 1
                    for n in range(3):
                        act.wait_ge(unit_done, 3 * k + n + 1)
                        ge(act, gated_ready, 3 * k + n - 2)
                        w = 512 if n < 2 else D
                        nc.scalar.activation(tanh[:, n, 0:w], bank_g[n][:, 0:w], ACT.Tanh, scale=0.5).then_inc(tanh_ready, 1)
                        if n == 1 and not last:
                            copy_x(k + 1, 1 - u)
                    if not last:
                        route_exp(k + 1)
                    for n, (lo, hi) in enumerate(UNITS):
                        act.wait_ge(actsT_done, 3 * k + n + 1)
                        ge(act, out_done, k)
                        nc.scalar.activation(actsT[:, lo:hi, :].rearrange("p e t -> p (e t)"), bank_a[n % 2][:, 0:(hi - lo) * P],
                                             ACT.Copy).then_inc(actsT_copied, 1)

                copy_x(0, 0)
                route_exp(0)
                steps(act, slot)

            @block.gpsimd
            def _(pool):
                pool.wait_ge(stats_ready, nb)
                nc.gpsimd.tensor_tensor(net.rstd[:, :, 0], net.var_eps[:, :, 0], net.minus_half[:, :, 0], ALU.pow).then_inc(final, 1)
                pool.wait_ge(final, 1)

            @block.vector
            def _(v):
                def norm(k, u):
                    ge(v, xT_done, k - 1)
                    nc.vector.tensor_scalar(normed[:, u, :], at(net.x, k), at(net.mean, k), at(net.rstd, k),
                                            ALU.subtract, ALU.mult).then_inc(normed_ready, 1)

                def route_begin(k):
                    v.wait_ge(logits_done, k + 1)
                    nc.vector.tensor_copy(left[:, 8:16], logits).then_inc(route, 1)
                    v.wait_ge(route, 9 * k + 1)
                    nc.vector.tensor_reduce(neg_top[:, :], left[:, 8:16], X, ALU.max, negate=True).then_inc(route, 1)

                def route_end(k, u):
                    v.wait_ge(exp_ready, k + 1)
                    nc.vector.reciprocal(recip[:, :], exp_sum[:, :]).then_inc(route, 1)
                    v.wait_ge(route, 9 * k + 3)
                    nc.vector.tensor_scalar(prob[:, 0:NE], expd[:, :], recip[:, :], None, ALU.mult).then_inc(route, 1)
                    apart(v, route, 9 * k + 4)
                    nc.vector.max(top[:, :], prob[:, 0:NE]).then_inc(route, 1)
                    v.wait_ge(route, 9 * k + 5)
                    nc.vector.tensor_copy(best[:, 0:2], top[:, 0:2]).then_inc(route, 1)
                    apart(v, route, 9 * k + 6)
                    nc.vector.match_replace(left[:, :], best[:, :], prob[:, :], 0.0).then_inc(route, 1)
                    v.wait_ge(route, 9 * k + 7)
                    nc.vector.tensor_tensor(left[:, 0:NE], prob[:, 0:NE], left[:, 0:NE], ALU.subtract).then_inc(route, 1)
                    v.wait_ge(route, 9 * k + 8)
                    nc.vector.tensor_scalar(coef[:, u, :], left[:, 0:NE], 0.5, None, ALU.mult).then_inc(route, 1)

                def slot(k, u):
                    last = isinstance(k, int) and k == nb - 1
                    if not last:
                        norm(k + 1, 1 - u)
                    v.wait_ge(route, 9 * k + 9)
                    for n, (lo, hi) in enumerate(UNITS):
                        w = 512 if n < 2 else D
                        v.wait_ge(tanh_ready, 3 * k + n + 1)
                        nc.vector.scalar_tensor_tensor(out=gated[:, n, 0:w], in0=tanh[:, n, 0:w], scalar=1.0, in1=bank_g[n][:, 0:w],
                                                       op0=ALU.add, op1=ALU.mult).then_inc(gated_ready, 1)
                        v.wait_ge(gated_ready, 3 * k + n + 1)
                        ge(v, actsT_done, 3 * k)
                        if n < 2:
                            for e in range(lo, hi):
                                i = nc.vector.scalar_tensor_tensor(
                                    out=acts[:, e, :], in0=gated[:, n, (e - lo) * DE:(e - lo + 1) * DE], scalar=coef[:, u, e:e + 1],
                                    in1=bank_u[n][:, (e - lo) * DE:(e - lo + 1) * DE], op0=ALU.mult, op1=ALU.mult)
                        else:
                            i = nc.vector.scalar_tensor_tensor(
                                out=acts[:, NE:NC, :].rearrange("p e d -> p (e d)"), in0=gated[:, n, 0:D], scalar=0.5,
                                in1=bank_u[n][:, D:2 * D], op0=ALU.mult, op1=ALU.mult)
                        i.then_inc(acts_ready, 1)
                    if not last:
                        route_begin(k + 1)
                        route_end(k + 1, 1 - u)
                    v.wait_ge(out_done, k + 1)
                    nc.vector.tensor_tensor(at(net.x, k), bank_o[:, 0:D], at(net.x, k), ALU.add).then_inc(x_added, 1)
                    apart(v, x_added, k + 1)
                    nc.vector.bn_stats(stats[:, :], at(net.x, k)).then_inc(ln, 1)
                    apart(v, ln, 2 * k + 1)
                    nc.vector.bn_aggr(agg[:, :], stats[:, :]).then_inc(ln, 1)
                    v.wait_ge(ln, 2 * k + 2)
                    nc.vector.tensor_scalar(at(net.var_eps, k), agg[:, 1:2], LN_EPS, None, ALU.add)
                    nc.vector.tensor_copy(at(net.mean, k), agg[:, 0:1]).then_inc(stats_ready, 1)

                nc.vector.memset(prob[:, :], -5.0).then_inc(filled, 1)
                nc.vector.memset(best[:, :], -5.0).then_inc(filled, 1)
                v.wait_ge(filled, 2)
                norm(0, 0)
                route_begin(0)
                route_end(0, 0)
                steps(v, slot)
                v.wait_ge(stats_ready, nb)
        sem.release()


def bitnet(nc, net, out):
    nb = net.nb
    with ExitStack() as ctx:
        def sb(name, shape, dt=F32):
            return ctx.enter_context(nc.sbuf_tensor(f"f_{name}", shape, dt))

        sem = Semaphores(nc, "f")

        conv_w = sb("conv_w", [P, HC, 3])
        out_scale = sb("out_scale", [P, 1])
        normed = sb("normed", [P, D])
        big1 = sb("big1", [P, 2, 1])
        scale1 = sb("scale1", [P, 1])
        inv1 = sb("inv1", [P, 1])
        round1 = sb("round1", [P, D])
        q1 = sb("q1", [P, D], BF16)
        diag = sb("diag", [P, P])
        q1T = sb("q1T", [P, C, P], BF16)
        inv_row = sb("inv_row", [P, P])
        hid = sb("hid", [P, 2, HC, P + 2])
        conv = sb("conv", [P, 2, HC, P])
        tanh = sb("tanh", [P, HID])
        silu2 = sb("silu2", [P, HID])
        big2 = sb("big2", [P, 1])
        scale2 = sb("scale2", [P, 1])
        inv2 = sb("inv2", [P, 1])
        round2 = sb("round2", [P, HID])
        q2 = sb("q2", [P, HID], BF16)
        q2T = sb("q2T", [P, HC, P], BF16)
        result = sb("result", [P, 2, D])

        init = sem("init")
        quant1 = sem("quant1")
        q1_ready = sem("q1_ready")
        diag_ready = sem("diag_ready")
        q1T_done = sem("q1T_done")
        q1T_copied = sem("q1T_copied")
        row_copied = sem("row_copied")
        hid_done = sem("hid_done")
        hid_ready = sem("hid_ready")
        centre = sem("centre")
        left = sem("left")
        conv_ready = sem("conv_ready")
        back_done = sem("back_done")
        tanh_ready = sem("tanh_ready")
        silu_ready = sem("silu_ready")
        quant2 = sem("quant2")
        rounded = sem("rounded")
        q2_ready = sem("q2_ready")
        q2T_done = sem("q2T_done")
        q2T_copied = sem("q2T_copied")
        out_done = sem("out_done")
        result_ready = sem("result_ready")
        stored = [sem(f"stored{i}") for i in range(2)]

        bank_q = net.bank[0]
        q1T_ps = bank_q[:, 0:P].bitcast(BF16)
        row_ps = bank_q[:, D:D + P]
        bank_h = net.bank[1:3]
        bank_b = net.bank[3:5]
        bank_q2 = net.bank[5]
        bank_o = net.bank[6]

        def steps(engine, slot):
            for k in range(4):
                slot(k, k % 2, k // 2)
            with engine.Fori(2, nb // 2) as t:
                for u in range(2):
                    slot(2 * t + u, u, t)
            slot(nb, 0, nb // 2)

        def active(k):
            return not isinstance(k, int) or k < nb, not isinstance(k, int) or k >= 1

        with nc.Block() as block:
            @block.sync
            def _(sp):
                def slot(k, u, t):
                    _, second = active(k)
                    if second:
                        n, b = k - 1, (u - 1) % 2
                        sp.wait_ge(result_ready, n + 1)
                        sp.dma_start(out[bass.ds(n, 1)].rearrange("n p d -> p (n d)"), result[:, b, :]).then_inc(stored[b], 16)

                steps(sp, slot)
                for b in range(2):
                    sp.wait_ge(stored[b], 16 * (nb // 2))

            @block.gpsimd
            def _(pool):
                def slot(k, u, t):
                    first, _ = active(k)
                    if first:
                        pool.wait_ge(quant1, 5 * k + 4)
                        apart(pool, q1T_done, k)
                        nc.gpsimd.tensor_scalar(diag[:, :], net.id_f[:, :], inv1[:, :], None, ALU.mult).then_inc(diag_ready, 1)

                steps(pool, slot)

            @block.tensor
            def _(pe):
                def slot(k, u, t):
                    first, second = active(k)
                    n = k - 1
                    if first:
                        pe.wait_ge(q1_ready, k + 1)
                        ge(pe, row_copied, k)
                        for c in range(C):
                            nc.tensor.transpose(q1T_ps[:, c * P:(c + 1) * P], q1[:, c * P:(c + 1) * P], net.id_b[:, :])
                        pe.wait_ge(diag_ready, k + 1)
                        nc.tensor.matmul(row_ps, net.ones_f[:, :], diag[:, :], start=True, stop=True).then_inc(q1T_done, 1)
                    if second:
                        for n2 in range(2):
                            pe.wait_ge(conv_ready, 2 * n + n2 + 1)
                            ge(pe, silu_ready, 2 * n + n2 - 1)
                            for c in range(4):
                                i = nc.tensor.transpose(bank_b[n2][:, c * P:(c + 1) * P], conv[:, (u - 1) % 2, 4 * n2 + c, :], net.id_f[:, :])
                            i.then_inc(back_done, 1)
                    if first:
                        pe.wait_ge(q1T_copied, k + 1)
                        for n2 in range(2):
                            ge(pe, hid_ready, 2 * k + n2 - 1)
                            for c in range(4):
                                for kc in range(C):
                                    s = (4 * n2 + c) * P
                                    i = nc.tensor.matmul(bank_h[n2][:, c * P:(c + 1) * P], net.w1T[:, kc, s:s + P], q1T[:, kc, :],
                                                         start=(kc == 0), stop=(kc == C - 1))
                            i.then_inc(hid_done, 1)
                    if second:
                        pe.wait_ge(q2_ready, n + 1)
                        ge(pe, q2T_copied, n)
                        for c in range(HC):
                            i = nc.tensor.transpose(bank_q2[:, :].bitcast(BF16)[:, c * P:(c + 1) * P], q2[:, c * P:(c + 1) * P], net.id_b[:, :])
                        i.then_inc(q2T_done, 1)
                        pe.wait_ge(q2T_copied, n + 1)
                        ge(pe, result_ready, n)
                        for c in range(HC):
                            i = nc.tensor.matmul(bank_o[:, 0:D], q2T[:, c, :], net.w2T[:, c, :], start=(c == 0), stop=(c == HC - 1))
                        i.then_inc(out_done, 1)

                pe.wait_ge(init, 3)
                steps(pe, slot)

            @block.scalar
            def _(act):
                def slot(k, u, t):
                    first, second = active(k)
                    n = k - 1
                    if first:
                        act.wait_ge(q1T_done, k + 1)
                        ge(act, hid_done, 2 * k)
                        nc.scalar.activation(q1T[:, :, :].rearrange("p c t -> p (c t)"), q1T_ps, ACT.Copy).then_inc(q1T_copied, 1)
                        ge(act, hid_ready, 2 * k)
                        nc.scalar.activation(inv_row[:, :], row_ps, ACT.Copy).then_inc(row_copied, 1)
                    if second:
                        for n2 in range(2):
                            act.wait_ge(back_done, 2 * n + n2 + 1)
                            ge(act, silu_ready, 2 * n + n2 - 1)
                            nc.scalar.activation(tanh[:, n2 * 512:(n2 + 1) * 512], bank_b[n2][:, :], ACT.Tanh, scale=0.5).then_inc(tanh_ready, 1)
                    if first:
                        for c in range(HC):
                            if c % 4 == 0:
                                act.wait_ge(hid_ready, 2 * k + c // 4 + 1)
                                ge(act, back_done, 2 * (k - 1) + c // 4 - 1)
                            nc.scalar.activation(conv[:, u, c, :], hid[:, u, c, 1:P + 1], ACT.Identity, bias=net.conv_b[:, c:c + 1],
                                                 scale=conv_w[:, c, 1:2]).then_inc(centre, 1)
                    if second:
                        act.wait_ge(quant2, 4 * n + 4)
                        ge(act, q2_ready, n)
                        nc.scalar.activation(round2[:, :], silu2[:, :], ACT.Copy, bias=ROUND, scale=scale2[:, :]).then_inc(rounded, 1)
                        act.wait_ge(q2T_done, n + 1)
                        ge(act, out_done, n)
                        nc.scalar.activation(q2T[:, :, :].rearrange("p c t -> p (c t)"), bank_q2[:, :].bitcast(BF16), ACT.Copy).then_inc(q2T_copied, 1)

                act.wait_ge(init, 3)
                steps(act, slot)

            @block.vector
            def _(v):
                def quantise(k):
                    nc.vector.tensor_scalar(normed[:, :], at(net.x, k), at(net.mean, k), at(net.rstd, k),
                                            ALU.subtract, ALU.mult).then_inc(quant1, 1)
                    v.wait_ge(quant1, 5 * k + 1)
                    nc.vector.tensor_reduce(big1[:, 0, :], normed[:, :], X, ALU.max, apply_absolute_value=True).then_inc(quant1, 1)
                    v.wait_ge(quant1, 5 * k + 2)
                    ge(v, diag_ready, k)
                    nc.vector.tensor_scalar(inv1[:, :], big1[:, 0, :], 1e-5, 1.0 / 127.0, ALU.max, ALU.mult).then_inc(quant1, 1)
                    v.wait_ge(quant1, 5 * k + 3)
                    nc.vector.reciprocal(scale1[:, :], inv1[:, :]).then_inc(quant1, 1)
                    v.wait_ge(quant1, 5 * k + 4)
                    nc.vector.tensor_scalar(round1[:, :], normed[:, :], scale1[:, :], ROUND, ALU.mult, ALU.add).then_inc(quant1, 1)
                    v.wait_ge(quant1, 5 * k + 5)
                    ge(v, q1T_done, k)
                    nc.vector.tensor_scalar(q1[:, :], round1[:, :], -ROUND, 127.0, ALU.add, ALU.min).then_inc(q1_ready, 1)

                def slot(k, u, t):
                    first, second = active(k)
                    n = k - 1
                    if second:
                        for n2 in range(2):
                            s = slice(n2 * 512, (n2 + 1) * 512)
                            v.wait_ge(tanh_ready, 2 * n + n2 + 1)
                            ge(v, rounded, n)
                            nc.vector.scalar_tensor_tensor(out=silu2[:, s], in0=tanh[:, s], scalar=1.0, in1=bank_b[n2][:, :],
                                                           op0=ALU.add, op1=ALU.mult).then_inc(silu_ready, 1)
                        v.wait_ge(silu_ready, 2 * n + 2)
                        nc.vector.tensor_reduce(big2[:, :], silu2[:, :], X, ALU.max, apply_absolute_value=True).then_inc(quant2, 1)
                        v.wait_ge(quant2, 4 * n + 1)
                        nc.vector.tensor_scalar(big2[:, :], big2[:, :], 2e-5, 1.0 / 127.0, ALU.max, ALU.mult).then_inc(quant2, 1)
                        v.wait_ge(quant2, 4 * n + 2)
                        nc.vector.reciprocal(scale2[:, :], big2[:, :]).then_inc(quant2, 1)
                        nc.vector.tensor_scalar(inv2[:, :], big2[:, :], out_scale[:, :], None, ALU.mult).then_inc(quant2, 1)
                    if first:
                        for n2 in range(2):
                            v.wait_ge(hid_done, 2 * k + n2 + 1)
                            v.wait_ge(row_copied, k + 1)
                            ge(v, centre, 8 * (k - 1))
                            nc.vector.tensor_tensor(hid[:, u, 4 * n2:4 * n2 + 4, 1:P + 1], bank_h[n2][:, :].rearrange("p (c t) -> p c t", c=4),
                                                    inv_row[:, :].unsqueeze(1).to_broadcast([P, 4, P]), ALU.mult).then_inc(hid_ready, 1)
                        v.wait_ge(hid_ready, 2 * k + 2)
                    if second:
                        v.wait_ge(rounded, n + 1)
                        ge(v, q2T_done, n)
                        nc.vector.tensor_scalar(q2[:, :], round2[:, :], -ROUND, 127.0, ALU.add, ALU.min).then_inc(q2_ready, 1)
                    if first:
                        for c in range(HC):
                            v.wait_ge(centre, 8 * k + c + 1)
                            nc.vector.scalar_tensor_tensor(out=conv[:, u, c, :], in0=hid[:, u, c, 0:P], scalar=conv_w[:, c, 0:1],
                                                           in1=conv[:, u, c, :], op0=ALU.mult, op1=ALU.add).then_inc(left, 1)
                        for c in range(HC):
                            v.wait_ge(left, 8 * k + c + 1)
                            i = nc.vector.scalar_tensor_tensor(out=conv[:, u, c, :], in0=hid[:, u, c, 2:P + 2], scalar=conv_w[:, c, 2:3],
                                                               in1=conv[:, u, c, :], op0=ALU.mult, op1=ALU.add)
                            if c % 4 == 3:
                                i.then_inc(conv_ready, 1)
                    if first and not (isinstance(k, int) and k == nb - 1) and not isinstance(k, int):
                        pass
                    if second:
                        v.wait_ge(out_done, n + 1)
                        b = (u - 1) % 2
                        ge(v, stored[b], 16 * (t if b == 0 else t - 1))
                        nc.vector.scalar_tensor_tensor(out=result[:, b, :], in0=bank_o[:, 0:D], scalar=inv2[:, :], in1=at(net.x, n),
                                                       op0=ALU.mult, op1=ALU.add).then_inc(result_ready, 1)

                nc.vector.tensor_tensor(conv_w[:, :, :], net.conv_w[:, :, :],
                                        net.w_dequant[:, 0:1].unsqueeze(1).to_broadcast([P, HC, 3]), ALU.mult).then_inc(init, 1)
                nc.vector.tensor_scalar(out_scale[:, :], net.w_dequant[:, 1:2], 0.5, None, ALU.mult).then_inc(init, 1)
                nc.vector.memset(hid[:, :, :, :], 0.0).then_inc(init, 1)
                v.wait_ge(init, 3)

                def whole(k, u, t):
                    if active(k)[0]:
                        quantise(k)
                    slot(k, u, t)

                steps(v, whole)


def build(nc, ins, out):
    net = Net()
    net.nb = ins["x"].shape[0]
    pairs = net.nb // 2
    net.q_scr = [nc.dram_tensor(f"q_scratch{n}", (pairs, PARTS, P, C * 2 * P), BF16, kind="Internal").ap() for n in range(2)]
    net.k_scr = [nc.dram_tensor(f"k_scratch{n}", (pairs, PARTS, P, C * 2 * P), BF16, kind="Internal").ap() for n in range(2)]
    net.v_scr = [nc.dram_tensor(f"v_scratch{n}", (pairs, P, 2 * H * VW), F32, kind="Internal").ap() for n in range(2)]
    with ExitStack() as ctx:
        lay_out(nc, ctx, net)
        prepare(nc, net, ins)
        project(nc, net, 0, True, ins)
        attend(nc, net, 0)
        experts(nc, net, ins)
        project(nc, net, 1, False, ins)
        attend(nc, net, 1)
        bitnet(nc, net, out)


def kernel(**inputs):
    import numpy as _np
    import concourse.bacc as _bacc
    from concourse import mybir as _mybir
    from concourse.bass_utils import run_bass_kernel_spmd as _run

    nc = _bacc.Bacc("TRN2", target_bir_lowering=False, num_devices=1)
    arrays, ins = {}, {}
    for name, value in inputs.items():
        a = _np.ascontiguousarray(value)
        arrays[f"in_{name}_dram"] = a
        ins[name] = nc.dram_tensor(f"in_{name}_dram", a.shape, _mybir.dt.from_np(a.dtype), kind="ExternalInput").ap()
    shape = inputs["x"].shape
    out = nc.dram_tensor("out_0_dram", shape, _mybir.dt.float32, kind="ExternalOutput").ap()
    build(nc, ins, out)
    return _run(nc, [arrays], core_ids=[0]).results[0]["out_0_dram"]
```

```python
import math
from contextlib import ExitStack

import concourse.bass as bass
from concourse import mybir
from concourse.alu_op_type import AluOpType as ALU

F32 = mybir.dt.float32
BF16 = mybir.dt.bfloat16
F16 = mybir.dt.float16
ACT = mybir.ActivationFunctionType
X = mybir.AxisListType.X

P = 128
D = 256
C = D // P
H = 16
DK = D // H
H8 = H // C
QUADS = H // 4
VW = DK + 1
PARTS = 3
ROWS = 6 * DK
NE = 8
DE = 128
HID = 1024
HC = HID // P
LN_EPS = 1e-5
ROUND = 12582912.0
MAXLEN = 512

ATT = ["L0_xattn_w_q", "L0_xattn_w_k", "L0_xattn_w_v", "L0_xattn_w_o",
       "L1_xattn_wq", "L1_xattn_wk", "L1_xattn_wv", "L1_xattn_wo"]
BIASES = ["L0_xattn_b_q", "L0_xattn_b_k", "L1_xattn_bq", "L1_xattn_bk"]
ROW_BIASES = ["L0_xattn_b_v", "L0_xattn_b_o", "L1_xattn_bv", "L1_xattn_bo"]


class Net:
    pass


class Semaphores:

    def __init__(self, nc, tag):
        self.nc, self.tag, self.all = nc, tag, []

    def __call__(self, name):
        self.all.append(self.nc.alloc_semaphore(f"{self.tag}_{name}"))
        return self.all[-1]

    def release(self):
        self.nc.clear_and_free_semaphores(self.all)
        self.nc.all_engine_barrier()


def at(ap, index):
    return ap[:, bass.ds(index, 1), :].rearrange("p o n -> p (o n)")


def lay_out(nc, ctx, net):
    def sb(name, shape, dt=F32):
        return ctx.enter_context(nc.sbuf_tensor(name, shape, dt))

    net.bank = [ctx.enter_context(nc.psum_tensor(f"bank{i}", [P, 512], F32)) for i in range(8)]
    nb = net.nb
    net.x = sb("x_all", [P, nb, D])
    net.moments = sb("moments_all", [P, nb, 2])
    net.var_eps = sb("var_eps_all", [P, nb, 1])
    net.rstd = sb("rstd_all", [P, nb, 1])
    net.minus_half = sb("minus_half", [P, nb, 1])
    net.wT = sb("wT", [P, 8, C, D])
    net.w1T = sb("w1T", [P, C, HID], BF16)
    net.w2T = sb("w2T", [P, HC, D], BF16)
    net.w_dequant = sb("w_dequant", [P, 2])
    net.conv_w = sb("conv_w", [P, HC, 3])
    net.conv_b = sb("conv_b", [P, HC])
    net.rel = sb("rel", [P, 2 * P], BF16)
    net.bias_col = sb("bias_col", [P, C, 4])
    net.bias_row = sb("bias_row", [P, 4, D])
    net.prob_bias = sb("prob_bias", [P, 1])
    net.id_f = sb("id_f", [P, P])
    net.id_b = sb("id_b", [P, P], BF16)
    net.ones_f = sb("ones_f", [P, P])
    net.pick = sb("pick", [PARTS * H, H, P], BF16)


def prepare(nc, net, ins):
    with ExitStack() as ctx:
        def sb(name, shape, dt=F32):
            return ctx.enter_context(nc.sbuf_tensor(name, shape, dt))

        sem = Semaphores(nc, "w")

        raw = sb("raw_att", [P, 8, C, D])
        w_raw = sb("w_raw", [P, 2, 2048])
        w_q = sb("w_q", [P, 2, 2048], BF16)
        w_abs = sb("w_abs", [P, 2])
        w_mean = sb("w_mean", [P, 2])
        w_scale = sb("w_scale", [P, 2])
        rel_raw = sb("rel_raw", [P, 2, DK])
        rel_r1 = sb("rel_r1", [P, 2, DK])
        rel_r2 = sb("rel_r2", [P, 2, DK])
        rel_parts = sb("rel_parts", [P, 2, 6, DK], BF16)
        bias_raw = sb("bias_raw", [4, D])
        conv_b_raw = sb("conv_b_raw", [HC, P])
        bias_apart = sb("bias_apart", [4, C, P])
        stats = sb("stats0", [P, 4, 6])
        agg = sb("agg0", [P, 4, 2])

        att_loaded = sem("att_loaded")
        w12_loaded = sem("w12_loaded")
        x_loaded = sem("x_loaded")
        small_loaded = sem("small_loaded")
        rows_loaded = sem("rows_loaded")
        zeroed = sem("zeroed")
        consts = sem("consts")
        att_done = sem("att_done")
        att_copied = sem("att_copied")
        abs_done = sem("abs_done")
        mean_done = sem("mean_done")
        dve = sem("dve")
        w12_quantised = sem("w12_quantised")
        w12_done = sem("w12_done")
        w12_copied = sem("w12_copied")
        rel_ready = sem("rel_ready")
        rel_done = sem("rel_done")
        bias_ordered = sem("bias_ordered")
        bias_done = sem("bias_done")
        small_copied = sem("small_copied")
        ln_stats = sem("ln_stats")
        ln_aggregated = sem("ln_aggregated")
        ln = sem("ln")
        var_ready = sem("var_ready")
        nb = net.nb

        with nc.Block() as block:
            @block.sync
            def _(sp):
                for m in range(8):
                    sp.dma_start(raw[:, m, :, :], ins[ATT[m]].rearrange("(c p) i -> p c i", p=P)).then_inc(att_loaded, 16)
                sp.dma_start(w_raw[:, 0, :].rearrange("p (c i) -> p c i", c=HC),
                             ins["L1_ffn_w1"].rearrange("(c p) i -> p c i", p=P)).then_inc(w12_loaded, 16)
                sp.dma_start(w_raw[:, 1, :].rearrange("p (c i) -> p c i", c=C),
                             ins["L1_ffn_w2"].rearrange("(c p) i -> p c i", p=P)).then_inc(w12_loaded, 16)
                for n in range(4):
                    s = slice(n * nb // 4, (n + 1) * nb // 4)
                    sp.dma_start(net.x[:, s, :], ins["x"][s].rearrange("b p d -> p b d")).then_inc(x_loaded, 16)
                for s in (att_loaded,):
                    sp.wait_ge(s, 128)
                sp.wait_ge(x_loaded, 64)
                sp.wait_ge(w12_loaded, 32)

            @block.scalar
            def _(act):
                act.dma_start(rel_raw[:, :, :], ins["L1_xattn_rel_emb"][MAXLEN - P + 1:MAXLEN + P + 1, :]
                              .rearrange("(c p) d -> p c d", p=P)).then_inc(small_loaded, 16)
                for n, name in enumerate(BIASES):
                    act.dma_start(bias_raw[n:n + 1, :], ins[name].rearrange("(a n) -> a n", a=1)).then_inc(small_loaded, 16)
                for n, name in enumerate(ROW_BIASES):
                    act.dma_start(net.bias_row[:, n, :], ins[name].partition_broadcast(P)).then_inc(rows_loaded, 16)
                act.dma_start(net.conv_w[:, :, :], ins["L1_ffn_conv_w"].rearrange("(c p) o k -> p c (o k)", p=P)).then_inc(rows_loaded, 16)
                act.dma_start(conv_b_raw[:, :], ins["L1_ffn_conv_b"].rearrange("(c p) -> c p", p=P)).then_inc(small_loaded, 16)
                act.wait_ge(small_loaded, 96)
                nc.scalar.activation(bias_apart[:, :, :].rearrange("n o (d h) -> n o d h", d=DK),
                                     bias_raw[:, :].rearrange("n (h o d) -> n o d h", o=C, d=DK), ACT.Copy).then_inc(bias_ordered, 1)
                for m in range(8):
                    act.wait_ge(att_done, m + 1)
                    src = net.bank[m % 4][:, :]
                    quarter = 0.25 if m in (0, 4) else 1.0
                    if m % 4 < 2:
                        for c in range(C):
                            i = nc.scalar.activation(
                                net.wT[:, m, c, :].rearrange("p (o d h) -> p o d h", o=C, d=DK),
                                src[:, c * D:(c + 1) * D].rearrange("p (h o d) -> p o d h", o=C, d=DK),
                                ACT.Copy, scale=quarter)
                    else:
                        i = nc.scalar.activation(net.wT[:, m, :, :].rearrange("p c o -> p (c o)"), src, ACT.Copy)
                    i.then_inc(att_copied, 1)
                for n in range(4):
                    act.wait_ge(w12_done, n + 1)
                    src = net.bank[4 + n][:, :].bitcast(BF16)
                    if n < 2:
                        i = nc.scalar.activation(net.w1T[:, n, :], src, ACT.Copy)
                    else:
                        i = nc.scalar.activation(net.w2T[:, :, (n - 2) * P:(n - 1) * P],
                                                 src.rearrange("p (c o) -> p c o", c=HC), ACT.Copy)
                    i.then_inc(w12_copied, 1)
                act.wait_ge(rel_done, 1)
                nc.scalar.activation(net.rel[0:ROWS, :], net.bank[1][0:ROWS, 0:P].bitcast(BF16), ACT.Copy).then_inc(small_copied, 1)
                act.wait_ge(bias_done, 1)
                for o in range(C):
                    nc.scalar.activation(net.bias_col[:, o, 0:4:2], net.bank[0][:, 4 * o:4 * o + 4:2], ACT.Copy, scale=0.25).then_inc(small_copied, 1)
                    nc.scalar.activation(net.bias_col[:, o, 1:4:2], net.bank[0][:, 4 * o + 1:4 * o + 4:2], ACT.Copy).then_inc(small_copied, 1)
                nc.scalar.activation(net.conv_b[:, :], net.bank[0][:, 8:8 + HC], ACT.Copy).then_inc(small_copied, 1)
                act.wait_ge(small_copied, 6)
                act.wait_ge(att_copied, 8)
                act.wait_ge(w12_copied, 4)
                act.wait_ge(rows_loaded, 80)
                act.wait_ge(small_loaded, 96)

            @block.gpsimd
            def _(pool):
                nc.gpsimd.memset(net.id_f[:, :], 0.0).then_inc(zeroed, 1)
                nc.gpsimd.memset(net.id_b[:, :], 0.0).then_inc(zeroed, 1)
                nc.gpsimd.memset(net.pick[:, :, :], 0.0).then_inc(zeroed, 1)
                nc.gpsimd.memset(net.ones_f[:, :], 1.0).then_inc(consts, 1)
                nc.gpsimd.memset(net.minus_half[:, :, :], -0.5).then_inc(consts, 1)
                nc.gpsimd.memset(net.prob_bias[:, :], math.log(2.0 ** 13)).then_inc(consts, 1)
                pool.wait_ge(zeroed, 3)
                for m in (net.id_f, net.id_b):
                    nc.gpsimd.affine_select(out=m[:, :], in_=m[:, :], compare_op=ALU.not_equal, fill=1.0, base=0,
                                            pattern=[[-1, P]], channel_multiplier=1).then_inc(consts, 1)
                for part in range(PARTS):
                    pool.wait_ge(zeroed, 3 + part)
                    nc.gpsimd.affine_select(out=net.pick[:, :, :], in_=net.pick[:, :, :], compare_op=ALU.not_equal,
                                            fill=1.0, base=-part * H, pattern=[[-1, H], [0, P]],
                                            channel_multiplier=1).then_inc(zeroed, 1)
                pool.wait_ge(zeroed, 6)
                pool.wait_ge(var_ready, 1)
                pool.wait_ge(consts, 5)
                nc.gpsimd.tensor_tensor(net.rstd[:, :, 0], net.var_eps[:, :, 0], net.minus_half[:, :, 0], ALU.pow).then_inc(consts, 1)
                pool.wait_ge(consts, 6)

            @block.vector
            def _(v):
                step = 0
                v.wait_ge(w12_loaded, 32)
                nc.vector.tensor_reduce(w_abs[:, :], w_raw[:, :, :], X, ALU.add, apply_absolute_value=True).then_inc(abs_done, 1)
                v.wait_ge(mean_done, 1)
                nc.vector.tensor_scalar(w_mean[:, :], net.bank[7][:, 0:2], 1.0 / (HID * D), 1e-5, ALU.mult, ALU.max).then_inc(dve, 1)
                v.wait_ge(dve, 1)
                nc.vector.reciprocal(w_scale[:, :], w_mean[:, :]).then_inc(dve, 1)
                v.wait_ge(dve, 2)
                nc.vector.reciprocal(net.w_dequant[:, :], w_scale[:, :]).then_inc(dve, 1)
                for n in range(2):
                    nc.vector.tensor_scalar(w_raw[:, n, :], w_raw[:, n, :], w_scale[:, n:n + 1], 1.0, ALU.mult, ALU.min).then_inc(dve, 1)
                    v.wait_ge(dve, 4 + 2 * n)
                    nc.vector.tensor_scalar(w_raw[:, n, :], w_raw[:, n, :], -1.0, ROUND, ALU.max, ALU.add).then_inc(dve, 1)
                    v.wait_ge(dve, 5 + 2 * n)
                    nc.vector.tensor_scalar(w_q[:, n, :], w_raw[:, n, :], -ROUND, None, ALU.add).then_inc(w12_quantised, 1)
                v.wait_ge(dve, 7)
                v.wait_ge(small_loaded, 96)
                ra, rb, rc = (rel_parts[:, :, n, :] for n in (2, 1, 0))
                nc.vector.tensor_copy(ra, rel_raw[:, :, :]).then_inc(dve, 1)
                v.wait_ge(dve, 8)
                nc.vector.tensor_tensor(rel_r1[:, :, :], rel_raw[:, :, :], ra, ALU.subtract).then_inc(dve, 1)
                v.wait_ge(dve, 9)
                nc.vector.tensor_copy(rb, rel_r1[:, :, :]).then_inc(dve, 1)
                v.wait_ge(dve, 10)
                nc.vector.tensor_tensor(rel_r2[:, :, :], rel_r1[:, :, :], rb, ALU.subtract).then_inc(dve, 1)
                v.wait_ge(dve, 11)
                nc.vector.tensor_copy(rc, rel_r2[:, :, :]).then_inc(rel_ready, 1)
                nc.vector.tensor_copy(rel_parts[:, :, 3, :], rb).then_inc(rel_ready, 1)
                nc.vector.tensor_copy(rel_parts[:, :, 4, :], ra).then_inc(rel_ready, 1)
                nc.vector.tensor_copy(rel_parts[:, :, 5, :], ra).then_inc(rel_ready, 1)
                v.wait_ge(x_loaded, 64)
                with v.Fori(0, nb // 4) as t:
                    for i in range(4):
                        nc.vector.bn_stats(stats[:, i, :], at(net.x, 4 * t + i)).then_inc(ln_stats, 1)
                    for i in range(4):
                        apart(v, ln_stats, 4 * t + i + 1)
                        nc.vector.bn_aggr(agg[:, i, :], stats[:, i, :]).then_inc(ln_aggregated, 1)
                    v.wait_ge(ln_aggregated, 4 * t + 4)
                    nc.vector.tensor_copy(net.moments[:, bass.ds(4 * t, 4), :], agg[:, :, :]).then_inc(ln, 1)
                v.wait_ge(ln, nb // 4)
                nc.vector.tensor_scalar(net.var_eps[:, :, 0], net.moments[:, :, 1], LN_EPS, None, ALU.add).then_inc(var_ready, 1)
                v.wait_ge(var_ready, 1)

            @block.tensor
            def _(pe):
                pe.wait_ge(consts, 5)
                pe.wait_ge(att_loaded, 128)
                for m in range(8):
                    if m >= 4:
                        pe.wait_ge(att_copied, m - 3)
                    for c in range(C):
                        for o in range(C):
                            i = nc.tensor.transpose(net.bank[m % 4][:, (c * C + o) * P:(c * C + o + 1) * P],
                                                    raw[:, m, o, c * P:(c + 1) * P], net.id_f[:, :])
                    i.then_inc(att_done, 1)
                pe.wait_ge(abs_done, 1)
                nc.tensor.matmul(net.bank[7][:, 0:2], net.ones_f[:, :], w_abs[:, :], start=True, stop=True).then_inc(mean_done, 1)
                pe.wait_ge(w12_quantised, 2)
                pe.wait_ge(dve, 1)
                for n in range(4):
                    dst = net.bank[4 + n][:, :].bitcast(BF16)
                    for c in range(HC):
                        if n < 2:
                            src = w_q[:, 0, c * D + n * P:c * D + (n + 1) * P]
                        else:
                            src = w_q[:, 1, (n - 2) * HID + c * P:(n - 2) * HID + (c + 1) * P]
                        i = nc.tensor.transpose(dst[:, c * P:(c + 1) * P], src, net.id_b[:, :])
                    i.then_inc(w12_done, 1)
                pe.wait_ge(att_copied, 8)
                pe.wait_ge(rel_ready, 4)
                for c in range(2):
                    i = nc.tensor.transpose(net.bank[1][0:ROWS, 0:P].bitcast(BF16)[:, c * P:(c + 1) * P],
                                            rel_parts[:, c, :, :].rearrange("p n d -> p (n d)"), net.id_b[:, :])
                i.then_inc(rel_done, 1)
                pe.wait_ge(small_loaded, 96)
                pe.wait_ge(bias_ordered, 1)
                for o in range(C):
                    i = nc.tensor.transpose(net.bank[0][:, 4 * o:4 * o + 4], bias_apart[:, o, :], net.id_f[0:4, 0:4])
                i = nc.tensor.transpose(net.bank[0][:, 8:8 + HC], conv_b_raw[:, :], net.id_f[0:HC, 0:HC])
                i.then_inc(bias_done, 1)
        sem.release()


def project(nc, net, layer, with_context, ins):
    tag = f"p{layer}"
    pairs = net.nb // 2
    jobs = [(4 * layer, 2 * layer, net.q_scr[layer], (0, 1, 2))]
    if with_context:
        jobs += [(1, 1, net.k_scr[0], (2, 1, 0)), (5, 3, net.k_scr[1], (2, 1, 0))]
    nj = len(jobs)
    values = [(2, 0, net.v_scr[0]), (6, 2, net.v_scr[1])] if with_context else []
    with ExitStack() as ctx:
        def sb(name, shape, dt=F32):
            return ctx.enter_context(nc.sbuf_tensor(f"{tag}_{name}", shape, dt))

        sem = Semaphores(nc, tag)

        normed = sb("normed", [P, 2, 2, D])
        ctx_in = sb("ctx_in", [P, 2, 2, D])
        xT = sb("xT", [P, 2, C, 2 * P])
        cT = sb("cT", [P, 2, C, 2 * P])
        parts = [sb(f"parts{j}", [P, 2, PARTS, C * 2 * P], BF16) for j in range(nj)]
        rest = [sb(f"rest{j}", [P, 2, C * 2 * P]) for j in range(nj)]
        val = [sb(f"val{j}", [P, 2, 2 * H, DK]) for j in range(len(values))]
        val_parts = [sb(f"val_parts{j}", [P, 2, 2 * H, PARTS, VW], BF16) for j in range(len(values))]

        ctx_loaded = [sem(f"ctx_loaded{i}") for i in range(2)]
        normed_ready = sem("normed_ready")
        xT_done = sem("xT_done")
        cT_done = sem("cT_done")
        xT_copied = sem("xT_copied")
        cT_copied = sem("cT_copied")
        proj_done = [sem(f"proj_done{j}") for j in range(nj)]
        val_done = [sem(f"val_done{j}") for j in range(len(values))]
        part_a = [sem(f"part_a{j}") for j in range(nj)]
        rest1 = [sem(f"rest1_{j}") for j in range(nj)]
        part_b = [sem(f"part_b{j}") for j in range(nj)]
        part_c = [sem(f"part_c{j}") for j in range(nj)]
        val_read = [sem(f"val_read{j}") for j in range(len(values))]
        val_rest = [sem(f"val_rest{j}") for j in range(len(values))]
        val_b = [sem(f"val_b{j}") for j in range(len(values))]
        val_c = [sem(f"val_c{j}") for j in range(len(values))]
        val_stored = [sem(f"val_stored{i}") for i in range(2)]
        ones = sem("ones")
        stored = [sem(f"stored{i}") for i in range(2)]
        per_store = 16 * nj
        bank_x, bank_c = net.bank[0], net.bank[1]
        bank_j = net.bank[2:2 + nj]
        bank_v = net.bank[5:7]

        with nc.Block() as block:
            @block.sync
            def _(sp):
                def load(p, u):
                    sp.dma_start(ctx_in[:, u, :, :], ins["ctx_1024"].rearrange("(n b) p d -> n p b d", b=2)[bass.ds(p, 1)]
                                 .rearrange("n p b d -> p (n b) d")).then_inc(ctx_loaded[u], 16)

                def store(p, u):
                    for j, (_, _, scr, _) in enumerate(jobs):
                        sp.wait_ge(part_c[j], p + 1)
                        sp.wait_ge(part_b[j], p + 1)
                        sp.dma_start(scr.rearrange("n k p t -> n p k t")[bass.ds(p, 1)].rearrange("n p k t -> p (n k) t"),
                                     parts[j][:, u, :, :]).then_inc(stored[u], 16)

                def store_values(p, u):
                    for j, (_, _, scr) in enumerate(values):
                        sp.wait_ge(val_c[j], p + 1)
                        sp.dma_start(scr[bass.ds(p, 1)].rearrange("n p t -> p (n t)"),
                                     val_parts[j][:, u, :, :, :].rearrange("p h n w -> p (h n w)")).then_inc(val_stored[u], 16)

                if with_context:
                    load(0, 0)
                    load(1, 1)

                def work(p, u):
                    if not (isinstance(p, int) and p == 0):
                        store_values(p - 1, 1 - u)
                    store(p, u)
                    if with_context and not (isinstance(p, int) and p >= pairs - 2):
                        sp.wait_ge(cT_done, p + 1)
                        load(p + 2, u)

                for u in range(2):
                    work(u, u)
                with sp.Fori(1, pairs // 2 - 1) as t:
                    for u in range(2):
                        work(2 * t + u, u)
                for u in range(2):
                    work(pairs - 2 + u, u)
                store_values(pairs - 1, 1)
                for u in range(2):
                    sp.wait_ge(stored[u], per_store * (pairs // 2))
                    if values:
                        sp.wait_ge(val_stored[u], 16 * len(values) * (pairs // 2))

            @block.vector
            def _(v):
                def norm(p, u, first):
                    if not first:
                        v.wait_ge(xT_done, p - 1)
                    for s in range(2):
                        i = nc.vector.tensor_scalar(normed[:, u, s, :], at(net.x, 2 * p + s), at(net.moments[:, :, 0:1], 2 * p + s),
                                                    at(net.rstd, 2 * p + s), ALU.subtract, ALU.mult)
                    i.then_inc(normed_ready, 1)

                def work(p, u, first, t):
                    if not (isinstance(p, int) and p == 0):
                        value_part_c(p - 1, 1 - u)
                    for j, (_, bias, _, _) in enumerate(jobs):
                        v.wait_ge(part_a[j], p + 1)
                        if not first:
                            v.wait_ge(part_c[j], p - 1)
                        for o in range(C):
                            s = slice(o * 2 * P, (o + 1) * 2 * P)
                            i = nc.vector.scalar_tensor_tensor(
                                out=rest[j][:, u, s], in0=bank_j[j][:, s], scalar=net.bias_col[:, o, bias:bias + 1],
                                in1=parts[j][:, u, jobs[j][3].index(0), s], op0=ALU.add, op1=ALU.subtract)
                        i.then_inc(rest1[j], 1)
                    for j, (_, bias, _) in enumerate(values):
                        v.wait_ge(val_done[j], p + 1)
                        if not first:
                            v.wait_ge(val_stored[u], 16 * len(values) * t)
                        product = bank_v[j][:, :].rearrange("p (b h w) -> p b h w", b=2, w=DK)
                        row = net.bias_row[:, bias, :].rearrange("p (h w) -> p h w", w=DK).unsqueeze(1).to_broadcast([P, 2, H, DK])
                        nc.vector.tensor_tensor(val[j][:, u, :, :].rearrange("p (b h) w -> p b h w", b=2), product, row,
                                                ALU.add).then_inc(val_read[j], 1)
                        nc.vector.tensor_tensor(val_parts[j][:, u, :, 0, 0:DK].rearrange("p (b h) w -> p b h w", b=2), product, row,
                                                ALU.add).then_inc(val_read[j], 1)
                    for j in range(len(values)):
                        v.wait_ge(val_read[j], 2 * p + 2)
                        nc.vector.tensor_tensor(val[j][:, u, :, :], val[j][:, u, :, :], val_parts[j][:, u, :, 0, 0:DK],
                                                ALU.subtract).then_inc(val_rest[j], 1)

                def value_part_c(p, u):
                    for j in range(len(values)):
                        v.wait_ge(val_b[j], p + 1)
                        nc.vector.tensor_tensor(val_parts[j][:, u, :, 2, 0:DK], val[j][:, u, :, :], val_parts[j][:, u, :, 1, 0:DK],
                                                ALU.subtract).then_inc(val_c[j], 1)

                for j in range(len(values)):
                    for u in range(2):
                        nc.vector.memset(val_parts[j][:, u, :, :, DK:VW], 0.0).then_inc(ones, 1)
                for j in range(len(values)):
                    for u in range(2):
                        v.wait_ge(ones, 2 * len(values))
                        nc.vector.memset(val_parts[j][:, u, :, 0, DK:VW], 1.0).then_inc(ones, 1)
                if values:
                    v.wait_ge(ones, 4 * len(values))
                norm(0, 0, True)
                norm(1, 1, True)
                for u in range(2):
                    work(u, u, True, 0)
                    norm(2 + u, u, False)
                with v.Fori(1, pairs // 2 - 1) as t:
                    for u in range(2):
                        work(2 * t + u, u, False, t)
                        norm(2 * t + u + 2, u, False)
                for u in range(2):
                    work(pairs - 2 + u, u, False, pairs // 2 - 1)
                value_part_c(pairs - 1, 1)

            @block.scalar
            def _(act):
                def value_part_b(p, u):
                    for j in range(len(values)):
                        act.wait_ge(val_rest[j], p + 1)
                        nc.scalar.activation(val_parts[j][:, u, :, 1, 0:DK], val[j][:, u, :, :], ACT.Copy).then_inc(val_b[j], 1)

                def work(p, u, first, t):
                    act.wait_ge(xT_done, p + 1)
                    if not first:
                        act.wait_ge(proj_done[0], p - 1)
                    nc.scalar.activation(xT[:, u, :, :].rearrange("p c t -> p (c t)"), bank_x[:, :], ACT.Copy).then_inc(xT_copied, 1)
                    if with_context:
                        act.wait_ge(cT_done, p + 1)
                        if not first:
                            act.wait_ge(val_done[1], p - 1)
                        nc.scalar.activation(cT[:, u, :, :].rearrange("p c t -> p (c t)"), bank_c[:, :], ACT.Copy).then_inc(cT_copied, 1)
                    if not (isinstance(p, int) and p == 0):
                        value_part_b(p - 1, 1 - u)
                    if not first:
                        act.wait_ge(stored[u], per_store * t)
                    for j, (_, bias, _, order) in enumerate(jobs):
                        act.wait_ge(proj_done[j], p + 1)
                        for o in range(C):
                            s = slice(o * 2 * P, (o + 1) * 2 * P)
                            i = nc.scalar.activation(parts[j][:, u, order.index(0), s], bank_j[j][:, s], ACT.Identity,
                                                     bias=net.bias_col[:, o, bias:bias + 1])
                        i.then_inc(part_a[j], 1)

                for u in range(2):
                    work(u, u, True, 0)
                with act.Fori(1, pairs // 2) as t:
                    for u in range(2):
                        work(2 * t + u, u, False, t)
                value_part_b(pairs - 1, 1)

            @block.gpsimd
            def _(pool):
                def work(p, u, first, t):
                    for j, (_, _, _, order) in enumerate(jobs):
                        ge(pool, rest1[j], p + 1)
                        if not first:
                            apart(pool, stored[u], per_store * t)
                        nc.gpsimd.tensor_copy(parts[j][:, u, order.index(1), :], rest[j][:, u, :]).then_inc(part_b[j], 1)
                        pool.wait_ge(part_b[j], p + 1)
                        nc.gpsimd.tensor_tensor(parts[j][:, u, order.index(2), :], rest[j][:, u, :],
                                                parts[j][:, u, order.index(1), :], ALU.subtract).then_inc(part_c[j], 1)

                for u in range(2):
                    work(u, u, True, 0)
                with pool.Fori(1, pairs // 2) as t:
                    for u in range(2):
                        work(2 * t + u, u, False, t)

            @block.tensor
            def _(pe):
                def turn(p, u, first, loads):
                    pe.wait_ge(normed_ready, p + 1)
                    if not first:
                        pe.wait_ge(xT_copied, p)
                    for c in range(C):
                        for s in range(2):
                            i = nc.tensor.transpose(bank_x[:, (c * 2 + s) * P:(c * 2 + s + 1) * P],
                                                    normed[:, u, s, c * P:(c + 1) * P], net.id_f[:, :])
                    i.then_inc(xT_done, 1)
                    if with_context:
                        if not first:
                            pe.wait_ge(cT_copied, p)
                        pe.wait_ge(ctx_loaded[u], 16 * loads)
                        for c in range(C):
                            for s in range(2):
                                i = nc.tensor.transpose(bank_c[:, (c * 2 + s) * P:(c * 2 + s + 1) * P],
                                                        ctx_in[:, u, s, c * P:(c + 1) * P], net.id_f[:, :])
                        i.then_inc(cT_done, 1)

                def products(p, u, first):
                    pe.wait_ge(xT_copied, p + 1)
                    for j, (m, _, _, _) in enumerate(jobs):
                        src = xT if j == 0 else cT
                        if j == 1:
                            pe.wait_ge(cT_copied, p + 1)
                        if not first:
                            pe.wait_ge(rest1[j], p)
                        for o in range(C):
                            for c in range(C):
                                i = nc.tensor.matmul(bank_j[j][:, o * 2 * P:(o + 1) * 2 * P], net.wT[:, m, c, o * P:(o + 1) * P],
                                                     src[:, u, c, :], start=(c == 0), stop=(c == C - 1))
                        i.then_inc(proj_done[j], 1)
                    for j, (m, _, _) in enumerate(values):
                        if not first:
                            pe.wait_ge(val_read[j], 2 * p)
                        for s in range(2):
                            for c in range(C):
                                i = nc.tensor.matmul(bank_v[j][:, s * D:(s + 1) * D], cT[:, u, c, s * P:(s + 1) * P],
                                                     net.wT[:, m, c, :], start=(c == 0), stop=(c == C - 1))
                        i.then_inc(val_done[j], 1)

                turn(0, 0, True, 1)
                turn(1, 1, False, 1)
                products(0, 0, True)
                turn(2, 0, False, 2)
                products(1, 1, False)
                with pe.Fori(1, pairs // 2 - 1) as t:
                    turn(2 * t + 1, 1, False, t + 1)
                    products(2 * t, 0, False)
                    turn(2 * t + 2, 0, False, t + 2)
                    products(2 * t + 1, 1, False)
                turn(pairs - 1, 1, False, pairs // 2)
                products(pairs - 2, 0, False)
                products(pairs - 1, 1, False)
        sem.release()


def pipeline(engine, nb, slot):
    groups = nb // 4
    for u in range(4):
        slot(u, u, 0)
    with engine.Fori(1, groups - 1) as t:
        for u in range(4):
            slot(4 * t + u, u, t)
    for u in range(4):
        slot(nb - 4 + u, u, groups - 1)
    for u in range(2):
        slot(nb + u, u, groups)


def ge(engine, semaphore, value):
    if not (isinstance(value, int) and value <= 0):
        engine.wait_ge(semaphore, value)


def apart(engine, semaphore, value):
    ge(engine, semaphore, value)
    if not isinstance(value, int):
        engine.nop(nofuse=True)


def attend(nc, net, layer):
    tag = f"a{layer}"
    nb = net.nb
    pos = layer == 1
    m_out = 4 * layer + 3
    with ExitStack() as ctx:
        def sb(name, shape, dt=F32):
            return ctx.enter_context(nc.sbuf_tensor(f"{tag}_{name}", shape, dt))

        sem = Semaphores(nc, tag)

        qr = sb("q_rows", [ROWS, 2, H, 2, P], BF16)
        kr = sb("k_rows", [ROWS, 2, H, 2, P], BF16)
        val = sb("values", [P, 2, 2, H, PARTS, VW], BF16)
        probs = sb("probs", [P, H, P])
        high = sb("probs_high", [P, 2, H, P], F16)
        low = sb("probs_low", [P, 2, H, P], F16)
        neg_max = sb("neg_max", [P, 2, H])
        neg_rest = sb("neg_rest", [P, H])
        neg_parts = sb("neg_parts", [P, 2, PARTS, H], BF16)
        neg_rows = sb("neg_rows", [PARTS * H, 2, P], BF16)
        sums = sb("recip_sums", [P, H])
        attn = sb("attn", [P, D])
        attnT = sb("attnT", [P, C, P])
        x_bias = sb("x_bias", [P, 2, D])
        stats = sb("stats", [P, 6])
        agg = sb("agg", [P, 2])
        if pos:
            pos_T = sb("pos_T", [P, 2, P, 2 * H])
            s_T = sb("scores_T", [P, 2, H, P])

        qk_loaded = [sem(f"qk_loaded{g}") for g in range(2)]
        v_loaded = [sem(f"v_loaded{g}") for g in range(2)]
        scores_done = sem("scores_done")
        added = sem("added")
        turned = sem("turned")
        max_done = sem("max_done")
        neg_step = sem("neg_step")
        neg_ready = sem("neg_ready")
        rows_done = sem("rows_done")
        rows_copied = sem("rows_copied")
        shifted = sem("shifted")
        z_ready = sem("z_ready")
        probs_ready = sem("probs_ready")
        high_ready = sem("high_ready")
        low_ready = {e: sem(f"low_ready_{e}") for e in ("v", "pool")}
        pv_done = sem("pv_done")
        recip = sem("recip")
        attn_ready = sem("attn_ready")
        attnT_done = sem("attnT_done")
        attnT_copied = sem("attnT_copied")
        out_done = sem("out_done")
        x_biased = sem("x_biased")
        x_added = sem("x_added")
        ln = sem("ln")
        stats_ready = sem("stats_ready")
        var_ready = sem("var_ready")
        final = sem("final")
        pos_done = sem("pos_done")
        pos_copied = sem("pos_copied")

        bank_s = net.bank[0:2]
        bank_t = net.bank[2:4]
        bank_pv = net.bank[4]
        bank_turn = net.bank[5]
        bank_pos = net.bank[6]
        bank_misc = net.bank[7]
        rows_ps = bank_misc[0:PARTS * H, D:D + P // 2].bitcast(BF16)
        LOW = ("pool", "pool", "v", "v") if not pos else ("pool",) * QUADS

        def low_waits(engine, n, q):
            ge(engine, low_ready[LOW[q]], LOW.count(LOW[q]) * n + LOW[:q].count(LOW[q]) + 1)

        def make_low(namespace, engine, m, u, q):
            ge(engine, high_ready, 4 * m + q + 1)
            if q == 0 or LOW[q] not in LOW[:q]:
                ge(engine, pv_done, m - 1)
            z = slice(4 * q, 4 * q + 4)
            namespace.tensor_tensor(low[:, (u - 1) % 2, z, :], probs[:, z, :], high[:, (u - 1) % 2, z, :],
                                    ALU.subtract).then_inc(low_ready[LOW[q]], 1)
        FILLS = 8
        fill = P // FILLS

        with nc.Block() as block:
            @block.sync
            def _(sp):
                def load(p, g, first):
                    if not first:
                        sp.wait_ge(scores_done if pos else shifted, 8 * p - 8)
                    for r0, r1, c0, c1 in ((0, 3, 0, 3), (3, 5, 0, 2), (5, 6, 0, 1)):
                        for dst, scr, lo in ((qr, net.q_scr[layer], c0), (kr, net.k_scr[layer], PARTS - (c1 - c0))):
                            sp.dma_start(
                                dst[r0 * DK:r1 * DK, g, :, :, :].rearrange("r h b t -> r (h b t)"),
                                scr.rearrange("n k (d h) t -> n (k d) (h t)", d=DK)[bass.ds(p, 1), lo * DK:(lo + c1 - c0) * DK, :]
                                .rearrange("n r t -> (n r) t")).then_inc(qk_loaded[g], 16)
                    if not first:
                        sp.wait_ge(pv_done, 2 * p - 2)
                    sp.dma_start(val[:, g, :, :, :, :].rearrange("p b h n w -> p (b h n w)"),
                                 net.v_scr[layer][bass.ds(p, 1)].rearrange("n p t -> (n p) t")).then_inc(v_loaded[g], 16)

                for g in range(2):
                    load(g, g, True)
                with sp.Fori(1, nb // 4) as t:
                    for g in range(2):
                        load(2 * t + g, g, False)

            def fills(k, u, t, do_s):
                if not pos or not do_s or isinstance(k, int) and k >= nb - 2:
                    return {}
                pair, g, loads = (2 * t + 1, 1, t + 1) if u < 2 else (2 * t + 2, 0, t + 2)
                places = "BCDE" if u % 2 == 0 else "ABCD"
                first = 4 * (u % 2)
                return {place: (pair, g, first + i, loads) for i, place in enumerate(places)}

            def some(plan, place, make):
                if place in plan:
                    make(*plan[place])

            def active(k, u, t):
                static = isinstance(k, int)
                return (not static or k < nb, not static or 1 <= k <= nb, not static or k >= 2)

            @block.tensor
            def _(pe):
                def scores(k, u, q):
                    g, b = u // 2, u % 2
                    ge(pe, added if pos else max_done, 4 * k + q - 1)
                    for n in range(4):
                        h = 4 * q + n
                        a, o = (kr, qr) if pos else (qr, kr)
                        i = nc.tensor.matmul(bank_s[q % 2][:, n * P:(n + 1) * P], a[0:ROWS, g, h, b, :], o[0:ROWS, g, h, b, :],
                                             start=True, stop=True)
                    i.then_inc(scores_done, 1)

                def turn(k, u, q):
                    pe.wait_ge(added, 4 * k + q + 1)
                    ge(pe, max_done, 4 * k + q)
                    for n in range(4):
                        i = nc.tensor.transpose(bank_turn[:, n * P:(n + 1) * P], s_T[:, u % 2, 4 * q + n, :], net.id_f[:, :])
                    i.then_inc(turned, 1)

                def cross(m, u):
                    pe.wait_ge(neg_ready, m + 1)
                    ge(pe, x_added, m - 1)
                    apart(pe, rows_copied, m)
                    nc.tensor.transpose(rows_ps, neg_parts[:, (u - 1) % 2, :, :].rearrange("p n h -> p (n h)"), net.id_b[:, :]).then_inc(rows_done, 1)

                def shift(m, u, q):
                    g, b = ((u - 1) % 4) // 2, (u - 1) % 2
                    if q == 0:
                        pe.wait_ge(rows_copied, m + 1)
                    ge(pe, z_ready if pos else high_ready, 4 * m + q - 1)
                    for n in range(4):
                        h = 4 * q + n
                        dst = bank_t[q % 2][:, n * P:(n + 1) * P]
                        if not pos:
                            nc.tensor.matmul(dst, kr[0:ROWS, g, h, b, :], qr[0:ROWS, g, h, b, :], start=True, stop=False)
                        i = nc.tensor.matmul(dst, net.pick[:, h, :], neg_rows[:, b, :], start=pos, stop=True)
                    i.then_inc(shifted, 1)

                def weigh(n, u, t, quads):
                    g, b = ((u - 2) % 4) // 2, u % 2
                    if 0 in quads:
                        pe.wait_ge(v_loaded[g], 16 * (t + 1 if u >= 2 else t))
                        ge(pe, attn_ready, n)
                    for q in quads:
                        pe.wait_ge(high_ready, 4 * n + q + 1)
                        low_waits(pe, n, q)
                        for j in range(4):
                            h = 4 * q + j
                            pairs = [(high, c) for c in range(PARTS)] + [(low, c) for c in range(2)]
                            for w, (half, c) in enumerate(pairs):
                                i = nc.tensor.matmul(bank_pv[:, h * VW:(h + 1) * VW], half[:, b, h, :], val[:, g, b, h, c, :],
                                                     start=(w == 0), stop=(w == len(pairs) - 1))
                    if QUADS - 1 in quads:
                        i.then_inc(pv_done, 1)

                def attention_turned(n):
                    pe.wait_ge(attn_ready, n + 1)
                    ge(pe, x_added, n)
                    for c in range(C):
                        i = nc.tensor.transpose(bank_misc[:, c * P:(c + 1) * P], attn[:, c * P:(c + 1) * P], net.id_f[:, :])
                    i.then_inc(attnT_done, 1)

                def output(n):
                    pe.wait_ge(attnT_copied, n + 1)
                    for c in range(C):
                        i = nc.tensor.matmul(bank_misc[:, 0:D], attnT[:, c, :], net.wT[:, m_out, c, :], start=(c == 0), stop=(c == C - 1))
                    i.then_inc(out_done, 1)

                def positions(p, g, f):
                    ge(pe, pos_copied, FILLS * p + f)
                    for n in range(fill):
                        i0 = f * fill + n
                        i = nc.tensor.matmul(bank_pos[:, n * 2 * H:(n + 1) * 2 * H], net.rel[0:ROWS, P - 1 - i0:2 * P - 1 - i0],
                                             qr[0:ROWS, g, :, :, i0],
                                             start=True, stop=True)
                    i.then_inc(pos_done, 1)

                def slot(k, u, t):
                    do_s, do_e, do_o = active(k, u, t)
                    m, n = k - 1, k - 2
                    plan = fills(k, u, t, do_s)
                    if do_s:
                        if u % 2 == 0:
                            pe.wait_ge(qk_loaded[u // 2], 96 * (t + 1))
                        scores(k, u, 0)
                        scores(k, u, 1)
                    if do_o:
                        weigh(n, u, t, (0, 1))
                    if do_s and pos:
                        turn(k, u, 0)
                        scores(k, u, 2)
                    if do_o:
                        weigh(n, u, t, (2,))
                    if do_e:
                        cross(m, u)
                    if do_o:
                        weigh(n, u, t, (3,))
                    if pos:
                        if do_s:
                            turn(k, u, 1)
                        some(plan, "A", load_and_fill)
                        if do_e:
                            shift(m, u, 0)
                        if do_s:
                            scores(k, u, 3)
                        if do_o:
                            attention_turned(n)
                        some(plan, "B", load_and_fill)
                        if do_e:
                            shift(m, u, 1)
                        if do_s:
                            turn(k, u, 2)
                        some(plan, "C", load_and_fill)
                        if do_e:
                            shift(m, u, 2)
                        if do_s:
                            turn(k, u, 3)
                        if do_o:
                            output(n)
                        some(plan, "D", load_and_fill)
                        if do_e:
                            shift(m, u, 3)
                        some(plan, "E", load_and_fill)
                    else:
                        if do_e:
                            shift(m, u, 0)
                        if do_s:
                            scores(k, u, 2)
                        if do_e:
                            shift(m, u, 1)
                        if do_o:
                            attention_turned(n)
                        if do_s:
                            scores(k, u, 3)
                        if do_e:
                            shift(m, u, 2)
                        if do_o:
                            output(n)
                        if do_e:
                            shift(m, u, 3)

                def load_and_fill(p, g, f, loads):
                    pe.wait_ge(qk_loaded[g], 96 * loads)
                    positions(p, g, f)

                if pos:
                    pe.wait_ge(qk_loaded[0], 96)
                    for f in range(FILLS):
                        positions(0, 0, f)
                pipeline(pe, nb, slot)

            @block.scalar
            def _(act):
                def copy_positions(p, g, f):
                    act.wait_ge(pos_done, FILLS * p + f + 1)
                    if f == 0:
                        ge(act, added, 8 * p - 8)
                    nc.scalar.activation(pos_T[:, g, f * fill:(f + 1) * fill, :].rearrange("p i n -> p (i n)"), bank_pos[:, :],
                                         ACT.Copy).then_inc(pos_copied, 1)

                def exponential(m, u, q):
                    b = (u - 1) % 2
                    act.wait_ge(z_ready if pos else shifted, 4 * m + q + 1)
                    if q == 0:
                        ge(act, pv_done, m - 1)
                    low_waits_before(act, m, q)
                    z = slice(4 * q, 4 * q + 4)
                    src = s_T[:, b, z, :].rearrange("p h t -> p (h t)") if pos else bank_t[q % 2][:, :]
                    nc.scalar.activation(probs[:, z, :].rearrange("p h t -> p (h t)"), src, ACT.Exp,
                                         bias=net.prob_bias[:, :]).then_inc(probs_ready, 1)
                    nc.scalar.activation(high[:, b, z, :].rearrange("p h t -> p (h t)"), src, ACT.Exp,
                                         bias=net.prob_bias[:, :]).then_inc(high_ready, 1)

                def low_waits_before(engine, m, q):
                    if not (isinstance(m, int) and m == 0):
                        low_waits(engine, m - 1, q)

                def slot(k, u, t):
                    do_s, do_e, do_o = active(k, u, t)
                    m, n = k - 1, k - 2
                    plan = fills(k, u, t, do_s)

                    def copy(p, g, f, loads):
                        copy_positions(p, g, f)

                    if do_e:
                        act.wait_ge(rows_done, m + 1)
                        ge(act, shifted, 4 * m - 4)
                        nc.scalar.activation(neg_rows[:, (u - 1) % 2, :], rows_ps, ACT.Copy).then_inc(rows_copied, 1)
                    some(plan, "A", copy)
                    if do_e:
                        exponential(m, u, 0)
                        if not pos:
                            exponential(m, u, 1)
                    if do_o:
                        act.wait_ge(attnT_done, n + 1)
                        ge(act, out_done, n)
                        nc.scalar.activation(attnT[:, :, :].rearrange("p c t -> p (c t)"), bank_misc[:, 0:D], ACT.Copy).then_inc(attnT_copied, 1)
                    some(plan, "B", copy)
                    if do_e and pos:
                        exponential(m, u, 1)
                    some(plan, "C", copy)
                    if do_e:
                        exponential(m, u, 2)
                    some(plan, "D", copy)
                    if do_e:
                        exponential(m, u, 3)
                    some(plan, "E", copy)

                if pos:
                    for f in range(FILLS):
                        copy_positions(0, 0, f)
                pipeline(act, nb, slot)

            @block.gpsimd
            def _(pool):
                def negative_parts(k, u):
                    b = u % 2
                    a, bb, c = (neg_parts[:, b, n, :] for n in range(PARTS))
                    pool.wait_ge(max_done, 4 * k + 4)
                    apart(pool, rows_done, k - 1)
                    nc.gpsimd.tensor_copy(a, neg_max[:, b, :]).then_inc(neg_step, 1)
                    pool.wait_ge(neg_step, 3 * k + 1)
                    nc.gpsimd.tensor_tensor(neg_rest[:, :], neg_max[:, b, :], a, ALU.subtract).then_inc(neg_step, 1)
                    apart(pool, neg_step, 3 * k + 2)
                    nc.gpsimd.tensor_copy(bb, neg_rest[:, :]).then_inc(neg_step, 1)
                    pool.wait_ge(neg_step, 3 * k + 3)
                    nc.gpsimd.tensor_tensor(c, neg_rest[:, :], bb, ALU.subtract).then_inc(neg_ready, 1)

                def slot(k, u, t):
                    do_s, do_e, do_o = active(k, u, t)
                    if do_o:
                        n = k - 2
                        ge(pool, x_added, n - 1)
                        nc.gpsimd.tensor_tensor(x_bias[:, u % 2, :], at(net.x, n), net.bias_row[:, 2 * layer + 1, :], ALU.add).then_inc(x_biased, 1)
                    for q in range(QUADS):
                        if do_s and q == (3 if pos else 2):
                            negative_parts(k, u)
                        if do_e and LOW[q] == "pool":
                            make_low(nc.gpsimd, pool, k - 1, u, q)

                pipeline(pool, nb, slot)
                pool.wait_ge(var_ready, 1)
                nc.gpsimd.tensor_tensor(net.rstd[:, :, 0], net.var_eps[:, :, 0], net.minus_half[:, :, 0], ALU.pow).then_inc(final, 1)
                pool.wait_ge(final, 1)

            @block.vector
            def _(v):
                def quad(ap, q):
                    return ap[:, 4 * q:4 * q + 4, :]

                def maximum(k, u, q):
                    v.wait_ge(turned if pos else scores_done, 4 * k + q + 1)
                    if q == 0:
                        ge(v, neg_ready, k - 1)
                    src = (bank_turn if pos else bank_s[q % 2])[:, :].rearrange("p (h t) -> p h t", h=4)
                    nc.vector.tensor_reduce(neg_max[:, u % 2, 4 * q:4 * q + 4], src, X, ALU.max, negate=True).then_inc(max_done, 1)

                def add_positions(k, u, q, pair):
                    v.wait_ge(scores_done, 4 * k + q + 1)
                    ge(v, high_ready, 4 * k + q - 7)
                    if q == 0:
                        v.wait_ge(pos_copied, FILLS * (pair + 1))
                    nc.vector.tensor_tensor(quad(s_T[:, u % 2, :, :], q), bank_s[q % 2][:, :].rearrange("p (h t) -> p h t", h=4),
                                            pos_T[:, u // 2, :, :].rearrange("p i (h b) -> p b h i", b=2)[:, u % 2, 4 * q:4 * q + 4, :],
                                            ALU.add).then_inc(added, 1)

                def add_shift(m, u, q):
                    b = (u - 1) % 2
                    v.wait_ge(shifted, 4 * m + q + 1)
                    z = quad(s_T[:, b, :, :], q)
                    nc.vector.tensor_tensor(z, bank_t[q % 2][:, :].rearrange("p (h t) -> p h t", h=4), z, ALU.add).then_inc(z_ready, 1)

                def normalise(n):
                    v.wait_ge(pv_done, n + 1)
                    out = bank_pv[:, 0:H * VW].rearrange("p (h w) -> p h w", w=VW)
                    nc.vector.reciprocal(sums[:, :], out[:, :, DK]).then_inc(recip, 1)
                    v.wait_ge(recip, n + 1)
                    ge(v, attnT_done, n)
                    nc.vector.tensor_tensor(attn[:, :].rearrange("p (h w) -> p h w", w=DK), out[:, :, 0:DK],
                                            sums[:, :].unsqueeze(2).to_broadcast([P, H, DK]), ALU.mult).then_inc(attn_ready, 1)

                def add_output(n, u):
                    v.wait_ge(out_done, n + 1)
                    v.wait_ge(x_biased, n + 1)
                    nc.vector.tensor_tensor(at(net.x, n), bank_misc[:, 0:D], x_bias[:, u % 2, :], ALU.add).then_inc(x_added, 1)

                def statistics(n):
                    apart(v, x_added, n + 1)
                    nc.vector.bn_stats(stats[:, :], at(net.x, n)).then_inc(ln, 1)

                def moments(n):
                    apart(v, ln, 2 * n + 1)
                    nc.vector.bn_aggr(agg[:, :], stats[:, :]).then_inc(ln, 1)

                def keep_moments(n):
                    apart(v, ln, 2 * n + 2)
                    nc.vector.tensor_copy(at(net.moments, n), agg[:, :]).then_inc(stats_ready, 1)

                def slot(k, u, t):
                    do_s, do_e, do_o = active(k, u, t)
                    m, n = k - 1, k - 2
                    if pos:
                        pair = 2 * t + u // 2
                        if do_s:
                            add_positions(k, u, 0, pair)
                            add_positions(k, u, 1, pair)
                            maximum(k, u, 0)
                            add_positions(k, u, 2, pair)
                        if do_o:
                            normalise(n)
                        if do_s:
                            maximum(k, u, 1)
                        if do_e:
                            add_shift(m, u, 0)
                        if do_s:
                            add_positions(k, u, 3, pair)
                        if do_e:
                            add_shift(m, u, 1)
                        if do_s:
                            maximum(k, u, 2)
                        if do_e:
                            add_shift(m, u, 2)
                        if do_s:
                            maximum(k, u, 3)
                        if do_o:
                            add_output(n, u)
                            statistics(n)
                        if do_e:
                            add_shift(m, u, 3)
                        if do_o:
                            moments(n)
                            keep_moments(n)
                    else:
                        if do_s:
                            maximum(k, u, 0)
                            maximum(k, u, 1)
                        if do_o:
                            normalise(n)
                        if do_s:
                            maximum(k, u, 2)
                            maximum(k, u, 3)
                        if do_e:
                            make_low(nc.vector, v, m, u, 2)
                        if do_o:
                            add_output(n, u)
                            statistics(n)
                        if do_e:
                            make_low(nc.vector, v, m, u, 3)
                        if do_o:
                            moments(n)
                            keep_moments(n)

                pipeline(v, nb, slot)
                v.wait_ge(stats_ready, nb)
                nc.vector.tensor_scalar(net.var_eps[:, :, 0], net.moments[:, :, 1], LN_EPS, None, ALU.add).then_inc(var_ready, 1)
                v.wait_ge(var_ready, 1)
        sem.release()


def experts(nc, net, ins):
    nb = net.nb
    with ExitStack() as ctx:
        def sb(name, shape, dt=F32):
            return ctx.enter_context(nc.sbuf_tensor(f"m_{name}", shape, dt))

        sem = Semaphores(nc, "m")

        NC = NE + C
        gate = sb("gate", [P, C, NE, DE])
        up = sb("up", [P, C, NE, DE])
        shared = sb("shared", [P, C, 2, D])
        down = sb("down", [P, NC, D])
        router = sb("router", [P, C, NE])
        normed = sb("normed", [P, 2, D])
        xT = sb("xT", [P, 2, C, P])
        tanh = sb("tanh", [P, 3, 512])
        gated = sb("gated", [P, 3, 512])
        acts = sb("acts", [P, NC, P])
        actsT = sb("actsT", [P, NC, P])
        top = sb("top", [P, 8])
        neg_top = sb("neg_top", [P, 1])
        expd = sb("expd", [P, NE])
        exp_sum = sb("exp_sum", [P, 1])
        recip = sb("recip", [P, 1])
        prob = sb("prob", [P, 16])
        best = sb("best", [P, 8])
        left = sb("left", [P, 16])
        coef = sb("coef", [P, 2, NE])
        stats = sb("stats", [P, 6])
        agg = sb("agg", [P, 2])

        loaded = sem("loaded")
        filled = sem("filled")
        normed_ready = sem("normed_ready")
        xT_done = sem("xT_done")
        xT_copied = sem("xT_copied")
        logits_done = sem("logits_done")
        route = sem("route")
        exp_ready = sem("exp_ready")
        unit_done = sem("unit_done")
        tanh_ready = sem("tanh_ready")
        gated_ready = sem("gated_ready")
        acts_ready = sem("acts_ready")
        actsT_done = sem("actsT_done")
        actsT_copied = sem("actsT_copied")
        out_done = sem("out_done")
        x_added = sem("x_added")
        ln = sem("ln")
        stats_ready = sem("stats_ready")
        var_ready = sem("var_ready")
        final = sem("final")

        bank_x = net.bank[0]
        logits = bank_x[:, D:D + NE]
        bank_g = [net.bank[1], net.bank[3], net.bank[1]]
        bank_u = [net.bank[2], net.bank[4], net.bank[1]]
        bank_a = net.bank[5:7]
        bank_o = net.bank[7]
        UNITS = ((0, 4), (4, 8), (8, 10))

        def steps(engine, slot):
            for u in range(2):
                slot(u, u)
            with engine.Fori(1, nb // 2 - 1) as t:
                for u in range(2):
                    slot(2 * t + u, u)
            for u in range(2):
                slot(nb - 2 + u, u)

        with nc.Block() as block:
            @block.sync
            def _(sp):
                sp.dma_start(router[:, :, :], ins["L0_ffn_router"].rearrange("(c p) e -> p c e", p=P)).then_inc(loaded, 16)
                for c in range(C):
                    s = slice(c * P, (c + 1) * P)
                    sp.dma_start(gate[:, c, :, :], ins["L0_ffn_experts_gate"][:, s, :].rearrange("e p d -> p e d")).then_inc(loaded, 16)
                    sp.dma_start(up[:, c, :, :], ins["L0_ffn_experts_up"][:, s, :].rearrange("e p d -> p e d")).then_inc(loaded, 16)
                    sp.dma_start(shared[:, c, 0, :], ins["L0_ffn_shared_gate"][s, :]).then_inc(loaded, 16)
                    sp.dma_start(shared[:, c, 1, :], ins["L0_ffn_shared_up"][s, :]).then_inc(loaded, 16)
                    sp.dma_start(down[:, NE + c, :], ins["L0_ffn_shared_down"][s, :]).then_inc(loaded, 16)
                sp.dma_start(down[:, 0:NE, :], ins["L0_ffn_experts_down"].rearrange("e p d -> p e d")).then_inc(loaded, 16)
                sp.wait_ge(loaded, 192)

            @block.tensor
            def _(pe):
                def turn(k, u):
                    pe.wait_ge(normed_ready, k + 1)
                    ge(pe, exp_ready, k)
                    for c in range(C):
                        i = nc.tensor.transpose(bank_x[:, c * P:(c + 1) * P], normed[:, u, c * P:(c + 1) * P], net.id_f[:, :])
                    i.then_inc(xT_done, 1)

                def route_logits(k, u):
                    pe.wait_ge(xT_copied, k + 1)
                    for c in range(C):
                        i = nc.tensor.matmul(logits, xT[:, u, c, :], router[:, c, :], start=(c == 0), stop=(c == C - 1))
                    i.then_inc(logits_done, 1)

                def slot(k, u):
                    for n, (lo, hi) in enumerate(UNITS):
                        if n == 2:
                            pe.wait_ge(acts_ready, 3 * k + 1)
                            if not (isinstance(k, int) and k == nb - 1):
                                turn(k + 1, 1 - u)
                        elif n == 0:
                            ge(pe, acts_ready, 3 * k)
                        else:
                            ge(pe, acts_ready, 3 * k - 1)
                        for w, bank in (((gate, bank_g[n]), (up, bank_u[n])) if n < 2 else ((shared, bank_g[n]),)):
                            for c in range(C):
                                rhs = w[:, c, lo:hi, :] if n < 2 else w[:, c, :, :]
                                i = nc.tensor.matmul(bank[:, :], xT[:, u, c, :], rhs.rearrange("p e d -> p (e d)"),
                                                     start=(c == 0), stop=(c == C - 1))
                        i.then_inc(unit_done, 1)
                    if not (isinstance(k, int) and k == nb - 1):
                        route_logits(k + 1, 1 - u)

                    def turn_acts(n):
                        lo, hi = UNITS[n]
                        pe.wait_ge(acts_ready, 3 * k + n + 1)
                        ge(pe, actsT_copied, 3 * k + n - 1)
                        for e in range(lo, hi):
                            i = nc.tensor.transpose(bank_a[n % 2][:, (e - lo) * P:(e - lo + 1) * P], acts[:, e, :], net.id_f[:, :])
                        i.then_inc(actsT_done, 1)

                    def sum_down(n):
                        lo, hi = UNITS[n]
                        pe.wait_ge(actsT_copied, 3 * k + n + 1)
                        for e in range(lo, hi):
                            i = nc.tensor.matmul(bank_o[:, 0:D], actsT[:, e, :], down[:, e, :], start=(e == 0), stop=(e == NC - 1))
                        return i

                    turn_acts(0)
                    turn_acts(1)
                    ge(pe, x_added, k)
                    sum_down(0)
                    turn_acts(2)
                    sum_down(1)
                    sum_down(2).then_inc(out_done, 1)

                pe.wait_ge(loaded, 192)
                turn(0, 0)
                route_logits(0, 0)
                steps(pe, slot)

            @block.scalar
            def _(act):
                def copy_x(k, u):
                    act.wait_ge(xT_done, k + 1)
                    ge(act, unit_done, 3 * k - 3)
                    nc.scalar.activation(xT[:, u, :, :].rearrange("p c t -> p (c t)"), bank_x[:, 0:D], ACT.Copy).then_inc(xT_copied, 1)

                def route_exp(k):
                    act.wait_ge(route, 9 * k + 2)
                    nc.scalar.activation(expd[:, :], logits, ACT.Exp, bias=neg_top[:, :], accum_out=exp_sum[:, :]).then_inc(exp_ready, 1)

                def slot(k, u):
                    last = isinstance(k, int) and k == nb - 1
                    for n in range(3):
                        act.wait_ge(unit_done, 3 * k + n + 1)
                        ge(act, gated_ready, 3 * k + n - 2)
                        w = 512 if n < 2 else D
                        nc.scalar.activation(tanh[:, n, 0:w], bank_g[n][:, 0:w], ACT.Tanh, scale=0.5).then_inc(tanh_ready, 1)
                        if n == 1 and not last:
                            copy_x(k + 1, 1 - u)
                    if not last:
                        route_exp(k + 1)
                    for n, (lo, hi) in enumerate(UNITS):
                        act.wait_ge(actsT_done, 3 * k + n + 1)
                        ge(act, out_done, k)
                        nc.scalar.activation(actsT[:, lo:hi, :].rearrange("p e t -> p (e t)"), bank_a[n % 2][:, 0:(hi - lo) * P],
                                             ACT.Copy).then_inc(actsT_copied, 1)

                copy_x(0, 0)
                route_exp(0)
                steps(act, slot)

            @block.gpsimd
            def _(pool):
                pool.wait_ge(var_ready, 1)
                nc.gpsimd.tensor_tensor(net.rstd[:, :, 0], net.var_eps[:, :, 0], net.minus_half[:, :, 0], ALU.pow).then_inc(final, 1)
                pool.wait_ge(final, 1)

            @block.vector
            def _(v):
                def norm(k, u):
                    ge(v, xT_done, k - 1)
                    nc.vector.tensor_scalar(normed[:, u, :], at(net.x, k), at(net.moments[:, :, 0:1], k), at(net.rstd, k),
                                            ALU.subtract, ALU.mult).then_inc(normed_ready, 1)

                def route_begin(k):
                    v.wait_ge(logits_done, k + 1)
                    nc.vector.tensor_copy(left[:, 8:16], logits).then_inc(route, 1)
                    v.wait_ge(route, 9 * k + 1)
                    nc.vector.tensor_reduce(neg_top[:, :], left[:, 8:16], X, ALU.max, negate=True).then_inc(route, 1)

                def route_end(k, u):
                    v.wait_ge(exp_ready, k + 1)
                    nc.vector.reciprocal(recip[:, :], exp_sum[:, :]).then_inc(route, 1)
                    v.wait_ge(route, 9 * k + 3)
                    nc.vector.tensor_scalar(prob[:, 0:NE], expd[:, :], recip[:, :], None, ALU.mult).then_inc(route, 1)
                    apart(v, route, 9 * k + 4)
                    nc.vector.max(top[:, :], prob[:, 0:NE]).then_inc(route, 1)
                    v.wait_ge(route, 9 * k + 5)
                    nc.vector.tensor_copy(best[:, 0:2], top[:, 0:2]).then_inc(route, 1)
                    apart(v, route, 9 * k + 6)
                    nc.vector.match_replace(left[:, :], best[:, :], prob[:, :], 0.0).then_inc(route, 1)
                    v.wait_ge(route, 9 * k + 7)
                    nc.vector.tensor_tensor(left[:, 0:NE], prob[:, 0:NE], left[:, 0:NE], ALU.subtract).then_inc(route, 1)
                    v.wait_ge(route, 9 * k + 8)
                    nc.vector.tensor_scalar(coef[:, u, :], left[:, 0:NE], 0.5, None, ALU.mult).then_inc(route, 1)

                def slot(k, u):
                    last = isinstance(k, int) and k == nb - 1
                    if not last:
                        norm(k + 1, 1 - u)
                    v.wait_ge(route, 9 * k + 9)
                    for n, (lo, hi) in enumerate(UNITS):
                        w = 512 if n < 2 else D
                        v.wait_ge(tanh_ready, 3 * k + n + 1)
                        nc.vector.scalar_tensor_tensor(out=gated[:, n, 0:w], in0=tanh[:, n, 0:w], scalar=1.0, in1=bank_g[n][:, 0:w],
                                                       op0=ALU.add, op1=ALU.mult).then_inc(gated_ready, 1)
                        v.wait_ge(gated_ready, 3 * k + n + 1)
                        ge(v, actsT_done, 3 * k)
                        if n < 2:
                            for e in range(lo, hi):
                                i = nc.vector.scalar_tensor_tensor(
                                    out=acts[:, e, :], in0=gated[:, n, (e - lo) * DE:(e - lo + 1) * DE], scalar=coef[:, u, e:e + 1],
                                    in1=bank_u[n][:, (e - lo) * DE:(e - lo + 1) * DE], op0=ALU.mult, op1=ALU.mult)
                        else:
                            i = nc.vector.scalar_tensor_tensor(
                                out=acts[:, NE:NC, :].rearrange("p e d -> p (e d)"), in0=gated[:, n, 0:D], scalar=0.5,
                                in1=bank_u[n][:, D:2 * D], op0=ALU.mult, op1=ALU.mult)
                        i.then_inc(acts_ready, 1)
                    if not last:
                        route_begin(k + 1)
                        route_end(k + 1, 1 - u)
                    v.wait_ge(out_done, k + 1)
                    nc.vector.tensor_tensor(at(net.x, k), bank_o[:, 0:D], at(net.x, k), ALU.add).then_inc(x_added, 1)
                    apart(v, x_added, k + 1)
                    nc.vector.bn_stats(stats[:, :], at(net.x, k)).then_inc(ln, 1)
                    apart(v, ln, 2 * k + 1)
                    nc.vector.bn_aggr(agg[:, :], stats[:, :]).then_inc(ln, 1)
                    apart(v, ln, 2 * k + 2)
                    nc.vector.tensor_copy(at(net.moments, k), agg[:, :]).then_inc(stats_ready, 1)

                nc.vector.memset(prob[:, :], -5.0).then_inc(filled, 1)
                nc.vector.memset(best[:, :], -5.0).then_inc(filled, 1)
                v.wait_ge(filled, 2)
                norm(0, 0)
                route_begin(0)
                route_end(0, 0)
                steps(v, slot)
                v.wait_ge(stats_ready, nb)
                nc.vector.tensor_scalar(net.var_eps[:, :, 0], net.moments[:, :, 1], LN_EPS, None, ALU.add).then_inc(var_ready, 1)
                v.wait_ge(var_ready, 1)
        sem.release()


def bitnet(nc, net, out):
    nb = net.nb
    with ExitStack() as ctx:
        def sb(name, shape, dt=F32):
            return ctx.enter_context(nc.sbuf_tensor(f"f_{name}", shape, dt))

        sem = Semaphores(nc, "f")

        conv_w = sb("conv_w", [P, HC, 3])
        out_scale = sb("out_scale", [P, 1])
        normed = sb("normed", [P, D])
        big1 = sb("big1", [P, 2, 1])
        scale1 = sb("scale1", [P, 1])
        inv1 = sb("inv1", [P, 1])
        round1 = sb("round1", [P, D])
        q1 = sb("q1", [P, D], BF16)
        diag = sb("diag", [P, P])
        q1T = sb("q1T", [P, C, P], BF16)
        inv_row = sb("inv_row", [P, P])
        hid = sb("hid", [P, 2, HC, P + 2])
        conv = sb("conv", [P, 2, HC, P])
        tanh = sb("tanh", [P, HID])
        silu2 = sb("silu2", [P, HID])
        big2 = sb("big2", [P, 1])
        scale2 = sb("scale2", [P, 1])
        inv2 = sb("inv2", [P, 1])
        round2 = sb("round2", [P, HID])
        q2 = sb("q2", [P, HID], BF16)
        q2T = sb("q2T", [P, HC, P], BF16)
        result = sb("result", [P, 2, D])

        init = sem("init")
        quant1 = sem("quant1")
        q1_ready = sem("q1_ready")
        diag_ready = sem("diag_ready")
        q1T_done = sem("q1T_done")
        q1T_copied = sem("q1T_copied")
        row_copied = sem("row_copied")
        hid_done = sem("hid_done")
        hid_ready = sem("hid_ready")
        centre = sem("centre")
        left = sem("left")
        conv_ready = sem("conv_ready")
        back_done = sem("back_done")
        tanh_ready = sem("tanh_ready")
        silu_ready = sem("silu_ready")
        quant2 = sem("quant2")
        rounded = sem("rounded")
        q2_ready = sem("q2_ready")
        q2T_done = sem("q2T_done")
        q2T_copied = sem("q2T_copied")
        out_done = sem("out_done")
        result_ready = sem("result_ready")
        stored = [sem(f"stored{i}") for i in range(2)]

        bank_q = net.bank[0]
        q1T_ps = bank_q[:, 0:P].bitcast(BF16)
        row_ps = bank_q[:, D:D + P]
        bank_h = net.bank[1:3]
        bank_b = net.bank[3:5]
        bank_q2 = net.bank[5]
        bank_o = net.bank[6]

        def steps(engine, slot):
            for k in range(4):
                slot(k, k % 2, k // 2)
            with engine.Fori(2, nb // 2) as t:
                for u in range(2):
                    slot(2 * t + u, u, t)
            slot(nb, 0, nb // 2)

        def active(k):
            return not isinstance(k, int) or k < nb, not isinstance(k, int) or k >= 1

        with nc.Block() as block:
            @block.sync
            def _(sp):
                def slot(k, u, t):
                    _, second = active(k)
                    if second:
                        n, b = k - 1, (u - 1) % 2
                        sp.wait_ge(result_ready, n + 1)
                        sp.dma_start(out[bass.ds(n, 1)].rearrange("n p d -> p (n d)"), result[:, b, :]).then_inc(stored[b], 16)

                steps(sp, slot)
                for b in range(2):
                    sp.wait_ge(stored[b], 16 * (nb // 2))

            @block.gpsimd
            def _(pool):
                def slot(k, u, t):
                    first, _ = active(k)
                    if first:
                        pool.wait_ge(quant1, 5 * k + 4)
                        apart(pool, q1T_done, k)
                        nc.gpsimd.tensor_scalar(diag[:, :], net.id_f[:, :], inv1[:, :], None, ALU.mult).then_inc(diag_ready, 1)

                steps(pool, slot)

            @block.tensor
            def _(pe):
                def slot(k, u, t):
                    first, second = active(k)
                    n = k - 1
                    if first:
                        pe.wait_ge(q1_ready, k + 1)
                        ge(pe, row_copied, k)
                        for c in range(C):
                            nc.tensor.transpose(q1T_ps[:, c * P:(c + 1) * P], q1[:, c * P:(c + 1) * P], net.id_b[:, :])
                        pe.wait_ge(diag_ready, k + 1)
                        nc.tensor.matmul(row_ps, net.ones_f[:, :], diag[:, :], start=True, stop=True).then_inc(q1T_done, 1)
                    if second:
                        for n2 in range(2):
                            pe.wait_ge(conv_ready, 2 * n + n2 + 1)
                            ge(pe, silu_ready, 2 * n + n2 - 1)
                            for c in range(4):
                                i = nc.tensor.transpose(bank_b[n2][:, c * P:(c + 1) * P], conv[:, (u - 1) % 2, 4 * n2 + c, :], net.id_f[:, :])
                            i.then_inc(back_done, 1)
                    if first:
                        pe.wait_ge(q1T_copied, k + 1)
                        for n2 in range(2):
                            ge(pe, hid_ready, 2 * k + n2 - 1)
                            for c in range(4):
                                for kc in range(C):
                                    s = (4 * n2 + c) * P
                                    i = nc.tensor.matmul(bank_h[n2][:, c * P:(c + 1) * P], net.w1T[:, kc, s:s + P], q1T[:, kc, :],
                                                         start=(kc == 0), stop=(kc == C - 1))
                            i.then_inc(hid_done, 1)
                    if second:
                        pe.wait_ge(q2_ready, n + 1)
                        ge(pe, q2T_copied, n)
                        for c in range(HC):
                            i = nc.tensor.transpose(bank_q2[:, :].bitcast(BF16)[:, c * P:(c + 1) * P], q2[:, c * P:(c + 1) * P], net.id_b[:, :])
                        i.then_inc(q2T_done, 1)
                        pe.wait_ge(q2T_copied, n + 1)
                        ge(pe, result_ready, n)
                        for c in range(HC):
                            i = nc.tensor.matmul(bank_o[:, 0:D], q2T[:, c, :], net.w2T[:, c, :], start=(c == 0), stop=(c == HC - 1))
                        i.then_inc(out_done, 1)

                pe.wait_ge(init, 3)
                steps(pe, slot)

            @block.scalar
            def _(act):
                def slot(k, u, t):
                    first, second = active(k)
                    n = k - 1
                    if first:
                        act.wait_ge(q1T_done, k + 1)
                        ge(act, hid_done, 2 * k)
                        nc.scalar.activation(q1T[:, :, :].rearrange("p c t -> p (c t)"), q1T_ps, ACT.Copy).then_inc(q1T_copied, 1)
                        ge(act, hid_ready, 2 * k)
                        nc.scalar.activation(inv_row[:, :], row_ps, ACT.Copy).then_inc(row_copied, 1)
                    if second:
                        for n2 in range(2):
                            act.wait_ge(back_done, 2 * n + n2 + 1)
                            ge(act, silu_ready, 2 * n + n2 - 1)
                            nc.scalar.activation(tanh[:, n2 * 512:(n2 + 1) * 512], bank_b[n2][:, :], ACT.Tanh, scale=0.5).then_inc(tanh_ready, 1)
                    if first:
                        for c in range(HC):
                            if c % 4 == 0:
                                act.wait_ge(hid_ready, 2 * k + c // 4 + 1)
                                ge(act, back_done, 2 * (k - 1) + c // 4 - 1)
                            nc.scalar.activation(conv[:, u, c, :], hid[:, u, c, 1:P + 1], ACT.Identity, bias=net.conv_b[:, c:c + 1],
                                                 scale=conv_w[:, c, 1:2]).then_inc(centre, 1)
                    if second:
                        act.wait_ge(quant2, 4 * n + 4)
                        ge(act, q2_ready, n)
                        nc.scalar.activation(round2[:, :], silu2[:, :], ACT.Copy, bias=ROUND, scale=scale2[:, :]).then_inc(rounded, 1)
                        act.wait_ge(q2T_done, n + 1)
                        ge(act, out_done, n)
                        nc.scalar.activation(q2T[:, :, :].rearrange("p c t -> p (c t)"), bank_q2[:, :].bitcast(BF16), ACT.Copy).then_inc(q2T_copied, 1)

                act.wait_ge(init, 3)
                steps(act, slot)

            @block.vector
            def _(v):
                def quantise(k):
                    nc.vector.tensor_scalar(normed[:, :], at(net.x, k), at(net.moments[:, :, 0:1], k), at(net.rstd, k),
                                            ALU.subtract, ALU.mult).then_inc(quant1, 1)
                    v.wait_ge(quant1, 5 * k + 1)
                    nc.vector.tensor_reduce(big1[:, 0, :], normed[:, :], X, ALU.max, apply_absolute_value=True).then_inc(quant1, 1)
                    v.wait_ge(quant1, 5 * k + 2)
                    ge(v, diag_ready, k)
                    nc.vector.tensor_scalar(inv1[:, :], big1[:, 0, :], 1e-5, 1.0 / 127.0, ALU.max, ALU.mult).then_inc(quant1, 1)
                    v.wait_ge(quant1, 5 * k + 3)
                    nc.vector.reciprocal(scale1[:, :], inv1[:, :]).then_inc(quant1, 1)
                    v.wait_ge(quant1, 5 * k + 4)
                    nc.vector.tensor_scalar(round1[:, :], normed[:, :], scale1[:, :], ROUND, ALU.mult, ALU.add).then_inc(quant1, 1)
                    v.wait_ge(quant1, 5 * k + 5)
                    ge(v, q1T_done, k)
                    nc.vector.tensor_scalar(q1[:, :], round1[:, :], -ROUND, 127.0, ALU.add, ALU.min).then_inc(q1_ready, 1)

                def slot(k, u, t):
                    first, second = active(k)
                    n = k - 1
                    if second:
                        for n2 in range(2):
                            s = slice(n2 * 512, (n2 + 1) * 512)
                            v.wait_ge(tanh_ready, 2 * n + n2 + 1)
                            ge(v, rounded, n)
                            nc.vector.scalar_tensor_tensor(out=silu2[:, s], in0=tanh[:, s], scalar=1.0, in1=bank_b[n2][:, :],
                                                           op0=ALU.add, op1=ALU.mult).then_inc(silu_ready, 1)
                        v.wait_ge(silu_ready, 2 * n + 2)
                        nc.vector.tensor_reduce(big2[:, :], silu2[:, :], X, ALU.max, apply_absolute_value=True).then_inc(quant2, 1)
                        v.wait_ge(quant2, 4 * n + 1)
                        nc.vector.tensor_scalar(big2[:, :], big2[:, :], 2e-5, 1.0 / 127.0, ALU.max, ALU.mult).then_inc(quant2, 1)
                        v.wait_ge(quant2, 4 * n + 2)
                        nc.vector.reciprocal(scale2[:, :], big2[:, :]).then_inc(quant2, 1)
                        nc.vector.tensor_scalar(inv2[:, :], big2[:, :], out_scale[:, :], None, ALU.mult).then_inc(quant2, 1)
                    if first:
                        for n2 in range(2):
                            v.wait_ge(hid_done, 2 * k + n2 + 1)
                            v.wait_ge(row_copied, k + 1)
                            ge(v, centre, 8 * (k - 1))
                            nc.vector.tensor_tensor(hid[:, u, 4 * n2:4 * n2 + 4, 1:P + 1], bank_h[n2][:, :].rearrange("p (c t) -> p c t", c=4),
                                                    inv_row[:, :].unsqueeze(1).to_broadcast([P, 4, P]), ALU.mult).then_inc(hid_ready, 1)
                        v.wait_ge(hid_ready, 2 * k + 2)
                    if second:
                        v.wait_ge(rounded, n + 1)
                        ge(v, q2T_done, n)
                        nc.vector.tensor_scalar(q2[:, :], round2[:, :], -ROUND, 127.0, ALU.add, ALU.min).then_inc(q2_ready, 1)
                    if first:
                        for c in range(HC):
                            v.wait_ge(centre, 8 * k + c + 1)
                            nc.vector.scalar_tensor_tensor(out=conv[:, u, c, :], in0=hid[:, u, c, 0:P], scalar=conv_w[:, c, 0:1],
                                                           in1=conv[:, u, c, :], op0=ALU.mult, op1=ALU.add).then_inc(left, 1)
                        for c in range(HC):
                            v.wait_ge(left, 8 * k + c + 1)
                            i = nc.vector.scalar_tensor_tensor(out=conv[:, u, c, :], in0=hid[:, u, c, 2:P + 2], scalar=conv_w[:, c, 2:3],
                                                               in1=conv[:, u, c, :], op0=ALU.mult, op1=ALU.add)
                            if c % 4 == 3:
                                i.then_inc(conv_ready, 1)
                    if first and not (isinstance(k, int) and k == nb - 1) and not isinstance(k, int):
                        pass
                    if second:
                        v.wait_ge(out_done, n + 1)
                        b = (u - 1) % 2
                        ge(v, stored[b], 16 * (t if b == 0 else t - 1))
                        nc.vector.scalar_tensor_tensor(out=result[:, b, :], in0=bank_o[:, 0:D], scalar=inv2[:, :], in1=at(net.x, n),
                                                       op0=ALU.mult, op1=ALU.add).then_inc(result_ready, 1)

                nc.vector.tensor_tensor(conv_w[:, :, :], net.conv_w[:, :, :],
                                        net.w_dequant[:, 0:1].unsqueeze(1).to_broadcast([P, HC, 3]), ALU.mult).then_inc(init, 1)
                nc.vector.tensor_scalar(out_scale[:, :], net.w_dequant[:, 1:2], 0.5, None, ALU.mult).then_inc(init, 1)
                nc.vector.memset(hid[:, :, :, :], 0.0).then_inc(init, 1)
                v.wait_ge(init, 3)

                def whole(k, u, t):
                    if active(k)[0]:
                        quantise(k)
                    slot(k, u, t)

                steps(v, whole)


def build(nc, ins, out):
    net = Net()
    net.nb = ins["x"].shape[0]
    pairs = net.nb // 2
    net.q_scr = [nc.dram_tensor(f"q_scratch{n}", (pairs, PARTS, P, C * 2 * P), BF16, kind="Internal").ap() for n in range(2)]
    net.k_scr = [nc.dram_tensor(f"k_scratch{n}", (pairs, PARTS, P, C * 2 * P), BF16, kind="Internal").ap() for n in range(2)]
    net.v_scr = [nc.dram_tensor(f"v_scratch{n}", (pairs, P, 2 * H * PARTS * VW), BF16, kind="Internal").ap() for n in range(2)]
    with ExitStack() as ctx:
        lay_out(nc, ctx, net)
        prepare(nc, net, ins)
        project(nc, net, 0, True, ins)
        attend(nc, net, 0)
        experts(nc, net, ins)
        project(nc, net, 1, False, ins)
        attend(nc, net, 1)
        bitnet(nc, net, out)


def kernel(**inputs):
    import numpy as _np
    import concourse.bacc as _bacc
    from concourse import mybir as _mybir
    from concourse.bass_utils import run_bass_kernel_spmd as _run

    nc = _bacc.Bacc("TRN2", target_bir_lowering=False, num_devices=1)
    arrays, ins = {}, {}
    for name, value in inputs.items():
        a = _np.ascontiguousarray(value)
        arrays[f"in_{name}_dram"] = a
        ins[name] = nc.dram_tensor(f"in_{name}_dram", a.shape, _mybir.dt.from_np(a.dtype), kind="ExternalInput").ap()
    shape = inputs["x"].shape
    out = nc.dram_tensor("out_0_dram", shape, _mybir.dt.float32, kind="ExternalOutput").ap()
    build(nc, ins, out)
    return _run(nc, [arrays], core_ids=[0]).results[0]["out_0_dram"]
```

```python
import math
from contextlib import ExitStack

import concourse.bass as bass
from concourse import mybir
from concourse.alu_op_type import AluOpType as ALU

F32 = mybir.dt.float32
BF16 = mybir.dt.bfloat16
F16 = mybir.dt.float16
ACT = mybir.ActivationFunctionType
X = mybir.AxisListType.X

P = 128
D = 256
C = D // P
H = 16
DK = D // H
H8 = H // C
QUADS = H // 4
VW = DK + 1
PARTS = 3
PRODUCTS = 8
ROWS = PRODUCTS * DK
NE = 8
DE = 128
PIECES = 10
HID = 1024
HC = HID // P
HALF = HID // 2
ACT_SCALE = 2.0 ** 10
TAP_SCALE = 2.0 ** 13
LN_EPS = 1e-5
ROUND = 12582912.0
MAXLEN = 512

ATT = ["L0_xattn_w_q", "L0_xattn_w_k", "L0_xattn_w_v", "L0_xattn_w_o",
       "L1_xattn_wq", "L1_xattn_wk", "L1_xattn_wv", "L1_xattn_wo"]
BIASES = ["L0_xattn_b_q", "L0_xattn_b_k", "L1_xattn_bq", "L1_xattn_bk"]
ROW_BIASES = ["L0_xattn_b_v", "L0_xattn_b_o", "L1_xattn_bv", "L1_xattn_bo"]


class Net:
    pass


class Semaphores:

    def __init__(self, nc, tag):
        self.nc, self.tag, self.all = nc, tag, []

    def __call__(self, name):
        self.all.append(self.nc.alloc_semaphore(f"{self.tag}_{name}"))
        return self.all[-1]

    def release(self):
        self.nc.clear_and_free_semaphores(self.all)
        self.nc.all_engine_barrier()


def at(ap, index):
    return ap[:, bass.ds(index, 1), :].rearrange("p o n -> p (o n)")


def lay_out(nc, ctx, net):
    def sb(name, shape, dt=F32):
        return ctx.enter_context(nc.sbuf_tensor(name, shape, dt))

    net.bank = [ctx.enter_context(nc.psum_tensor(f"bank{i}", [P, 512], F32)) for i in range(8)]
    nb = net.nb
    net.x = sb("x_all", [P, nb, D])
    net.moments = sb("moments_all", [P, nb, 2])
    net.var_eps = sb("var_eps_all", [P, nb, 1])
    net.rstd = sb("rstd_all", [P, nb, 1])
    net.minus_half = sb("minus_half", [P, nb, 1])
    net.eps = sb("eps", [P, 1])
    net.wT = sb("wT", [P, 8, C, D])
    net.w1T = sb("w1T", [P, C, HID], BF16)
    net.w2T = sb("w2T", [P, HC, D], BF16)
    net.w_dequant = sb("w_dequant", [P, 2])
    net.conv_w = sb("conv_w", [P, C, 3, 2, HID], F16)
    net.conv_bias = sb("conv_bias", [P, HID], BF16)
    net.half_scale = sb("half_scale", [P, 1])
    net.half_scale_127 = sb("half_scale_127", [P, 1])
    net.rel = sb("rel", [P, 2 * P], BF16)
    net.bias_col = sb("bias_col", [P, C, 4])
    net.bias_row = sb("bias_row", [P, 4, D])
    net.prob_bias = sb("prob_bias", [P, 1])
    net.id_f = sb("id_f", [P, P])
    net.id_b = sb("id_b", [P, P], BF16)
    net.ones_b = sb("ones_b", [P, P], BF16)
    net.pick = sb("pick", [PARTS * H, H, P], BF16)


def lay_out_experts(nc, ctx, net):
    def sb(name, shape, dt=F32):
        return ctx.enter_context(nc.sbuf_tensor(name, shape, dt))

    net.w_pieces = sb("w_pieces", [P, PIECES, 512])
    net.down = sb("down", [P, NE + C, D])
    net.router = sb("router", [P, C, NE])
    net.piece_max = sb("piece_max", [P, net.nb // 2, 1])
    net.down_max = sb("down_max", [P, net.nb // 2, 1])
    net.moe_loaded = nc.alloc_semaphore("moe_loaded")
    net.ups_loaded = nc.alloc_semaphore("ups_loaded")


def load_experts(engine, net, ins):
    for n in range(PIECES):
        c = n % 2
        s = slice(c * P, (c + 1) * P)
        piece = net.w_pieces[:, n, :]
        if n < 8:
            name = ("L0_ffn_experts_gate", "L0_ffn_experts_up")[n // 2 % 2]
            lo = 4 * (n // 4)
            engine.dma_start(piece.rearrange("p (e d) -> p e d", e=4), ins[name][lo:lo + 4, s, :].rearrange("e p d -> p e d")).then_inc(net.ups_loaded, 16)
        else:
            engine.dma_start(piece[:, 0:D], ins["L0_ffn_shared_gate"][s, :]).then_inc(net.ups_loaded, 16)
            engine.dma_start(piece[:, D:2 * D], ins["L0_ffn_shared_up"][s, :]).then_inc(net.ups_loaded, 16)
    engine.dma_start(net.router[:, :, :], ins["L0_ffn_router"].rearrange("(c p) e -> p c e", p=P)).then_inc(net.moe_loaded, 16)
    for c in range(C):
        engine.dma_start(net.down[:, NE + c, :], ins["L0_ffn_shared_down"][c * P:(c + 1) * P, :]).then_inc(net.moe_loaded, 16)
    engine.dma_start(net.down[:, 0:NE, :], ins["L0_ffn_experts_down"].rearrange("e p d -> p e d")).then_inc(net.moe_loaded, 16)


def prepare(nc, net, ins):
    with ExitStack() as ctx:
        def sb(name, shape, dt=F32):
            return ctx.enter_context(nc.sbuf_tensor(name, shape, dt))

        sem = Semaphores(nc, "w")
        nb = net.nb
        quarters = [slice(n * nb // 4, (n + 1) * nb // 4) for n in range(4)]

        raw = sb("raw_att", [P, 8, C, D])
        w_raw = sb("w_raw", [P, 2, 2048])
        w_q = sb("w_q", [P, 2, 2048], BF16)
        w_abs = sb("w_abs", [P, 2])
        w_mean = sb("w_mean", [P, 2])
        w_scale = sb("w_scale", [P, 2])
        rel_raw = sb("rel_raw", [P, 2, DK])
        rel_r1 = sb("rel_r1", [P, 2, DK])
        rel_r2 = sb("rel_r2", [P, 2, DK])
        rel_parts = sb("rel_parts", [P, 2, PRODUCTS, DK], BF16)
        bias_raw = sb("bias_raw", [4, D])
        bias_apart = sb("bias_apart", [4, C, P])
        stats = sb("stats0", [P, nb // 4, 6])
        ones_f = sb("ones_f", [P, P])

        att_loaded = sem("att_loaded")
        w12_loaded = sem("w12_loaded")
        x_loaded = [sem(f"x_loaded{n}") for n in range(4)]
        small_loaded = sem("small_loaded")
        rows_loaded = sem("rows_loaded")
        zeroed = sem("zeroed")
        consts = sem("consts")
        att_done = sem("att_done")
        att_copied = sem("att_copied")
        abs_done = sem("abs_done")
        mean_done = sem("mean_done")
        dve = sem("dve")
        w12_quantised = sem("w12_quantised")
        w12_done = sem("w12_done")
        w12_copied = sem("w12_copied")
        rel_ready = sem("rel_ready")
        rel_done = sem("rel_done")
        bias_ordered = sem("bias_ordered")
        bias_done = sem("bias_done")
        small_copied = sem("small_copied")
        ln_stats = sem("ln_stats")
        ln = sem("ln")
        var_ready = sem("var_ready")
        shifted = sem("shifted")

        with nc.Block() as block:
            @block.sync
            def _(sp):
                sp.dma_start(w_raw[:, 0, :].rearrange("p (c i) -> p c i", c=HC),
                             ins["L1_ffn_w1"].rearrange("(c p) i -> p c i", p=P)).then_inc(w12_loaded, 16)
                sp.dma_start(w_raw[:, 1, :].rearrange("p (c i) -> p c i", c=C),
                             ins["L1_ffn_w2"].rearrange("(c p) i -> p c i", p=P)).then_inc(w12_loaded, 16)
                for n, s in enumerate(quarters):
                    sp.dma_start(net.x[:, s, :], ins["x"][s].rearrange("b p d -> p b d")).then_inc(x_loaded[n], 16)
                for m in range(8):
                    sp.dma_start(raw[:, m, :, :], ins[ATT[m]].rearrange("(c p) i -> p c i", p=P)).then_inc(att_loaded, 16)
                load_experts(sp, net, ins)
                sp.wait_ge(att_loaded, 128)
                for n in range(4):
                    sp.wait_ge(x_loaded[n], 16)
                sp.wait_ge(w12_loaded, 32)

            @block.scalar
            def _(act):
                act.dma_start(rel_raw[:, :, :], ins["L1_xattn_rel_emb"][MAXLEN - P + 1:MAXLEN + P + 1, :]
                              .rearrange("(c p) d -> p c d", p=P)).then_inc(small_loaded, 16)
                for n, name in enumerate(BIASES):
                    act.dma_start(bias_raw[n:n + 1, :], ins[name].rearrange("(a n) -> a n", a=1)).then_inc(small_loaded, 16)
                for n, name in enumerate(ROW_BIASES):
                    act.dma_start(net.bias_row[:, n, :], ins[name].partition_broadcast(P)).then_inc(rows_loaded, 16)
                act.wait_ge(small_loaded, 80)
                nc.scalar.activation(bias_apart[:, :, :].rearrange("n o (d h) -> n o d h", d=DK),
                                     bias_raw[:, :].rearrange("n (h o d) -> n o d h", o=C, d=DK), ACT.Copy).then_inc(bias_ordered, 1)
                act.wait_ge(dve, 2)
                for n in range(2):
                    nc.scalar.activation(w_raw[:, n, :], w_raw[:, n, :], ACT.Copy, bias=ROUND, scale=w_scale[:, n:n + 1]).then_inc(shifted, 1)
                for m in range(8):
                    act.wait_ge(att_done, m + 1)
                    src = net.bank[m % 4][:, :]
                    quarter = 0.25 if m in (0, 4) else 1.0
                    if m % 4 < 2:
                        for c in range(C):
                            i = nc.scalar.activation(
                                net.wT[:, m, c, :].rearrange("p (o d h) -> p o d h", o=C, d=DK),
                                src[:, c * D:(c + 1) * D].rearrange("p (h o d) -> p o d h", o=C, d=DK),
                                ACT.Copy, scale=quarter)
                    else:
                        i = nc.scalar.activation(net.wT[:, m, :, :].rearrange("p c o -> p (c o)"), src, ACT.Copy)
                    i.then_inc(att_copied, 1)
                for n in range(4):
                    act.wait_ge(w12_done, n + 1)
                    src = net.bank[4 + n][:, :].bitcast(BF16)
                    if n < 2:
                        i = nc.scalar.activation(net.w1T[:, n, :], src, ACT.Copy)
                    else:
                        i = nc.scalar.activation(net.w2T[:, :, (n - 2) * P:(n - 1) * P],
                                                 src.rearrange("p (c o) -> p c o", c=HC), ACT.Copy)
                    i.then_inc(w12_copied, 1)
                act.wait_ge(rel_done, 1)
                nc.scalar.activation(net.rel[0:ROWS, :], net.bank[1][0:ROWS, 0:P].bitcast(BF16), ACT.Copy).then_inc(small_copied, 1)
                act.wait_ge(bias_done, 1)
                for o in range(C):
                    nc.scalar.activation(net.bias_col[:, o, 0:4:2], net.bank[0][:, 4 * o:4 * o + 4:2], ACT.Copy, scale=0.25).then_inc(small_copied, 1)
                    nc.scalar.activation(net.bias_col[:, o, 1:4:2], net.bank[0][:, 4 * o + 1:4 * o + 4:2], ACT.Copy).then_inc(small_copied, 1)
                act.wait_ge(small_copied, 5)
                act.wait_ge(att_copied, 8)
                act.wait_ge(w12_copied, 4)
                act.wait_ge(rows_loaded, 64)
                act.wait_ge(small_loaded, 80)

            @block.gpsimd
            def _(pool):
                nc.gpsimd.memset(net.id_f[:, :], 0.0).then_inc(zeroed, 1)
                nc.gpsimd.memset(net.id_b[:, :], 0.0).then_inc(zeroed, 1)
                nc.gpsimd.memset(net.pick[:, :, :], 0.0).then_inc(zeroed, 1)
                nc.gpsimd.memset(ones_f[:, :], 1.0).then_inc(consts, 1)
                nc.gpsimd.memset(net.ones_b[:, :], 1.0).then_inc(consts, 1)
                nc.gpsimd.memset(net.conv_bias[:, :], 0.0).then_inc(consts, 1)
                nc.gpsimd.memset(net.eps[:, :], LN_EPS).then_inc(consts, 1)
                nc.gpsimd.memset(net.minus_half[:, :, :], -0.5).then_inc(consts, 1)
                nc.gpsimd.memset(net.prob_bias[:, :], math.log(2.0 ** 13)).then_inc(consts, 1)
                pool.wait_ge(zeroed, 3)
                for m in (net.id_f, net.id_b):
                    nc.gpsimd.affine_select(out=m[:, :], in_=m[:, :], compare_op=ALU.not_equal, fill=1.0, base=0,
                                            pattern=[[-1, P]], channel_multiplier=1).then_inc(consts, 1)
                for part in range(PARTS):
                    pool.wait_ge(zeroed, 3 + part)
                    nc.gpsimd.affine_select(out=net.pick[:, :, :], in_=net.pick[:, :, :], compare_op=ALU.not_equal,
                                            fill=1.0, base=-part * H, pattern=[[-1, H], [0, P]],
                                            channel_multiplier=1).then_inc(zeroed, 1)
                pool.wait_ge(zeroed, 6)
                pool.wait_ge(consts, 8)
                for n, s in enumerate(quarters):
                    pool.wait_ge(var_ready, n + 1)
                    nc.gpsimd.tensor_tensor(net.rstd[:, s, 0], net.var_eps[:, s, 0], net.minus_half[:, s, 0], ALU.pow).then_inc(consts, 1)
                pool.wait_ge(consts, 12)

            @block.vector
            def _(v):
                def moments(n):
                    s = quarters[n]
                    v.wait_ge(x_loaded[n], 16)
                    for b in range(s.start, s.stop):
                        nc.vector.bn_stats(stats[:, b - s.start, :], net.x[:, b, :]).then_inc(ln_stats, 1)
                    for b in range(s.start, s.stop):
                        v.wait_ge(ln_stats, b + 1)
                        nc.vector.bn_aggr(net.moments[:, b, :], stats[:, b - s.start, :]).then_inc(ln, 1)
                    v.wait_ge(ln, s.stop)
                    nc.vector.tensor_scalar(net.var_eps[:, s, 0], net.moments[:, s, 1], LN_EPS, None, ALU.add).then_inc(var_ready, 1)

                v.wait_ge(w12_loaded, 32)
                nc.vector.tensor_reduce(w_abs[:, :], w_raw[:, :, :], X, ALU.add, apply_absolute_value=True).then_inc(abs_done, 1)
                v.wait_ge(mean_done, 1)
                nc.vector.tensor_scalar(w_mean[:, :], net.bank[7][:, 0:2], 1.0 / (HID * D), 1e-5, ALU.mult, ALU.max).then_inc(dve, 1)
                v.wait_ge(dve, 1)
                nc.vector.reciprocal(w_scale[:, :], w_mean[:, :]).then_inc(dve, 1)
                v.wait_ge(dve, 2)
                nc.vector.reciprocal(net.w_dequant[:, :], w_scale[:, :]).then_inc(dve, 1)
                moments(0)
                for n in range(2):
                    v.wait_ge(shifted, n + 1)
                    nc.vector.tensor_scalar(w_raw[:, n, :], w_raw[:, n, :], -ROUND, 1.0, ALU.add, ALU.min).then_inc(dve, 1)
                    v.wait_ge(dve, 4 + n)
                    nc.vector.tensor_scalar(w_q[:, n, :], w_raw[:, n, :], -1.0, None, ALU.max).then_inc(w12_quantised, 1)
                moments(1)
                v.wait_ge(small_loaded, 80)
                ra, rb, rc = (rel_parts[:, :, n, :] for n in (2, 1, 0))
                nc.vector.tensor_copy(ra, rel_raw[:, :, :]).then_inc(dve, 1)
                v.wait_ge(dve, 6)
                nc.vector.tensor_tensor(rel_r1[:, :, :], rel_raw[:, :, :], ra, ALU.subtract).then_inc(dve, 1)
                v.wait_ge(dve, 7)
                nc.vector.tensor_copy(rb, rel_r1[:, :, :]).then_inc(dve, 1)
                v.wait_ge(dve, 8)
                nc.vector.tensor_tensor(rel_r2[:, :, :], rel_r1[:, :, :], rb, ALU.subtract).then_inc(dve, 1)
                v.wait_ge(dve, 9)
                nc.vector.tensor_copy(rc, rel_r2[:, :, :]).then_inc(rel_ready, 1)
                nc.vector.tensor_copy(rel_parts[:, :, 3, :], rb).then_inc(rel_ready, 1)
                nc.vector.tensor_copy(rel_parts[:, :, 4, :], ra).then_inc(rel_ready, 1)
                nc.vector.tensor_copy(rel_parts[:, :, 5, :], ra).then_inc(rel_ready, 1)
                nc.vector.tensor_copy(rel_parts[:, :, 7, :], rb).then_inc(rel_ready, 1)
                v.wait_ge(rel_ready, 1)
                nc.vector.tensor_copy(rel_parts[:, :, 6, :], rc).then_inc(rel_ready, 1)
                moments(2)
                moments(3)
                v.wait_ge(var_ready, 4)

            @block.tensor
            def _(pe):
                pe.wait_ge(consts, 8)
                pe.wait_ge(abs_done, 1)
                nc.tensor.matmul(net.bank[7][:, 0:2], ones_f[:, :], w_abs[:, :], start=True, stop=True).then_inc(mean_done, 1)
                pe.wait_ge(att_loaded, 128)
                for m in range(8):
                    if m >= 4:
                        pe.wait_ge(att_copied, m - 3)
                    for c in range(C):
                        for o in range(C):
                            i = nc.tensor.transpose(net.bank[m % 4][:, (c * C + o) * P:(c * C + o + 1) * P],
                                                    raw[:, m, o, c * P:(c + 1) * P], net.id_f[:, :])
                    i.then_inc(att_done, 1)
                pe.wait_ge(w12_quantised, 2)
                pe.wait_ge(dve, 1)
                for n in range(4):
                    dst = net.bank[4 + n][:, :].bitcast(BF16)
                    for c in range(HC):
                        if n < 2:
                            src = w_q[:, 0, c * D + n * P:c * D + (n + 1) * P]
                        else:
                            src = w_q[:, 1, (n - 2) * HID + c * P:(n - 2) * HID + (c + 1) * P]
                        i = nc.tensor.transpose(dst[:, c * P:(c + 1) * P], src, net.id_b[:, :])
                    i.then_inc(w12_done, 1)
                pe.wait_ge(att_copied, 8)
                pe.wait_ge(rel_ready, 6)
                for c in range(2):
                    i = nc.tensor.transpose(net.bank[1][0:ROWS, 0:P].bitcast(BF16)[:, c * P:(c + 1) * P],
                                            rel_parts[:, c, :, :].rearrange("p n d -> p (n d)"), net.id_b[:, :])
                i.then_inc(rel_done, 1)
                pe.wait_ge(small_loaded, 80)
                pe.wait_ge(bias_ordered, 1)
                for o in range(C):
                    i = nc.tensor.transpose(net.bank[0][:, 4 * o:4 * o + 4], bias_apart[:, o, :], net.id_f[0:4, 0:4])
                i.then_inc(bias_done, 1)
        sem.release()


def project(nc, net, layer, with_context, ins):
    tag = f"p{layer}"
    pairs = net.nb // 2
    jobs = [(4 * layer, 2 * layer, net.q_scr[layer], (0, 1, 2))]
    if with_context:
        jobs += [(1, 1, net.k_scr[0], (2, 1, 0)), (5, 3, net.k_scr[1], (2, 1, 0))]
    nj = len(jobs)
    values = [(2, 0, net.v_scr[0]), (6, 2, net.v_scr[1])] if with_context else []
    with ExitStack() as ctx:
        def sb(name, shape, dt=F32):
            return ctx.enter_context(nc.sbuf_tensor(f"{tag}_{name}", shape, dt))

        sem = Semaphores(nc, tag)

        normed = sb("normed", [P, 2, 2, D])
        ctx_in = sb("ctx_in", [P, 2, 2, D])
        xT = sb("xT", [P, 2, C, 2 * P])
        cT = sb("cT", [P, 2, C, 2 * P])
        parts = [sb(f"parts{j}", [P, 2, PARTS, C * 2 * P], BF16) for j in range(nj)]
        rest = [sb(f"rest{j}", [P, 2, C * 2 * P]) for j in range(nj)]
        val = [sb(f"val{j}", [P, 2, 2 * H, DK]) for j in range(len(values))]
        val_parts = [sb(f"val_parts{j}", [P, 2, 2 * H, PARTS, VW], BF16) for j in range(len(values))]

        ctx_loaded = [sem(f"ctx_loaded{i}") for i in range(2)]
        normed_ready = sem("normed_ready")
        xT_done = sem("xT_done")
        cT_done = sem("cT_done")
        xT_copied = sem("xT_copied")
        cT_copied = sem("cT_copied")
        proj_done = [sem(f"proj_done{j}") for j in range(nj)]
        val_done = [sem(f"val_done{j}") for j in range(len(values))]
        part_a = [sem(f"part_a{j}") for j in range(nj)]
        rest1 = [sem(f"rest1_{j}") for j in range(nj)]
        part_b = [sem(f"part_b{j}") for j in range(nj)]
        part_c = [sem(f"part_c{j}") for j in range(nj)]
        val_read = [sem(f"val_read{j}") for j in range(len(values))]
        val_rest = [sem(f"val_rest{j}") for j in range(len(values))]
        val_b = [sem(f"val_b{j}") for j in range(len(values))]
        val_c = [sem(f"val_c{j}") for j in range(len(values))]
        val_stored = [sem(f"val_stored{i}") for i in range(2)]
        ones = sem("ones")
        slices = sem("slices")
        stored = [sem(f"stored{i}") for i in range(2)]
        per_store = 16 * nj
        bank_x, bank_c = net.bank[0], net.bank[1]
        both = not with_context
        bank_j = [[net.bank[2 + j], net.bank[3 if both else 2 + j]] for j in range(nj)]
        bank_v = net.bank[5:7]

        with nc.Block() as block:
            @block.sync
            def _(sp):
                def load(p, u):
                    sp.dma_start(ctx_in[:, u, :, :], ins["ctx_1024"].rearrange("(n b) p d -> n p b d", b=2)[bass.ds(p, 1)]
                                 .rearrange("n p b d -> p (n b) d")).then_inc(ctx_loaded[u], 16)

                def store(p, u):
                    for j, (_, _, scr, _) in enumerate(jobs):
                        sp.wait_ge(part_c[j], p + 1)
                        sp.wait_ge(part_b[j], p + 1)
                        sp.dma_start(scr.rearrange("n k p t -> n p k t")[bass.ds(p, 1)].rearrange("n p k t -> p (n k) t"),
                                     parts[j][:, u, :, :]).then_inc(stored[u], 16)

                def store_values(p, u):
                    for j, (_, _, scr) in enumerate(values):
                        sp.wait_ge(val_c[j], p + 1)
                        sp.dma_start(scr[bass.ds(p, 1)].rearrange("n p t -> p (n t)"),
                                     val_parts[j][:, u, :, :, :].rearrange("p h n w -> p (h n w)")).then_inc(val_stored[u], 16)

                if with_context:
                    load(0, 0)
                    load(1, 1)

                def work(p, u):
                    if not (isinstance(p, int) and p == 0):
                        store_values(p - 1, 1 - u)
                    if with_context and not (isinstance(p, int) and p >= pairs - 2):
                        sp.wait_ge(cT_done, p + 1)
                        load(p + 2, u)
                    store(p, u)

                for u in range(2):
                    work(u, u)
                with sp.Fori(1, pairs // 2 - 1) as t:
                    for u in range(2):
                        work(2 * t + u, u)
                for u in range(2):
                    work(pairs - 2 + u, u)
                store_values(pairs - 1, 1)
                for u in range(2):
                    sp.wait_ge(stored[u], per_store * (pairs // 2))
                    if values:
                        sp.wait_ge(val_stored[u], 16 * len(values) * (pairs // 2))

            @block.vector
            def _(v):
                def norm(p, u, first):
                    if not first:
                        v.wait_ge(xT_done, p - 1)
                    for s in range(2):
                        i = nc.vector.tensor_scalar(normed[:, u, s, :], at(net.x, 2 * p + s), at(net.moments[:, :, 0:1], 2 * p + s),
                                                    at(net.rstd, 2 * p + s), ALU.subtract, ALU.mult)
                    i.then_inc(normed_ready, 1)

                def largest(p):
                    if isinstance(p, int) and p == 0:
                        v.wait_ge(net.ups_loaded, 16 * (PIECES + C))
                        v.wait_ge(net.moe_loaded, 64)
                    for weights, size, largest_of in ((net.w_pieces, PIECES * 512, net.piece_max), (net.down, (NE + C) * D, net.down_max)):
                        every = weights[:, :, :].rearrange("p n w -> p (n w)").rearrange("p (n w) -> p n w", w=size // pairs)
                        nc.vector.tensor_reduce(at(largest_of, p), at(every, p), X, ALU.max, apply_absolute_value=True).then_inc(slices, 1)

                def work(p, u, first, t):
                    if not (isinstance(p, int) and p == 0):
                        value_part_c(p - 1, 1 - u)
                    if with_context:
                        largest(p)
                    for j, (_, bias, _, _) in enumerate(jobs):
                        v.wait_ge(part_a[j], p + 1)
                        if not first:
                            v.wait_ge(part_c[j], p - 1)
                        for o in range(C):
                            s = slice(o * 2 * P, (o + 1) * 2 * P)
                            i = nc.vector.scalar_tensor_tensor(
                                out=rest[j][:, u, s], in0=bank_j[j][u][:, s], scalar=net.bias_col[:, o, bias:bias + 1],
                                in1=parts[j][:, u, jobs[j][3].index(0), s], op0=ALU.add, op1=ALU.subtract)
                        i.then_inc(rest1[j], 1)
                        if both:
                            v.wait_ge(rest1[j], p + 1)
                            if not first:
                                v.wait_ge(stored[u], per_store * t)
                            nc.vector.tensor_copy(parts[j][:, u, jobs[j][3].index(1), :], rest[j][:, u, :]).then_inc(part_b[j], 1)
                    for j, (_, bias, _) in enumerate(values):
                        v.wait_ge(val_done[j], p + 1)
                        if not first:
                            v.wait_ge(val_stored[u], 16 * len(values) * t)
                        product = bank_v[j][:, :].rearrange("p (b h w) -> p b h w", b=2, w=DK)
                        row = net.bias_row[:, bias, :].rearrange("p (h w) -> p h w", w=DK).unsqueeze(1).to_broadcast([P, 2, H, DK])
                        nc.vector.tensor_tensor(val[j][:, u, :, :].rearrange("p (b h) w -> p b h w", b=2), product, row,
                                                ALU.add).then_inc(val_read[j], 1)
                        nc.vector.tensor_tensor(val_parts[j][:, u, :, 0, 0:DK].rearrange("p (b h) w -> p b h w", b=2), product, row,
                                                ALU.add).then_inc(val_read[j], 1)
                    for j in range(len(values)):
                        v.wait_ge(val_read[j], 2 * p + 2)
                        nc.vector.tensor_tensor(val[j][:, u, :, :], val[j][:, u, :, :], val_parts[j][:, u, :, 0, 0:DK],
                                                ALU.subtract).then_inc(val_rest[j], 1)

                def value_part_c(p, u):
                    for j in range(len(values)):
                        v.wait_ge(val_b[j], p + 1)
                        nc.vector.tensor_tensor(val_parts[j][:, u, :, 2, 0:DK], val[j][:, u, :, :], val_parts[j][:, u, :, 1, 0:DK],
                                                ALU.subtract).then_inc(val_c[j], 1)

                for j in range(len(values)):
                    for u in range(2):
                        nc.vector.memset(val_parts[j][:, u, :, :, DK:VW], 0.0).then_inc(ones, 1)
                for j in range(len(values)):
                    for u in range(2):
                        v.wait_ge(ones, 2 * len(values))
                        nc.vector.memset(val_parts[j][:, u, :, 0, DK:VW], 1.0).then_inc(ones, 1)
                if values:
                    v.wait_ge(ones, 4 * len(values))
                norm(0, 0, True)
                norm(1, 1, True)
                for u in range(2):
                    norm(2 + u, u, False)
                    work(u, u, True, 0)
                with v.Fori(1, pairs // 2 - 1) as t:
                    for u in range(2):
                        norm(2 * t + u + 2, u, False)
                        work(2 * t + u, u, False, t)
                for u in range(2):
                    work(pairs - 2 + u, u, False, pairs // 2 - 1)
                value_part_c(pairs - 1, 1)
                if with_context:
                    v.wait_ge(slices, 2 * pairs)

            @block.scalar
            def _(act):
                def value_part_b(p, u):
                    for j in range(len(values)):
                        act.wait_ge(val_rest[j], p + 1)
                        nc.scalar.activation(val_parts[j][:, u, :, 1, 0:DK], val[j][:, u, :, :], ACT.Copy).then_inc(val_b[j], 1)

                def copies(p, u):
                    act.wait_ge(xT_done, p + 1)
                    ge(act, proj_done[0], p - 1)
                    nc.scalar.activation(xT[:, u, :, :].rearrange("p c t -> p (c t)"), bank_x[:, :], ACT.Copy).then_inc(xT_copied, 1)
                    if with_context:
                        act.wait_ge(cT_done, p + 1)
                        ge(act, val_done[1], p - 1)
                        nc.scalar.activation(cT[:, u, :, :].rearrange("p c t -> p (c t)"), bank_c[:, :], ACT.Copy).then_inc(cT_copied, 1)

                def work(p, u, first, t):
                    if not (isinstance(p, int) and p == pairs - 1):
                        copies(p + 1, 1 - u)
                    if not (isinstance(p, int) and p == 0):
                        value_part_b(p - 1, 1 - u)
                    if not first:
                        act.wait_ge(stored[u], per_store * t)
                    for j, (_, bias, _, order) in enumerate(jobs):
                        act.wait_ge(proj_done[j], p + 1)
                        for o in range(C):
                            s = slice(o * 2 * P, (o + 1) * 2 * P)
                            i = nc.scalar.activation(parts[j][:, u, order.index(0), s], bank_j[j][u][:, s], ACT.Identity,
                                                     bias=net.bias_col[:, o, bias:bias + 1])
                        i.then_inc(part_a[j], 1)

                copies(0, 0)
                for u in range(2):
                    work(u, u, True, 0)
                with act.Fori(1, pairs // 2 - 1) as t:
                    for u in range(2):
                        work(2 * t + u, u, False, t)
                for u in range(2):
                    work(pairs - 2 + u, u, False, pairs // 2 - 1)
                value_part_b(pairs - 1, 1)

            @block.gpsimd
            def _(pool):
                def work(p, u, first, t):
                    for j, (_, _, _, order) in enumerate(jobs):
                        if not both:
                            ge(pool, rest1[j], p + 1)
                            if not first:
                                apart(pool, stored[u], per_store * t)
                            nc.gpsimd.tensor_copy(parts[j][:, u, order.index(1), :], rest[j][:, u, :]).then_inc(part_b[j], 1)
                        pool.wait_ge(part_b[j], p + 1)
                        nc.gpsimd.tensor_tensor(parts[j][:, u, order.index(2), :], rest[j][:, u, :],
                                                parts[j][:, u, order.index(1), :], ALU.subtract).then_inc(part_c[j], 1)

                for u in range(2):
                    work(u, u, True, 0)
                with pool.Fori(1, pairs // 2) as t:
                    for u in range(2):
                        work(2 * t + u, u, False, t)

            @block.tensor
            def _(pe):
                def turn(p, u, first, loads):
                    pe.wait_ge(normed_ready, p + 1)
                    if not first:
                        pe.wait_ge(xT_copied, p)
                    for c in range(C):
                        for s in range(2):
                            i = nc.tensor.transpose(bank_x[:, (c * 2 + s) * P:(c * 2 + s + 1) * P],
                                                    normed[:, u, s, c * P:(c + 1) * P], net.id_f[:, :])
                    i.then_inc(xT_done, 1)
                    if with_context:
                        if not first:
                            pe.wait_ge(cT_copied, p)
                        pe.wait_ge(ctx_loaded[u], 16 * loads)
                        for c in range(C):
                            for s in range(2):
                                i = nc.tensor.transpose(bank_c[:, (c * 2 + s) * P:(c * 2 + s + 1) * P],
                                                        ctx_in[:, u, s, c * P:(c + 1) * P], net.id_f[:, :])
                        i.then_inc(cT_done, 1)

                def products(p, u, first):
                    pe.wait_ge(xT_copied, p + 1)
                    for j, (m, _, _, _) in enumerate(jobs):
                        src = xT if j == 0 else cT
                        if j == 1:
                            pe.wait_ge(cT_copied, p + 1)
                        ge(pe, rest1[j], p - both)
                        for o in range(C):
                            for c in range(C):
                                i = nc.tensor.matmul(bank_j[j][u][:, o * 2 * P:(o + 1) * 2 * P], net.wT[:, m, c, o * P:(o + 1) * P],
                                                     src[:, u, c, :], start=(c == 0), stop=(c == C - 1))
                        i.then_inc(proj_done[j], 1)
                    for j, (m, _, _) in enumerate(values):
                        if not first:
                            pe.wait_ge(val_read[j], 2 * p)
                        for s in range(2):
                            for c in range(C):
                                i = nc.tensor.matmul(bank_v[j][:, s * D:(s + 1) * D], cT[:, u, c, s * P:(s + 1) * P],
                                                     net.wT[:, m, c, :], start=(c == 0), stop=(c == C - 1))
                        i.then_inc(val_done[j], 1)

                turn(0, 0, True, 1)
                turn(1, 1, False, 1)
                products(0, 0, True)
                turn(2, 0, False, 2)
                products(1, 1, False)
                with pe.Fori(1, pairs // 2 - 1) as t:
                    turn(2 * t + 1, 1, False, t + 1)
                    products(2 * t, 0, False)
                    turn(2 * t + 2, 0, False, t + 2)
                    products(2 * t + 1, 1, False)
                turn(pairs - 1, 1, False, pairs // 2)
                products(pairs - 2, 0, False)
                products(pairs - 1, 1, False)
        sem.release()


def pipeline(engine, nb, slot):
    groups = nb // 4
    for u in range(4):
        slot(u, u, 0)
    with engine.Fori(1, groups - 1) as t:
        for u in range(4):
            slot(4 * t + u, u, t)
    for u in range(4):
        slot(nb - 4 + u, u, groups - 1)
    for u in range(2):
        slot(nb + u, u, groups)


def ge(engine, semaphore, value):
    if not (isinstance(value, int) and value <= 0):
        engine.wait_ge(semaphore, value)


def apart(engine, semaphore, value):
    ge(engine, semaphore, value)
    if not isinstance(value, int):
        engine.nop(nofuse=True)


def attend(nc, net, layer):
    tag = f"a{layer}"
    nb = net.nb
    pos = layer == 1
    m_out = 4 * layer + 3
    with ExitStack() as ctx:
        def sb(name, shape, dt=F32):
            return ctx.enter_context(nc.sbuf_tensor(f"{tag}_{name}", shape, dt))

        sem = Semaphores(nc, tag)

        qr = sb("q_rows", [ROWS, 2, H, 2, P], BF16)
        kr = sb("k_rows", [ROWS, 2, H, 2, P], BF16)
        val = sb("values", [P, 2, 2, H, PARTS, VW], BF16)
        probs = sb("probs", [P, H, P])
        high = sb("probs_high", [P, 2, H, P], F16)
        low = sb("probs_low", [P, 2, H, P], F16)
        neg_max = sb("neg_max", [P, 2, H])
        neg_rest = sb("neg_rest", [P, H])
        neg_parts = sb("neg_parts", [P, 2, PARTS, H], BF16)
        neg_rows = sb("neg_rows", [PARTS * H, 2, P], BF16)
        sums = sb("recip_sums", [P, H])
        attn = sb("attn", [P, D])
        attnT = sb("attnT", [P, C, P])
        x_bias = sb("x_bias", [P, 2, D])
        stats = sb("stats", [P, 6])
        agg = sb("agg", [P, 2])
        if pos:
            pos_T = sb("pos_T", [P, 2, P, 2 * H])
            s_T = sb("scores_T", [P, 2, H, P])

        qk_loaded = [sem(f"qk_loaded{g}") for g in range(2)]
        v_loaded = [sem(f"v_loaded{g}") for g in range(2)]
        scores_done = sem("scores_done")
        added = sem("added")
        turned = sem("turned")
        max_done = sem("max_done")
        neg_step = sem("neg_step")
        neg_ready = sem("neg_ready")
        rows_done = sem("rows_done")
        rows_copied = sem("rows_copied")
        shifted = sem("shifted")
        z_ready = sem("z_ready")
        probs_ready = sem("probs_ready")
        high_ready = sem("high_ready")
        low_ready = {e: sem(f"low_ready_{e}") for e in ("v", "pool")}
        pv_done = sem("pv_done")
        recip = sem("recip")
        attn_ready = sem("attn_ready")
        attnT_done = sem("attnT_done")
        attnT_copied = sem("attnT_copied")
        out_done = sem("out_done")
        x_biased = sem("x_biased")
        x_added = sem("x_added")
        ln = sem("ln")
        stats_ready = sem("stats_ready")
        final = sem("final")
        pos_done = sem("pos_done")
        pos_copied = sem("pos_copied")

        bank_s = net.bank[0:2] * 2 if pos else net.bank[0:2] + [net.bank[5], net.bank[0]]
        s_back = (2, 2, 2, 2) if pos else (1, 4, 4, 3)
        bank_t = net.bank[2:4]
        bank_pv = net.bank[4]
        bank_turn = net.bank[5]
        bank_pos = net.bank[6:8]
        bank_misc = net.bank[4 if pos else 7]
        rows_ps = net.bank[7 if pos else 6][0:PARTS * H, D:D + P // 2].bitcast(BF16)
        LOW = ("pool", "pool", "v", "v") if not pos else ("pool",) * QUADS

        def low_waits(engine, n, q):
            ge(engine, low_ready[LOW[q]], LOW.count(LOW[q]) * n + LOW[:q].count(LOW[q]) + 1)

        def make_low(namespace, engine, m, u, q):
            ge(engine, high_ready, 4 * m + q + 1)
            if q == 0 or LOW[q] not in LOW[:q]:
                ge(engine, pv_done, m - 1)
            z = slice(4 * q, 4 * q + 4)
            namespace.tensor_tensor(low[:, (u - 1) % 2, z, :], probs[:, z, :], high[:, (u - 1) % 2, z, :],
                                    ALU.subtract).then_inc(low_ready[LOW[q]], 1)
        QK_LOADS = 8 * 16
        FILLS = 8
        fill = P // FILLS

        with nc.Block() as block:
            @block.sync
            def _(sp):
                def load(p, g, first):
                    if not first:
                        sp.wait_ge(scores_done if pos else shifted, 8 * p - 8)
                    for r0, n, q_lo, k_lo in ((0, 3, 0, 0), (3, 2, 0, 1), (5, 1, 0, 2), (6, 2, 1, 0)):
                        for dst, scr, lo in ((qr, net.q_scr[layer], q_lo), (kr, net.k_scr[layer], k_lo)):
                            sp.dma_start(
                                dst[r0 * DK:(r0 + n) * DK, g, :, :, :].rearrange("r h b t -> r (h b t)"),
                                scr.rearrange("n k (d h) t -> n (k d) (h t)", d=DK)[bass.ds(p, 1), lo * DK:(lo + n) * DK, :]
                                .rearrange("n r t -> (n r) t")).then_inc(qk_loaded[g], 16)
                    if not first:
                        sp.wait_ge(pv_done, 2 * p - 2)
                    sp.dma_start(val[:, g, :, :, :, :].rearrange("p b h n w -> p (b h n w)"),
                                 net.v_scr[layer][bass.ds(p, 1)].rearrange("n p t -> (n p) t")).then_inc(v_loaded[g], 16)

                for g in range(2):
                    load(g, g, True)
                with sp.Fori(1, nb // 4) as t:
                    for g in range(2):
                        load(2 * t + g, g, False)

            def fills(k, u, t, do_s):
                if not pos or not do_s or isinstance(k, int) and k >= nb - 2:
                    return {}
                pair, g, loads = (2 * t + 1, 1, t + 1) if u < 2 else (2 * t + 2, 0, t + 2)
                places = "BCDE" if u % 2 == 0 else "ABCD"
                first = 4 * (u % 2)
                return {place: (pair, g, first + i, loads) for i, place in enumerate(places)}

            def some(plan, place, make):
                if place in plan:
                    make(*plan[place])

            def late(k):
                return not isinstance(k, int) or k >= 3

            def active(k, u, t):
                static = isinstance(k, int)
                return (not static or k < nb, not static or 1 <= k <= nb, not static or k >= 2)

            @block.tensor
            def _(pe):
                def scores(k, u, q):
                    g, b = u // 2, u % 2
                    ge(pe, added if pos else max_done, 4 * k + q - s_back[q] + 1)
                    for n in range(4):
                        h = 4 * q + n
                        a, o = (kr, qr) if pos else (qr, kr)
                        i = nc.tensor.matmul(bank_s[q][:, n * P:(n + 1) * P], a[0:ROWS, g, h, b, :], o[0:ROWS, g, h, b, :],
                                             start=True, stop=True)
                    i.then_inc(scores_done, 1)

                def turn(k, u, q):
                    pe.wait_ge(added, 4 * k + q + 1)
                    ge(pe, max_done, 4 * k + q)
                    for n in range(4):
                        i = nc.tensor.transpose(bank_turn[:, n * P:(n + 1) * P], s_T[:, u % 2, 4 * q + n, :], net.id_f[:, :])
                    i.then_inc(turned, 1)

                def cross(m, u, t):
                    pe.wait_ge(neg_ready, m + 1)
                    if pos:
                        if isinstance(m, int) and m >= nb - 2:
                            pe.wait_ge(pos_copied, FILLS * nb // 2)
                        else:
                            pe.wait_ge(pos_copied, FILLS * (2 * t + u // 2 + 1) + FILLS // 2 * (u % 2))
                    apart(pe, rows_copied, m)
                    nc.tensor.transpose(rows_ps, neg_parts[:, (u - 1) % 2, :, :].rearrange("p n h -> p (n h)"), net.id_b[:, :]).then_inc(rows_done, 1)

                def shift(m, u, q):
                    g, b = ((u - 1) % 4) // 2, (u - 1) % 2
                    if q == 0:
                        pe.wait_ge(rows_copied, m + 1)
                    ge(pe, z_ready if pos else high_ready, 4 * m + q - 1)
                    for n in range(4):
                        h = 4 * q + n
                        dst = bank_t[q % 2][:, n * P:(n + 1) * P]
                        if not pos:
                            nc.tensor.matmul(dst, kr[0:ROWS, g, h, b, :], qr[0:ROWS, g, h, b, :], start=True, stop=False)
                        i = nc.tensor.matmul(dst, net.pick[:, h, :], neg_rows[:, b, :], start=pos, stop=True)
                    i.then_inc(shifted, 1)

                def weigh(n, u, t, quads):
                    g, b = ((u - 2) % 4) // 2, u % 2
                    if 0 in quads:
                        pe.wait_ge(v_loaded[g], 16 * (t + 1 if u >= 2 else t))
                        ge(pe, x_added if pos else attn_ready, n)
                    for q in quads:
                        pe.wait_ge(high_ready, 4 * n + q + 1)
                        low_waits(pe, n, q)
                        for j in range(4):
                            h = 4 * q + j
                            pairs = [(high, c) for c in range(PARTS)] + [(low, c) for c in range(2)]
                            for w, (half, c) in enumerate(pairs):
                                i = nc.tensor.matmul(bank_pv[:, h * VW:(h + 1) * VW], half[:, b, h, :], val[:, g, b, h, c, :],
                                                     start=(w == 0), stop=(w == len(pairs) - 1))
                    if QUADS - 1 in quads:
                        i.then_inc(pv_done, 1)

                def attention_turned(n):
                    pe.wait_ge(attn_ready, n + 1)
                    ge(pe, x_added, n)
                    for c in range(C):
                        i = nc.tensor.transpose(bank_misc[:, c * P:(c + 1) * P], attn[:, c * P:(c + 1) * P], net.id_f[:, :])
                    i.then_inc(attnT_done, 1)

                def output(n):
                    pe.wait_ge(attnT_copied, n + 1)
                    for c in range(C):
                        i = nc.tensor.matmul(bank_misc[:, 0:D], attnT[:, c, :], net.wT[:, m_out, c, :], start=(c == 0), stop=(c == C - 1))
                    i.then_inc(out_done, 1)

                def positions(p, g, f):
                    ge(pe, pos_copied, FILLS * p + f - 1)
                    for n in range(fill):
                        i0 = f * fill + n
                        i = nc.tensor.matmul(bank_pos[f % 2][:, n * 2 * H:(n + 1) * 2 * H], net.rel[0:ROWS, P - 1 - i0:2 * P - 1 - i0],
                                             qr[0:ROWS, g, :, :, i0],
                                             start=True, stop=True)
                    i.then_inc(pos_done, 1)

                def slot(k, u, t):
                    do_s, do_e, do_o = active(k, u, t)
                    m, n = k - 1, k - 2
                    plan = fills(k, u, t, do_s)
                    if do_s:
                        if u % 2 == 0:
                            pe.wait_ge(qk_loaded[u // 2], QK_LOADS * (t + 1))
                        scores(k, u, 0)
                        scores(k, u, 1)
                    if pos:
                        if do_s:
                            turn(k, u, 0)
                            scores(k, u, 2)
                        if do_e:
                            cross(m, u, t)
                        if do_o:
                            weigh(n, u, t, (0, 1))
                        if do_s:
                            turn(k, u, 1)
                        if do_e:
                            pe.wait_ge(rows_copied, m + 1)
                        some(plan, "A", load_and_fill)
                        if do_e:
                            shift(m, u, 0)
                        if do_o:
                            weigh(n, u, t, (2, 3))
                        if do_s:
                            scores(k, u, 3)
                        some(plan, "B", load_and_fill)
                        if do_e:
                            shift(m, u, 1)
                        if do_o:
                            attention_turned(n)
                        if do_s:
                            turn(k, u, 2)
                        some(plan, "C", load_and_fill)
                        if do_e:
                            shift(m, u, 2)
                        if do_s:
                            turn(k, u, 3)
                        some(plan, "D", load_and_fill)
                        if do_e:
                            shift(m, u, 3)
                        if do_o:
                            output(n)
                        some(plan, "E", load_and_fill)
                    else:
                        if do_e:
                            cross(m, u, t)
                        if do_s:
                            scores(k, u, 2)
                            scores(k, u, 3)
                        if do_e:
                            shift(m, u, 0)
                        if late(k):
                            output(n - 1)
                        if do_e:
                            shift(m, u, 1)
                        if do_o:
                            weigh(n, u, t, (0, 1))
                        if do_e:
                            shift(m, u, 2)
                        if do_o:
                            weigh(n, u, t, (2, 3))
                        if do_e:
                            shift(m, u, 3)
                        if do_o:
                            attention_turned(n)

                def load_and_fill(p, g, f, loads):
                    pe.wait_ge(qk_loaded[g], QK_LOADS * loads)
                    positions(p, g, f)

                if pos:
                    pe.wait_ge(qk_loaded[0], QK_LOADS)
                    for f in range(FILLS):
                        positions(0, 0, f)
                pipeline(pe, nb, slot)
                if not pos:
                    output(nb - 1)

            @block.scalar
            def _(act):
                def copy_positions(p, g, f):
                    act.wait_ge(pos_done, FILLS * p + f + 1)
                    if f == 0:
                        ge(act, added, 8 * p - 8)
                    nc.scalar.activation(pos_T[:, g, f * fill:(f + 1) * fill, :].rearrange("p i n -> p (i n)"), bank_pos[f % 2][:, :],
                                         ACT.Copy).then_inc(pos_copied, 1)

                def exponential(m, u, q):
                    b = (u - 1) % 2
                    act.wait_ge(z_ready if pos else shifted, 4 * m + q + 1)
                    if q == 0:
                        ge(act, pv_done, m - 1)
                    low_waits_before(act, m, q)
                    z = slice(4 * q, 4 * q + 4)
                    src = s_T[:, b, z, :].rearrange("p h t -> p (h t)") if pos else bank_t[q % 2][:, :]
                    nc.scalar.activation(probs[:, z, :].rearrange("p h t -> p (h t)"), src, ACT.Exp,
                                         bias=net.prob_bias[:, :]).then_inc(probs_ready, 1)
                    nc.scalar.activation(high[:, b, z, :].rearrange("p h t -> p (h t)"), src, ACT.Exp,
                                         bias=net.prob_bias[:, :]).then_inc(high_ready, 1)

                def low_waits_before(engine, m, q):
                    if not (isinstance(m, int) and m == 0):
                        low_waits(engine, m - 1, q)

                def slot(k, u, t):
                    do_s, do_e, do_o = active(k, u, t)
                    m, n = k - 1, k - 2
                    plan = fills(k, u, t, do_s)

                    def copy(p, g, f, loads):
                        copy_positions(p, g, f)

                    if do_e:
                        act.wait_ge(rows_done, m + 1)
                        ge(act, shifted, 4 * m - 4)
                        nc.scalar.activation(neg_rows[:, (u - 1) % 2, :], rows_ps, ACT.Copy).then_inc(rows_copied, 1)
                    some(plan, "A", copy)
                    if do_e:
                        exponential(m, u, 0)
                        if not pos:
                            exponential(m, u, 1)
                            exponential(m, u, 2)
                            exponential(m, u, 3)
                    some(plan, "B", copy)
                    if do_o:
                        act.wait_ge(attnT_done, n + 1)
                        ge(act, out_done, n)
                        nc.scalar.activation(attnT[:, :, :].rearrange("p c t -> p (c t)"), bank_misc[:, 0:D], ACT.Copy).then_inc(attnT_copied, 1)
                    if do_e and pos:
                        exponential(m, u, 1)
                    some(plan, "C", copy)
                    if do_e and pos:
                        exponential(m, u, 2)
                    some(plan, "D", copy)
                    if do_e and pos:
                        exponential(m, u, 3)
                    some(plan, "E", copy)

                if pos:
                    for f in range(FILLS):
                        copy_positions(0, 0, f)
                pipeline(act, nb, slot)

            @block.gpsimd
            def _(pool):
                def deviation(n):
                    pool.wait_ge(stats_ready, n + 1)
                    nc.gpsimd.tensor_tensor(at(net.var_eps, n), at(net.moments[:, :, 1:2], n), net.eps[:, :], ALU.add).then_inc(final, 1)
                    pool.wait_ge(final, 2 * n + 1)
                    nc.gpsimd.tensor_tensor(at(net.rstd, n), at(net.var_eps, n), net.minus_half[:, 0, :], ALU.pow).then_inc(final, 1)

                def negative_parts(k, u):
                    b = u % 2
                    a, bb, c = (neg_parts[:, b, n, :] for n in range(PARTS))
                    pool.wait_ge(max_done, 4 * k + 4)
                    apart(pool, rows_done, k - 1)
                    nc.gpsimd.tensor_copy(a, neg_max[:, b, :]).then_inc(neg_step, 1)
                    pool.wait_ge(neg_step, 3 * k + 1)
                    nc.gpsimd.tensor_tensor(neg_rest[:, :], neg_max[:, b, :], a, ALU.subtract).then_inc(neg_step, 1)
                    apart(pool, neg_step, 3 * k + 2)
                    nc.gpsimd.tensor_copy(bb, neg_rest[:, :]).then_inc(neg_step, 1)
                    pool.wait_ge(neg_step, 3 * k + 3)
                    nc.gpsimd.tensor_tensor(c, neg_rest[:, :], bb, ALU.subtract).then_inc(neg_ready, 1)

                def slot(k, u, t):
                    do_s, do_e, do_o = active(k, u, t)
                    if do_o:
                        n = k - 2
                        ge(pool, x_added, n - 1)
                        nc.gpsimd.tensor_tensor(x_bias[:, u % 2, :], at(net.x, n), net.bias_row[:, 2 * layer + 1, :], ALU.add).then_inc(x_biased, 1)
                    for q in range(QUADS):
                        if do_s and q == (1 if pos else 2):
                            negative_parts(k, u)
                        if do_e and LOW[q] == "pool":
                            make_low(nc.gpsimd, pool, k - 1, u, q)
                    if not isinstance(k, int) or k >= 4:
                        deviation(k - 4)

                pipeline(pool, nb, slot)
                deviation(nb - 2)
                deviation(nb - 1)
                pool.wait_ge(final, 2 * nb)

            @block.vector
            def _(v):
                def quad(ap, q):
                    return ap[:, 4 * q:4 * q + 4, :]

                def maximum(k, u, q):
                    v.wait_ge(turned if pos else scores_done, 4 * k + q + 1)
                    if q == 0:
                        ge(v, neg_ready, k - 1)
                    src = (bank_turn if pos else bank_s[q])[:, :].rearrange("p (h t) -> p h t", h=4)
                    nc.vector.tensor_reduce(neg_max[:, u % 2, 4 * q:4 * q + 4], src, X, ALU.max, negate=True).then_inc(max_done, 1)

                def add_positions(k, u, q, pair):
                    v.wait_ge(scores_done, 4 * k + q + 1)
                    ge(v, high_ready, 4 * k + q - 7)
                    if q == 0:
                        v.wait_ge(pos_copied, FILLS * (pair + 1))
                    nc.vector.tensor_tensor(quad(s_T[:, u % 2, :, :], q), bank_s[q][:, :].rearrange("p (h t) -> p h t", h=4),
                                            pos_T[:, u // 2, :, :].rearrange("p i (h b) -> p b h i", b=2)[:, u % 2, 4 * q:4 * q + 4, :],
                                            ALU.add).then_inc(added, 1)

                def add_shift(m, u, q):
                    b = (u - 1) % 2
                    v.wait_ge(shifted, 4 * m + q + 1)
                    z = quad(s_T[:, b, :, :], q)
                    nc.vector.tensor_tensor(z, bank_t[q % 2][:, :].rearrange("p (h t) -> p h t", h=4), z, ALU.add).then_inc(z_ready, 1)

                def normalise(n):
                    v.wait_ge(pv_done, n + 1)
                    out = bank_pv[:, 0:H * VW].rearrange("p (h w) -> p h w", w=VW)
                    nc.vector.reciprocal(sums[:, :], out[:, :, DK]).then_inc(recip, 1)
                    v.wait_ge(recip, n + 1)
                    ge(v, attnT_done, n)
                    nc.vector.tensor_tensor(attn[:, :].rearrange("p (h w) -> p h w", w=DK), out[:, :, 0:DK],
                                            sums[:, :].unsqueeze(2).to_broadcast([P, H, DK]), ALU.mult).then_inc(attn_ready, 1)

                def add_output(n, u):
                    v.wait_ge(out_done, n + 1)
                    v.wait_ge(x_biased, n + 1)
                    nc.vector.tensor_tensor(at(net.x, n), bank_misc[:, 0:D], x_bias[:, u % 2, :], ALU.add).then_inc(x_added, 1)

                def statistics(n):
                    apart(v, x_added, n + 1)
                    nc.vector.bn_stats(stats[:, :], at(net.x, n)).then_inc(ln, 1)

                def moments(n):
                    apart(v, ln, 2 * n + 1)
                    nc.vector.bn_aggr(agg[:, :], stats[:, :]).then_inc(ln, 1)

                def keep_moments(n):
                    apart(v, ln, 2 * n + 2)
                    nc.vector.tensor_copy(at(net.moments, n), agg[:, :]).then_inc(stats_ready, 1)

                def slot(k, u, t):
                    do_s, do_e, do_o = active(k, u, t)
                    m, n = k - 1, k - 2
                    if pos:
                        pair = 2 * t + u // 2
                        if do_s:
                            add_positions(k, u, 0, pair)
                            add_positions(k, u, 1, pair)
                        if late(k):
                            add_output(n - 1, u - 1)
                        if do_s:
                            maximum(k, u, 0)
                        if late(k):
                            statistics(n - 1)
                        if do_s:
                            add_positions(k, u, 2, pair)
                            maximum(k, u, 1)
                        if late(k):
                            moments(n - 1)
                        if do_e:
                            add_shift(m, u, 0)
                        if do_o:
                            normalise(n)
                        if do_s:
                            add_positions(k, u, 3, pair)
                        if late(k):
                            keep_moments(n - 1)
                        if do_e:
                            add_shift(m, u, 1)
                        if do_s:
                            maximum(k, u, 2)
                        if do_e:
                            add_shift(m, u, 2)
                        if do_s:
                            maximum(k, u, 3)
                        if do_e:
                            add_shift(m, u, 3)
                    else:
                        if do_s:
                            maximum(k, u, 0)
                            maximum(k, u, 1)
                        if do_o:
                            make_low(nc.vector, v, n, u - 1, 3)
                        if do_s:
                            maximum(k, u, 2)
                            maximum(k, u, 3)
                        if late(k):
                            add_output(n - 1, u - 1)
                            statistics(n - 1)
                            moments(n - 1)
                        if do_o:
                            normalise(n)
                        if do_e:
                            make_low(nc.vector, v, m, u, 2)
                        if late(k):
                            keep_moments(n - 1)

                pipeline(v, nb, slot)
                add_output(nb - 1, nb - 1)
                statistics(nb - 1)
                moments(nb - 1)
                keep_moments(nb - 1)
                v.wait_ge(stats_ready, nb)
        sem.release()


def experts(nc, net, ins):
    nb = net.nb
    with ExitStack() as ctx:
        def sb(name, shape, dt=F32):
            return ctx.enter_context(nc.sbuf_tensor(f"m_{name}", shape, dt))

        sem = Semaphores(nc, "m")

        NC = NE + C
        w_parts = sb("w_parts", [P, 2, PIECES, 512], F16)
        down_parts = sb("down_parts", [P, 2, NE + C, D], F16)
        largest = sb("largest", [P, 2])
        largest_row = sb("largest_row", [1, 2])
        ones_row = sb("ones_row", [1, P])
        w_scale = sb("w_scale", [P, 2])
        w_step = sb("w_step", [P, 10])
        down, router = net.down, net.router
        normed = sb("normed", [P, 2, D])
        xT = sb("xT", [P, 2, C, P])
        x_parts = sb("x_parts", [P, 2, 2, C, P], F16)
        tanh = sb("tanh", [P, 3, 512])
        gated = tanh
        taps = sb("taps", [P, HID, 3])
        tap_scale = sb("tap_scale", [P, 2])
        tap_step = sb("tap_step", [P, 3])
        taps_high = sb("taps_high", [P, HID, 3], F16)
        bias_all = sb("bias_all", [P, HID])
        bias_parts = sb("bias_parts", [P, PARTS, HID], BF16)
        acts = sb("acts", [P, NC, P])
        actsT = sb("actsT", [P, 2, NC, P], F16)
        top = sb("top", [P, 8])
        neg_top = sb("neg_top", [P, 1])
        expd = sb("expd", [P, NE])
        exp_sum = sb("exp_sum", [P, 1])
        recip = sb("recip", [P, 1])
        prob = sb("prob", [P, 16])
        best = sb("best", [P, 8])
        left = sb("left", [P, 16])
        coef = sb("coef", [P, 2, NE])
        stats = sb("stats", [P, 6])
        agg = sb("agg", [P, 2])

        filled = sem("filled")
        normed_ready = sem("normed_ready")
        taps_loaded = sem("taps_loaded")
        tap_scaled = sem("tap_scaled")
        tap_work = sem("tap_work")
        xT_done = sem("xT_done")
        xT_copied = sem("xT_copied")
        x_high = sem("x_high")
        x_low = sem("x_low")
        scaling = sem("scaling")
        largest_turned = sem("largest_turned")
        largest_spread = sem("largest_spread")
        w_high = sem("w_high")
        w_low = sem("w_low")
        logits_done = sem("logits_done")
        route = sem("route")
        exp_ready = sem("exp_ready")
        unit_done = sem("unit_done")
        tanh_ready = sem("tanh_ready")
        gated_ready = sem("gated_ready")
        acts_ready = sem("acts_ready")
        actsT_done = sem("actsT_done")
        actsT_copied = sem("actsT_copied")
        actsT_low = sem("actsT_low")
        down_high = sem("down_high")
        down_low = sem("down_low")
        down_done = sem("down_done")
        x_added = sem("x_added")
        ln = sem("ln")
        stats_ready = sem("stats_ready")
        final = sem("final")

        bank_x = net.bank[0]
        logits = bank_x[:, D:D + NE]
        bank_g = [net.bank[1], net.bank[3], net.bank[1]]
        bank_u = [net.bank[2], net.bank[4], net.bank[1]]
        bank_a = net.bank[5:7]
        bank_o = net.bank[7]
        UNITS = ((0, 4), (4, 8), (8, 10))

        def steps(engine, slot):
            for k in range(2):
                slot(k, k % 2)
            with engine.Fori(1, nb // 2 - 1) as t:
                for u in range(2):
                    slot(2 * t + u, u)
            for k in range(nb - 2, nb + 1):
                slot(k, k % 2)

        def active(k):
            static = isinstance(k, int)
            return not static or k < nb, not static or k >= 1, not static or k < nb - 1

        with nc.Block() as block:
            @block.sync
            def _(sp):
                sp.dma_start(taps[:, :, :].rearrange("p c k -> p (c k)"),
                             ins["L1_ffn_conv_w"].rearrange("c o k -> (c o k)").partition_broadcast(P)).then_inc(taps_loaded, 16)
                sp.dma_start(bias_all[:, :], ins["L1_ffn_conv_b"].partition_broadcast(P)).then_inc(taps_loaded, 16)
                sp.wait_ge(taps_loaded, 32)

            @block.tensor
            def _(pe):
                def turn(k, u):
                    pe.wait_ge(normed_ready, k + 1)
                    ge(pe, exp_ready, k)
                    for c in range(C):
                        i = nc.tensor.transpose(bank_x[:, c * P:(c + 1) * P], normed[:, u, c * P:(c + 1) * P], net.id_f[:, :])
                    i.then_inc(xT_done, 1)

                def route_logits(k, u):
                    pe.wait_ge(xT_copied, k + 1)
                    for c in range(C):
                        i = nc.tensor.matmul(logits, xT[:, u, c, :], router[:, c, :], start=(c == 0), stop=(c == C - 1))
                    i.then_inc(logits_done, 1)

                def unit(k, u, n):
                    if isinstance(k, int) and k == 0:
                        pe.wait_ge(w_low, (4, 8, PIECES)[n])
                    ge(pe, acts_ready, (3 * k, 3 * k - 1, 3 * k + 1)[n])
                    for m, bank in enumerate((bank_g[n], bank_u[n]) if n < 2 else (bank_g[n],)):
                        terms = [(c, a, b) for c in range(C) for a, b in ((0, 0), (0, 1), (1, 0))]
                        for j, (c, a, b) in enumerate(terms):
                            i = nc.tensor.matmul(bank[:, :], x_parts[:, u, a, c, :], w_parts[:, b, 4 * n + 2 * m + c, :],
                                                 start=(j == 0), stop=(j == len(terms) - 1))
                    i.then_inc(unit_done, 1)

                def turn_acts(k, n):
                    lo, hi = UNITS[n]
                    pe.wait_ge(acts_ready, 3 * k + n + 1)
                    ge(pe, actsT_low, 3 * k + n - (0 if n == 0 else 1))
                    for e in range(lo, hi):
                        i = nc.tensor.transpose(bank_a[n % 2][:, (e - lo) * P:(e - lo + 1) * P], acts[:, e, :], net.id_f[:, :])
                    i.then_inc(actsT_done, 1)

                def sum_down(k, n):
                    lo, hi = UNITS[n]
                    pe.wait_ge(actsT_copied, 3 * k + n + 1)
                    pe.wait_ge(actsT_low, 3 * k + n + 1)
                    if isinstance(k, int) and k == 0 and n == 0:
                        pe.wait_ge(down_low, 5)
                    if n == 0:
                        ge(pe, x_added, k)
                    for e in range(lo, hi):
                        for m, (a, b) in enumerate(((0, 0), (0, 1), (1, 0))):
                            i = nc.tensor.matmul(bank_o[:, 0:D], actsT[:, a, e, :], down_parts[:, b, e, :],
                                                 start=(e == 0 and m == 0), stop=(e == NC - 1 and m == 2))
                    i.then_inc(down_done, 1)

                def slot(k, u):
                    units, end, after = active(k)
                    if units:
                        pe.wait_ge(x_low, k + 1)
                        unit(k, u, 0)
                    if end:
                        turn_acts(k - 1, 2)
                        sum_down(k - 1, 1)
                    if units:
                        unit(k, u, 1)
                    if end:
                        sum_down(k - 1, 2)
                    if units:
                        turn_acts(k, 0)
                        unit(k, u, 2)
                        if after:
                            turn(k + 1, 1 - u)
                        sum_down(k, 0)
                        turn_acts(k, 1)
                        if after:
                            route_logits(k + 1, 1 - u)

                pe.wait_ge(scaling, 3)
                for n in range(2):
                    i = nc.tensor.transpose(bank_o[0:1, n * P:(n + 1) * P], largest[:, n:n + 1], net.id_f[:, :])
                i.then_inc(largest_turned, 1)
                pe.wait_ge(scaling, 4)
                nc.tensor.matmul(bank_o[:, 0:2], ones_row[:, :], largest_row[:, :], start=True, stop=True).then_inc(largest_spread, 1)
                turn(0, 0)
                pe.wait_ge(net.moe_loaded, 64)
                route_logits(0, 0)
                steps(pe, slot)

            @block.scalar
            def _(act):
                def copy_x(k, u):
                    act.wait_ge(xT_done, k + 1)
                    ge(act, unit_done, 3 * k - 3)
                    nc.scalar.activation(x_parts[:, u, 0, :, :].rearrange("p c t -> p (c t)"), bank_x[:, 0:D], ACT.Copy,
                                         scale=ACT_SCALE).then_inc(x_high, 1)
                    nc.scalar.activation(xT[:, u, :, :].rearrange("p c t -> p (c t)"), bank_x[:, 0:D], ACT.Copy).then_inc(xT_copied, 1)

                def route_exp(k):
                    act.wait_ge(route, 9 * k + 2)
                    nc.scalar.activation(expd[:, :], logits, ACT.Exp, bias=neg_top[:, :], accum_out=exp_sum[:, :]).then_inc(exp_ready, 1)

                def tangent(k, n):
                    act.wait_ge(unit_done, 3 * k + n + 1)
                    ge(act, acts_ready, 3 * k + n - 2)
                    w = 512 if n < 2 else D
                    nc.scalar.activation(tanh[:, n, 0:w], bank_g[n][:, 0:w], ACT.Tanh, scale=w_step[:, 3:4]).then_inc(tanh_ready, 1)

                def copy_acts(k, n):
                    lo, hi = UNITS[n]
                    act.wait_ge(actsT_done, 3 * k + n + 1)
                    ge(act, down_done, 3 * k + n - 2)
                    nc.scalar.activation(actsT[:, 0, lo:hi, :].rearrange("p e t -> p (e t)"), bank_a[n % 2][:, 0:(hi - lo) * P],
                                         ACT.Copy).then_inc(actsT_copied, 1)

                def slot(k, u):
                    units, end, after = active(k)
                    if units:
                        tangent(k, 0)
                    if end:
                        copy_acts(k - 1, 2)
                    if units:
                        tangent(k, 1)
                        copy_acts(k, 0)
                        tangent(k, 2)
                        if after:
                            copy_x(k + 1, 1 - u)
                        copy_acts(k, 1)
                        if after:
                            route_exp(k + 1)

                copy_x(0, 0)
                act.wait_ge(scaling, 6)
                for n in range(PIECES):
                    nc.scalar.activation(w_parts[:, 0, n, :], net.w_pieces[:, n, :], ACT.Copy, scale=w_scale[:, 0:1]).then_inc(w_high, 1)
                route_exp(0)
                for n in range(5):
                    nc.scalar.activation(down_parts[:, 0, 2 * n:2 * n + 2, :], down[:, 2 * n:2 * n + 2, :], ACT.Copy,
                                         scale=w_scale[:, 1:2]).then_inc(down_high, 1)
                act.wait_ge(scaling, 14)
                steps(act, slot)

            @block.gpsimd
            def _(pool):
                def subtract(out, in0, in1):
                    nc.gpsimd.tensor_tensor(out, in0, in1, ALU.subtract).then_inc(tap_work, 1)

                pool.wait_ge(tap_scaled, 6)
                flat = taps[:, :, :].rearrange("p c k -> p (c k)")
                high = taps_high[:, :, :].rearrange("p c k -> p (c k)")
                nc.gpsimd.tensor_scalar(flat, flat, tap_scale[:, 0:1], None, ALU.mult).then_inc(tap_work, 1)
                nc.gpsimd.tensor_scalar(bias_all[:, :], bias_all[:, :], tap_scale[:, 1:2], None, ALU.mult).then_inc(tap_work, 1)
                pool.wait_ge(tap_work, 2)
                nc.gpsimd.tensor_copy(high, flat).then_inc(tap_work, 1)
                nc.gpsimd.tensor_copy(bias_parts[:, 0, :], bias_all[:, :]).then_inc(tap_work, 1)
                pool.wait_ge(tap_work, 4)
                subtract(flat, flat, high)
                subtract(bias_all[:, :], bias_all[:, :], bias_parts[:, 0, :])
                pool.wait_ge(tap_work, 6)
                nc.gpsimd.tensor_copy(bias_parts[:, 1, :], bias_all[:, :]).then_inc(tap_work, 1)
                pool.wait_ge(tap_work, 7)
                subtract(bias_parts[:, 2, :], bias_all[:, :], bias_parts[:, 1, :])
                pool.wait_ge(tap_work, 8)
                for part in range(PARTS):
                    row = slice(32 * part, 32 * part + 1)
                    nc.gpsimd.tensor_copy(net.conv_bias[row, :], bias_parts[row, part, :]).then_inc(tap_work, 1)
                    pool.wait_ge(tap_work, 8 + part + 1)
                for part, values in enumerate((taps_high, taps)):
                    for c in range(C):
                        for tap in range(3):
                            nc.gpsimd.tensor_tensor(net.conv_w[:, c, tap, part, :], net.w1T[:, c, :], values[:, :, tap], ALU.mult).then_inc(tap_work, 1)
                pool.wait_ge(tap_work, 8 + PARTS + 6 * C)
                with pool.Fori(0, nb) as k:
                    pool.wait_ge(stats_ready, k + 1)
                    nc.gpsimd.tensor_tensor(at(net.var_eps, k), at(net.moments[:, :, 1:2], k), net.eps[:, :], ALU.add).then_inc(final, 1)
                    pool.wait_ge(final, 2 * k + 1)
                    nc.gpsimd.tensor_tensor(at(net.rstd, k), at(net.var_eps, k), net.minus_half[:, 0, :], ALU.pow).then_inc(final, 1)
                pool.wait_ge(final, 2 * nb)

            @block.vector
            def _(v):
                def norm(k, u):
                    ge(v, xT_done, k - 1)
                    nc.vector.tensor_scalar(normed[:, u, :], at(net.x, k), at(net.moments[:, :, 0:1], k), at(net.rstd, k),
                                            ALU.subtract, ALU.mult).then_inc(normed_ready, 1)

                def route_begin(k):
                    v.wait_ge(logits_done, k + 1)
                    nc.vector.tensor_copy(left[:, 8:16], logits).then_inc(route, 1)
                    v.wait_ge(route, 9 * k + 1)
                    nc.vector.tensor_reduce(neg_top[:, :], left[:, 8:16], X, ALU.max, negate=True).then_inc(route, 1)

                def route_end(k, u):
                    v.wait_ge(exp_ready, k + 1)
                    nc.vector.reciprocal(recip[:, :], exp_sum[:, :]).then_inc(route, 1)
                    v.wait_ge(route, 9 * k + 3)
                    nc.vector.tensor_scalar(prob[:, 0:NE], expd[:, :], recip[:, :], None, ALU.mult).then_inc(route, 1)
                    apart(v, route, 9 * k + 4)
                    nc.vector.max(top[:, :], prob[:, 0:NE]).then_inc(route, 1)
                    v.wait_ge(route, 9 * k + 5)
                    nc.vector.tensor_copy(best[:, 0:2], top[:, 0:2]).then_inc(route, 1)
                    apart(v, route, 9 * k + 6)
                    nc.vector.match_replace(left[:, :], best[:, :], prob[:, :], 0.0).then_inc(route, 1)
                    v.wait_ge(route, 9 * k + 7)
                    nc.vector.tensor_tensor(left[:, 0:NE], prob[:, 0:NE], left[:, 0:NE], ALU.subtract).then_inc(route, 1)
                    v.wait_ge(route, 9 * k + 8)
                    nc.vector.tensor_scalar(coef[:, u, :], left[:, 0:NE], w_step[:, 4:5], None, ALU.mult).then_inc(route, 1)

                def lower_x(k, u):
                    v.wait_ge(x_high, k + 1)
                    v.wait_ge(xT_copied, k + 1)
                    nc.vector.scalar_tensor_tensor(out=x_parts[:, u, 1, :, :].rearrange("p c t -> p (c t)"),
                                                   in0=xT[:, u, :, :].rearrange("p c t -> p (c t)"), scalar=ACT_SCALE,
                                                   in1=x_parts[:, u, 0, :, :].rearrange("p c t -> p (c t)"),
                                                   op0=ALU.mult, op1=ALU.subtract).then_inc(x_low, 1)

                def gate_unit(k, n):
                    w = 512 if n < 2 else D
                    v.wait_ge(tanh_ready, 3 * k + n + 1)
                    nc.vector.scalar_tensor_tensor(out=gated[:, n, 0:w], in0=tanh[:, n, 0:w], scalar=1.0, in1=bank_g[n][:, 0:w],
                                                   op0=ALU.add, op1=ALU.mult).then_inc(gated_ready, 1)

                def act_unit(k, u, n):
                    lo, hi = UNITS[n]
                    v.wait_ge(gated_ready, 3 * k + n + 1)
                    ge(v, actsT_done, 3 * k + n - 2)
                    if n < 2:
                        for e in range(lo, hi):
                            i = nc.vector.scalar_tensor_tensor(
                                out=acts[:, e, :], in0=gated[:, n, (e - lo) * DE:(e - lo + 1) * DE], scalar=coef[:, u, e:e + 1],
                                in1=bank_u[n][:, (e - lo) * DE:(e - lo + 1) * DE], op0=ALU.mult, op1=ALU.mult)
                    else:
                        i = nc.vector.scalar_tensor_tensor(
                            out=acts[:, NE:NC, :].rearrange("p e d -> p (e d)"), in0=gated[:, n, 0:D], scalar=w_step[:, 4:5],
                            in1=bank_u[n][:, D:2 * D], op0=ALU.mult, op1=ALU.mult)
                    i.then_inc(acts_ready, 1)

                def lower_acts(k, n):
                    lo, hi = UNITS[n]
                    v.wait_ge(actsT_copied, 3 * k + n + 1)
                    nc.vector.tensor_tensor(actsT[:, 1, lo:hi, :].rearrange("p e t -> p (e t)"), bank_a[n % 2][:, 0:(hi - lo) * P],
                                            actsT[:, 0, lo:hi, :].rearrange("p e t -> p (e t)"), ALU.subtract).then_inc(actsT_low, 1)

                def add_output(k):
                    v.wait_ge(down_done, 3 * k + 3)
                    nc.vector.scalar_tensor_tensor(out=at(net.x, k), in0=bank_o[:, 0:D], scalar=w_step[:, 8:9], in1=at(net.x, k),
                                                   op0=ALU.mult, op1=ALU.add).then_inc(x_added, 1)

                def moments(k):
                    apart(v, x_added, k + 1)
                    nc.vector.bn_stats(stats[:, :], at(net.x, k)).then_inc(ln, 1)
                    apart(v, ln, 2 * k + 1)
                    nc.vector.bn_aggr(agg[:, :], stats[:, :]).then_inc(ln, 1)
                    apart(v, ln, 2 * k + 2)
                    nc.vector.tensor_copy(at(net.moments, k), agg[:, :]).then_inc(stats_ready, 1)

                def slot(k, u):
                    units, end, after = active(k)
                    if after:
                        norm(k + 1, 1 - u)
                    if units:
                        v.wait_ge(route, 9 * k + 9)
                    if end:
                        lower_acts(k - 1, 2)
                    if units:
                        gate_unit(k, 0)
                        act_unit(k, u, 0)
                        gate_unit(k, 1)
                    if end:
                        add_output(k - 1)
                    if units:
                        lower_acts(k, 0)
                        act_unit(k, u, 1)
                    if units:
                        gate_unit(k, 2)
                    if after:
                        lower_x(k + 1, 1 - u)
                    if units:
                        act_unit(k, u, 2)
                        lower_acts(k, 1)
                    if after:
                        route_begin(k + 1)
                    if end:
                        moments(k - 1)
                    if after:
                        route_end(k + 1, 1 - u)

                def scale_weights():
                    nc.vector.memset(ones_row[:, :], 1.0).then_inc(scaling, 1)
                    nc.vector.tensor_reduce(largest[:, 0:1], net.piece_max[:, :, 0], X, ALU.max).then_inc(scaling, 1)
                    nc.vector.tensor_reduce(largest[:, 1:2], net.down_max[:, :, 0], X, ALU.max).then_inc(scaling, 1)
                    v.wait_ge(largest_turned, 1)
                    nc.vector.tensor_reduce(largest_row[:, :], bank_o[0:1, 0:2 * P].rearrange("p (n w) -> p n w", n=2), X, ALU.max).then_inc(scaling, 1)
                    v.wait_ge(largest_spread, 1)
                    nc.vector.tensor_scalar(w_step[:, 0:2], bank_o[:, 0:2], 1e-6, 1.0 / TAP_SCALE, ALU.max, ALU.mult).then_inc(scaling, 1)
                    v.wait_ge(scaling, 5)
                    nc.vector.reciprocal(w_scale[:, :], w_step[:, 0:2]).then_inc(scaling, 1)
                    nc.vector.tensor_scalar(w_step[:, 2:3], w_step[:, 0:1], 1.0 / ACT_SCALE, None, ALU.mult).then_inc(scaling, 1)
                    nc.vector.tensor_scalar(w_step[:, 5:6], w_step[:, 0:1], TAP_SCALE * D, None, ALU.mult).then_inc(scaling, 1)
                    v.wait_ge(scaling, 8)
                    nc.vector.tensor_scalar(w_step[:, 3:4], w_step[:, 2:3], 0.5, None, ALU.mult).then_inc(scaling, 1)
                    nc.vector.tensor_scalar(w_step[:, 6:7], w_step[:, 2:3], w_step[:, 2:3], 0.5, ALU.mult, ALU.mult).then_inc(scaling, 1)
                    nc.vector.tensor_scalar(w_step[:, 7:8], w_step[:, 5:6], w_step[:, 5:6], 2.0 ** -15, ALU.mult, ALU.mult).then_inc(scaling, 1)
                    v.wait_ge(scaling, 11)
                    nc.vector.tensor_scalar(w_step[:, 8:9], w_step[:, 7:8], w_step[:, 1:2], None, ALU.mult).then_inc(scaling, 1)
                    nc.vector.reciprocal(w_step[:, 9:10], w_step[:, 7:8]).then_inc(scaling, 1)
                    v.wait_ge(scaling, 13)
                    nc.vector.tensor_scalar(w_step[:, 4:5], w_step[:, 9:10], w_step[:, 6:7], None, ALU.mult).then_inc(scaling, 1)
                    v.wait_ge(scaling, 14)

                def lower_weights(first, end):
                    for n in range(first, end):
                        v.wait_ge(w_high, n + 1)
                        nc.vector.scalar_tensor_tensor(out=w_parts[:, 1, n, :], in0=net.w_pieces[:, n, :], scalar=w_scale[:, 0:1],
                                                       in1=w_parts[:, 0, n, :], op0=ALU.mult, op1=ALU.subtract).then_inc(w_low, 1)

                def scale_taps():
                    v.wait_ge(taps_loaded, 32)
                    nc.vector.tensor_reduce(tap_step[:, 0:1], taps[:, :, :].rearrange("p c k -> p (c k)"), X, ALU.max,
                                            apply_absolute_value=True).then_inc(tap_scaled, 1)
                    v.wait_ge(tap_scaled, 1)
                    nc.vector.tensor_scalar(tap_step[:, 1:2], tap_step[:, 0:1], 1e-6, 1.0 / TAP_SCALE, ALU.max, ALU.mult).then_inc(tap_scaled, 1)
                    v.wait_ge(tap_scaled, 2)
                    nc.vector.reciprocal(tap_scale[:, 0:1], tap_step[:, 1:2]).then_inc(tap_scaled, 1)
                    nc.vector.tensor_scalar(tap_step[:, 2:3], tap_step[:, 1:2], net.w_dequant[:, 0:1], 1.0 / ACT_SCALE, ALU.mult, ALU.mult).then_inc(tap_scaled, 1)
                    v.wait_ge(tap_scaled, 4)
                    nc.vector.reciprocal(tap_scale[:, 1:2], tap_step[:, 2:3]).then_inc(tap_scaled, 1)
                    nc.vector.tensor_scalar(net.half_scale[:, :], tap_step[:, 2:3], 0.5, None, ALU.mult).then_inc(tap_scaled, 1)
                    v.wait_ge(tap_scaled, 6)

                nc.vector.memset(prob[:, :], -5.0).then_inc(filled, 1)
                nc.vector.memset(best[:, :], -5.0).then_inc(filled, 1)
                v.wait_ge(filled, 2)
                norm(0, 0)
                scale_weights()
                lower_x(0, 0)
                lower_weights(0, 4)
                route_begin(0)
                route_end(0, 0)
                lower_weights(4, PIECES)
                for n in range(5):
                    v.wait_ge(down_high, n + 1)
                    nc.vector.scalar_tensor_tensor(out=down_parts[:, 1, 2 * n:2 * n + 2, :], in0=down[:, 2 * n:2 * n + 2, :], scalar=w_scale[:, 1:2],
                                                   in1=down_parts[:, 0, 2 * n:2 * n + 2, :], op0=ALU.mult, op1=ALU.subtract).then_inc(down_low, 1)
                scale_taps()
                steps(v, slot)
                v.wait_ge(stats_ready, nb)
        sem.release()


def bitnet(nc, net, out):
    nb = net.nb
    with ExitStack() as ctx:
        def sb(name, shape, dt=F32):
            return ctx.enter_context(nc.sbuf_tensor(f"f_{name}", shape, dt))

        sem = Semaphores(nc, "f")

        id_h = sb("id_h", [P, P], F16)
        normed = sb("normed", [P, D])
        big1 = sb("big1", [P, 1])
        scale1 = sb("scale1", [P, 1])
        inv1 = sb("inv1", [P, 2])
        round1 = sb("round1", [P, D])
        q1 = sb("q1", [P, D])
        deq = sb("dequantised", [P, D])
        deq_parts = sb("deq_parts", [P, 2, 2, D], F16)
        deqT = sb("deqT", [P, 2, C, 2, P + 2], F16)
        tanh = sb("tanh", [P, 2, HALF])
        silu2 = sb("silu2", [P, HID])
        big2 = sb("big2", [P, 2])
        big2_all = sb("big2_all", [P, 1])
        step2 = sb("step2", [P, 1])
        recip2 = sb("recip2", [P, 1])
        scale2 = sb("scale2", [P, 1])
        out_step = sb("out_step", [P, 2])
        round2 = sb("round2", [P, HID])
        q2 = sb("q2", [P, HID], BF16)
        q2T = sb("q2T", [P, HC, P], BF16)
        result = sb("result", [P, 2, D])

        init = sem("init")
        quant1 = sem("quant1")
        high_ready = sem("high_ready")
        low_ready = sem("low_ready")
        deqT_done = sem("deqT_done")
        deqT_copied = sem("deqT_copied")
        conv_done = sem("conv_done")
        tanh_ready = sem("tanh_ready")
        silu_ready = sem("silu_ready")
        quant2 = sem("quant2")
        rounded = sem("rounded")
        q2_ready = sem("q2_ready")
        q2T_done = sem("q2T_done")
        q2T_copied = sem("q2T_copied")
        out_done = sem("out_done")
        result_ready = sem("result_ready")
        stored = [sem(f"stored{i}") for i in range(2)]

        bank_y = (net.bank[0:2], net.bank[2:4])
        bank_t = net.bank[4]
        deqT_ps = bank_t[:, 0:2 * P].bitcast(F16)
        bank_q2 = net.bank[5]
        bank_o = net.bank[6]

        def steps(engine, slot):
            for k in range(4):
                slot(k, k % 2, k // 2)
            with engine.Fori(2, nb // 2 - 1) as t:
                for u in range(2):
                    slot(2 * t + u, u, t)
            for k in range(nb - 2, nb + 1):
                slot(k, k % 2, k // 2)

        def active(k):
            static = isinstance(k, int)
            return not static or k < nb - 1, not static or k < nb, not static or k >= 1

        with nc.Block() as block:
            @block.sync
            def _(sp):
                def slot(k, u, t):
                    if active(k)[2]:
                        n, b = k - 1, 1 - u
                        sp.wait_ge(result_ready, n + 1)
                        sp.dma_start(out[bass.ds(n, 1)].rearrange("n p d -> p (n d)"), result[:, b, :]).then_inc(stored[b], 16)

                steps(sp, slot)
                for b in range(2):
                    sp.wait_ge(stored[b], 16 * (nb // 2))

            @block.gpsimd
            def _(pool):
                def lower(k, u):
                    pool.wait_ge(high_ready, k + 1)
                    ge(pool, deqT_done, k - 1)
                    nc.gpsimd.tensor_tensor(deq_parts[:, u, 1, :], deq[:, :], deq_parts[:, u, 0, :], ALU.subtract).then_inc(low_ready, 1)

                def slot(k, u, t):
                    if active(k)[0]:
                        lower(k + 1, 1 - u)

                lower(0, 0)
                steps(pool, slot)

            @block.tensor
            def _(pe):
                def turn(k, u):
                    pe.wait_ge(low_ready, k + 1)
                    ge(pe, deqT_copied, k)
                    for c in range(C):
                        for part in range(2):
                            i = nc.tensor.transpose(deqT_ps[:, (c * 2 + part) * P:(c * 2 + part + 1) * P],
                                                    deq_parts[:, u, part, c * P:(c + 1) * P], id_h[:, :])
                    i.then_inc(deqT_done, 1)

                def product(k, u, half, first):
                    bank = bank_y[u][half][:, :]
                    ch = slice(half * HALF, (half + 1) * HALF)
                    if first:
                        pe.wait_ge(deqT_copied, k + 1)
                        ge(pe, silu_ready, 2 * k + half - 3)
                        nc.tensor.matmul(bank, net.ones_b[:, :], net.conv_bias[:, ch], start=True, stop=False)
                    terms = [(tap, c, a, w) for tap in range(3) for c in range(C) for a, w in ((0, 0), (0, 1), (1, 0))]
                    for n, (tap, c, a, w) in list(enumerate(terms))[0 if first else 9:9 if first else 18]:
                        i = nc.tensor.matmul(bank, deqT[:, u, c, a, tap:tap + P], net.conv_w[:, c, tap, w, ch],
                                             start=False, stop=(n == 17))
                    if not first:
                        i.then_inc(conv_done, 1)

                def slot(k, u, t):
                    before, product_too, end = active(k)
                    n = k - 1
                    if product_too:
                        product(k, u, 0, True)
                        product(k, u, 0, False)
                        product(k, u, 1, True)
                    if end:
                        pe.wait_ge(q2_ready, n + 1)
                        ge(pe, q2T_copied, n)
                        for c in range(HC):
                            i = nc.tensor.transpose(bank_q2[:, :].bitcast(BF16)[:, c * P:(c + 1) * P], q2[:, c * P:(c + 1) * P], net.id_b[:, :])
                        i.then_inc(q2T_done, 1)
                    if product_too:
                        product(k, u, 1, False)
                    if before:
                        turn(k + 1, 1 - u)
                    if end:
                        pe.wait_ge(q2T_copied, n + 1)
                        ge(pe, result_ready, n)
                        for c in range(HC):
                            i = nc.tensor.matmul(bank_o[:, 0:D], q2T[:, c, :], net.w2T[:, c, :], start=(c == 0), stop=(c == HC - 1))
                        i.then_inc(out_done, 1)

                pe.wait_ge(init, 4)
                turn(0, 0)
                steps(pe, slot)

            @block.scalar
            def _(act):
                def upper(k, u):
                    act.wait_ge(quant1, 8 * k + 8)
                    ge(act, deqT_done, k - 1)
                    nc.scalar.activation(deq_parts[:, u, 0, :], deq[:, :], ACT.Copy).then_inc(high_ready, 1)

                def copy_turned(k, u):
                    act.wait_ge(deqT_done, k + 1)
                    ge(act, conv_done, 2 * k - 2)
                    nc.scalar.activation(deqT[:, u, :, :, 1:P + 1], deqT_ps.rearrange("p (c n t) -> p c n t", c=C, n=2),
                                         ACT.Copy).then_inc(deqT_copied, 1)

                def tangent(k, u, half):
                    act.wait_ge(conv_done, 2 * k + half + 1)
                    ge(act, silu_ready, 2 * k + half - 1)
                    nc.scalar.activation(tanh[:, half, :], bank_y[u][half][:, :], ACT.Tanh, scale=net.half_scale[:, :]).then_inc(tanh_ready, 1)

                def slot(k, u, t):
                    before, product_too, end = active(k)
                    n = k - 1
                    if end:
                        tangent(n, 1 - u, 1)
                        act.wait_ge(quant2, 7 * n + 7)
                        ge(act, q2_ready, n)
                        nc.scalar.activation(round2[:, :], silu2[:, :], ACT.Copy, bias=ROUND, scale=scale2[:, :]).then_inc(rounded, 1)
                    if product_too:
                        tangent(k, u, 0)
                    if before:
                        upper(k + 1, 1 - u)
                    if end:
                        act.wait_ge(q2T_done, n + 1)
                        ge(act, out_done, n)
                        nc.scalar.activation(q2T[:, :, :].rearrange("p c t -> p (c t)"), bank_q2[:, :].bitcast(BF16), ACT.Copy).then_inc(q2T_copied, 1)
                    if before:
                        copy_turned(k + 1, 1 - u)

                act.wait_ge(init, 4)
                upper(0, 0)
                copy_turned(0, 0)
                steps(act, slot)

            @block.vector
            def _(v):
                def quantise(k):
                    nc.vector.tensor_scalar(normed[:, :], at(net.x, k), at(net.moments[:, :, 0:1], k), at(net.rstd, k),
                                            ALU.subtract, ALU.mult).then_inc(quant1, 1)
                    v.wait_ge(quant1, 8 * k + 1)
                    nc.vector.tensor_reduce(big1[:, :], normed[:, :], X, ALU.max, apply_absolute_value=True).then_inc(quant1, 1)
                    v.wait_ge(quant1, 8 * k + 2)
                    nc.vector.tensor_scalar(inv1[:, 0:1], big1[:, :], 1e-5, 1.0 / 127.0, ALU.max, ALU.mult).then_inc(quant1, 1)
                    v.wait_ge(quant1, 8 * k + 3)
                    nc.vector.reciprocal(scale1[:, :], inv1[:, 0:1]).then_inc(quant1, 1)
                    nc.vector.tensor_scalar(inv1[:, 1:2], inv1[:, 0:1], ACT_SCALE, None, ALU.mult).then_inc(quant1, 1)

                def quantise_end(k):
                    v.wait_ge(quant1, 8 * k + 5)
                    nc.vector.tensor_scalar(round1[:, :], normed[:, :], scale1[:, :], ROUND, ALU.mult, ALU.add).then_inc(quant1, 1)
                    v.wait_ge(quant1, 8 * k + 6)
                    nc.vector.tensor_scalar(q1[:, :], round1[:, :], -ROUND, 127.0, ALU.add, ALU.min).then_inc(quant1, 1)
                    v.wait_ge(quant1, 8 * k + 7)
                    ge(v, low_ready, k)
                    nc.vector.tensor_scalar(deq[:, :], q1[:, :], inv1[:, 1:2], None, ALU.mult).then_inc(quant1, 1)

                def silu(k, u, half):
                    s = slice(half * HALF, (half + 1) * HALF)
                    v.wait_ge(tanh_ready, 2 * k + half + 1)
                    ge(v, rounded, k)
                    nc.vector.scalar_tensor_tensor(out=silu2[:, s], in0=tanh[:, half, :], scalar=1.0, in1=bank_y[u][half][:, :],
                                                   op0=ALU.add, op1=ALU.mult).then_inc(silu_ready, 1)
                    v.wait_ge(silu_ready, 2 * k + half + 1)
                    ge(v, quant2, 7 * k)
                    nc.vector.tensor_reduce(big2[:, half:half + 1], silu2[:, s], X, ALU.max, apply_absolute_value=True).then_inc(quant2, 1)

                def slot(k, u, t):
                    before, product_too, end = active(k)
                    n, b = k - 1, 1 - u
                    if end:
                        silu(n, b, 1)
                        v.wait_ge(quant2, 7 * n + 2)
                        nc.vector.tensor_tensor(big2_all[:, :], big2[:, 0:1], big2[:, 1:2], ALU.max).then_inc(quant2, 1)
                        v.wait_ge(quant2, 7 * n + 3)
                        nc.vector.tensor_scalar(step2[:, :], big2_all[:, :], net.half_scale_127[:, :], 1e-5 / 127.0, ALU.mult, ALU.max).then_inc(quant2, 1)
                        v.wait_ge(quant2, 7 * n + 4)
                        nc.vector.reciprocal(recip2[:, :], step2[:, :]).then_inc(quant2, 1)
                        nc.vector.tensor_scalar(out_step[:, b:b + 1], step2[:, :], net.w_dequant[:, 1:2], None, ALU.mult).then_inc(quant2, 1)
                        v.wait_ge(quant2, 7 * n + 6)
                        nc.vector.tensor_scalar(scale2[:, :], recip2[:, :], net.half_scale[:, :], None, ALU.mult).then_inc(quant2, 1)
                    if before:
                        quantise(k + 1)
                    if end:
                        v.wait_ge(rounded, n + 1)
                        ge(v, q2T_done, n)
                        nc.vector.tensor_scalar(q2[:, :], round2[:, :], -ROUND, 127.0, ALU.add, ALU.min).then_inc(q2_ready, 1)
                    if before:
                        quantise_end(k + 1)
                    if product_too:
                        silu(k, u, 0)
                    if end:
                        v.wait_ge(out_done, n + 1)
                        ge(v, stored[b], 16 * (t - 1 + u))
                        nc.vector.scalar_tensor_tensor(out=result[:, b, :], in0=bank_o[:, 0:D], scalar=out_step[:, b:b + 1], in1=at(net.x, n),
                                                       op0=ALU.mult, op1=ALU.add).then_inc(result_ready, 1)

                nc.vector.tensor_copy(id_h[:, :], net.id_f[:, :]).then_inc(init, 1)
                nc.vector.memset(deqT[:, 0, :, :, :], 0.0).then_inc(init, 1)
                nc.vector.memset(deqT[:, 1, :, :, :], 0.0).then_inc(init, 1)
                nc.vector.tensor_scalar(net.half_scale_127[:, :], net.half_scale[:, :], 1.0 / 127.0, None, ALU.mult).then_inc(init, 1)
                v.wait_ge(init, 4)
                quantise(0)
                quantise_end(0)
                steps(v, slot)


def build(nc, ins, out):
    net = Net()
    net.nb = ins["x"].shape[0]
    pairs = net.nb // 2
    net.q_scr = [nc.dram_tensor(f"q_scratch{n}", (pairs, PARTS, P, C * 2 * P), BF16, kind="Internal").ap() for n in range(2)]
    net.k_scr = [nc.dram_tensor(f"k_scratch{n}", (pairs, PARTS, P, C * 2 * P), BF16, kind="Internal").ap() for n in range(2)]
    net.v_scr = [nc.dram_tensor(f"v_scratch{n}", (pairs, P, 2 * H * PARTS * VW), BF16, kind="Internal").ap() for n in range(2)]
    with ExitStack() as ctx:
        lay_out(nc, ctx, net)
        with ExitStack() as experts_ctx:
            lay_out_experts(nc, experts_ctx, net)
            prepare(nc, net, ins)
            project(nc, net, 0, True, ins)
            attend(nc, net, 0)
            experts(nc, net, ins)
        project(nc, net, 1, False, ins)
        attend(nc, net, 1)
        bitnet(nc, net, out)


def kernel(**inputs):
    import numpy as _np
    import concourse.bacc as _bacc
    from concourse import mybir as _mybir
    from concourse.bass_utils import run_bass_kernel_spmd as _run

    nc = _bacc.Bacc("TRN2", target_bir_lowering=False, num_devices=1)
    arrays, ins = {}, {}
    for name, value in inputs.items():
        a = _np.ascontiguousarray(value)
        arrays[f"in_{name}_dram"] = a
        ins[name] = nc.dram_tensor(f"in_{name}_dram", a.shape, _mybir.dt.from_np(a.dtype), kind="ExternalInput").ap()
    shape = inputs["x"].shape
    out = nc.dram_tensor("out_0_dram", shape, _mybir.dt.float32, kind="ExternalOutput").ap()
    build(nc, ins, out)
    return _run(nc, [arrays], core_ids=[0]).results[0]["out_0_dram"]
```
